# Optimizing a Trainium2 kernel written in Bass

```python
import numpy as np
import jax
import jax.numpy as jnp

def _softmax(x, axis=-1):
    return jax.nn.softmax(x, axis=axis)

def _gelu(x):
    return jax.nn.gelu(x, approximate=True)

def _silu(x):
    return jax.nn.silu(x)

def _sigmoid(x):
    return jax.nn.sigmoid(x)

def _layernorm(x, axis=-1, eps=1e-05):
    m = jnp.mean(x, axis=axis, keepdims=True)
    v = jnp.var(x, axis=axis, keepdims=True)
    return (x - m) / jnp.sqrt(v + eps)

def _scatter_add(tgt, idx, src, axis=0):
    return tgt.at[idx].add(src)

def _segment_sum(src, seg, n):
    return jax.ops.segment_sum(src, seg, n)
kernel_name = 'mk_macaron_d1_jaxref_r8_e076c8'

def setup_inputs(seed: int=0):
    np.random.seed(seed)
    _w = jnp.asarray

    def _L0_attn_setup():
        import jax, jax.numpy as jnp
        import numpy as np
        B, T, HIDDEN = (2, 512, 256)
        NUM_HEADS, HEAD_K, HEAD_V = (6, 32, 64)
        KEY_DIM, VALUE_DIM = (NUM_HEADS * HEAD_K, NUM_HEADS * HEAD_V)
        CONV_K, CHUNK, EPS = (4, 64, 1e-05)

        def short_conv(x, w):
            K = w.shape[1]
            xp = jnp.pad(x, ((0, 0), (K - 1, 0), (0, 0)))
            y = sum((xp[:, i:i + x.shape[1], :] * w[:, i] for i in range(K)))
            return jax.nn.silu(y)

        def l2norm(x):
            return x * jax.lax.rsqrt(jnp.sum(x * x, -1, keepdims=True))

        def _step(S, xs):
            qt, kt, vt, gt, bt = xs
            S = S * jnp.exp(gt)[..., None, None]
            pred = jnp.einsum('bhk,bhkv->bhv', kt, S)
            delta = (vt - pred) * bt[..., None]
            S = S + jnp.einsum('bhk,bhv->bhkv', kt, delta)
            return (S, jnp.einsum('bhk,bhkv->bhv', qt, S))

        def _chunk(S, xs):
            return jax.lax.scan(_step, S, xs)
        _chunk_ckpt = jax.checkpoint(_chunk)

        def gated_delta_rule(q, k, v, g, beta):
            b, t, h, dk = q.shape
            dv = v.shape[-1]
            q = l2norm(q) * dk ** (-0.5)
            k = l2norm(k)
            nc = t // CHUNK

            def to_scan(x):
                x = x.reshape(b, nc, CHUNK, *x.shape[2:])
                return jnp.moveaxis(x, 0, 2)
            xs = tuple(map(to_scan, (q, k, v, g, beta)))
            S0 = jnp.zeros((b, h, dk, dv), q.dtype)
            _, o = jax.lax.scan(_chunk_ckpt, S0, xs)
            return jnp.moveaxis(o, 2, 0).reshape(b, t, h, dv)
        key = jax.random.key(seed)
        ks = jax.random.split(key, 14)

        def lin(k, fi, fo):
            return jax.random.normal(k, (fi, fo), jnp.float32) / np.sqrt(fi)
        A = jax.random.uniform(ks[11], (NUM_HEADS,), minval=0.001, maxval=16.0)
        dt = jnp.exp(jax.random.uniform(ks[12], (NUM_HEADS,)) * (np.log(0.1) - np.log(0.001)) + np.log(0.001))
        dt = jnp.clip(dt, 0.0001)
        return {'hidden_states': jax.random.normal(ks[0], (B, T, HIDDEN), jnp.float32), 'Wq': lin(ks[1], HIDDEN, KEY_DIM), 'Wk': lin(ks[2], HIDDEN, KEY_DIM), 'Wv': lin(ks[3], HIDDEN, VALUE_DIM), 'Wa': lin(ks[4], HIDDEN, NUM_HEADS), 'Wb': lin(ks[5], HIDDEN, NUM_HEADS), 'Wg': lin(ks[6], HIDDEN, VALUE_DIM), 'Wo': lin(ks[7], VALUE_DIM, HIDDEN), 'conv_wq': jax.random.normal(ks[8], (KEY_DIM, CONV_K), jnp.float32) / np.sqrt(CONV_K), 'conv_wk': jax.random.normal(ks[9], (KEY_DIM, CONV_K), jnp.float32) / np.sqrt(CONV_K), 'conv_wv': jax.random.normal(ks[10], (VALUE_DIM, CONV_K), jnp.float32) / np.sqrt(CONV_K), 'A_log': jnp.log(A), 'dt_bias': dt + jnp.log(-jnp.expm1(-dt)), 'norm_weight': jnp.ones((HEAD_V,), jnp.float32)}
    _L0_attn_in = _L0_attn_setup()

    def _L0_ffn_setup():
        import jax, jax.numpy as jnp
        import numpy as np
        B, S, D = (2, 256, 256)
        E, H, TOP_K = (8, 176, 2)
        SH = 176
        ROUTED_SCALE = 2.5
        key = jax.random.key(seed)
        ks = jax.random.split(key, 8)
        std = 0.02
        return {'x': jax.random.normal(ks[0], (B, S, D), jnp.float32), 'gate_w': jax.random.normal(ks[1], (E, D), jnp.float32) * std, 'w1': jax.random.normal(ks[2], (E, D, H), jnp.float32) * std, 'w3': jax.random.normal(ks[3], (E, D, H), jnp.float32) * std, 'w2': jax.random.normal(ks[4], (E, H, D), jnp.float32) * std, 'sw1': jax.random.normal(ks[5], (D, SH), jnp.float32) * std, 'sw3': jax.random.normal(ks[6], (D, SH), jnp.float32) * std, 'sw2': jax.random.normal(ks[7], (SH, D), jnp.float32) * std}
    _L0_ffn_in = _L0_ffn_setup()
    _d = {'L0_attn_hidden_states': _L0_attn_in['hidden_states'], 'L0_attn_Wq': _L0_attn_in['Wq'], 'L0_attn_Wk': _L0_attn_in['Wk'], 'L0_attn_Wv': _L0_attn_in['Wv'], 'L0_attn_Wa': _L0_attn_in['Wa'], 'L0_attn_Wb': _L0_attn_in['Wb'], 'L0_attn_Wg': _L0_attn_in['Wg'], 'L0_attn_Wo': _L0_attn_in['Wo'], 'L0_attn_conv_wq': _L0_attn_in['conv_wq'], 'L0_attn_conv_wk': _L0_attn_in['conv_wk'], 'L0_attn_conv_wv': _L0_attn_in['conv_wv'], 'L0_attn_A_log': _L0_attn_in['A_log'], 'L0_attn_dt_bias': _L0_attn_in['dt_bias'], 'L0_attn_norm_weight': _L0_attn_in['norm_weight'], 'L0_ffn_gate_w': _L0_ffn_in['gate_w'], 'L0_ffn_w1': _L0_ffn_in['w1'], 'L0_ffn_w2': _L0_ffn_in['w2'], 'L0_ffn_w3': _L0_ffn_in['w3'], 'L0_ffn_sw1': _L0_ffn_in['sw1'], 'L0_ffn_sw2': _L0_ffn_in['sw2'], 'L0_ffn_sw3': _L0_ffn_in['sw3']}
    _x0 = _d['L0_attn_hidden_states']
    _d['L0_attn_hidden_states'] = jax.random.normal(jax.random.fold_in(jax.random.key(seed), 1), (8, 256, 256), dtype=_x0.dtype)
    del _x0
    return _d

def reference(L0_attn_hidden_states, L0_attn_Wq, L0_attn_Wk, L0_attn_Wv, L0_attn_Wa, L0_attn_Wb, L0_attn_Wg, L0_attn_Wo, L0_attn_conv_wq, L0_attn_conv_wk, L0_attn_conv_wv, L0_attn_A_log, L0_attn_dt_bias, L0_attn_norm_weight, L0_ffn_gate_w, L0_ffn_w1, L0_ffn_w2, L0_ffn_w3, L0_ffn_sw1, L0_ffn_sw2, L0_ffn_sw3):

    def _L0_attn_ref(hidden_states, Wq, Wk, Wv, Wa, Wb, Wg, Wo, conv_wq, conv_wk, conv_wv, A_log, dt_bias, norm_weight):
        import jax, jax.numpy as jnp
        import numpy as np
        B, T, HIDDEN = (2, 512, 256)
        NUM_HEADS, HEAD_K, HEAD_V = (6, 32, 64)
        KEY_DIM, VALUE_DIM = (NUM_HEADS * HEAD_K, NUM_HEADS * HEAD_V)
        CONV_K, CHUNK, EPS = (4, 64, 1e-05)

        def short_conv(x, w):
            K = w.shape[1]
            xp = jnp.pad(x, ((0, 0), (K - 1, 0), (0, 0)))
            y = sum((xp[:, i:i + x.shape[1], :] * w[:, i] for i in range(K)))
            return jax.nn.silu(y)

        def l2norm(x):
            return x * jax.lax.rsqrt(jnp.sum(x * x, -1, keepdims=True))

        def _step(S, xs):
            qt, kt, vt, gt, bt = xs
            S = S * jnp.exp(gt)[..., None, None]
            pred = jnp.einsum('bhk,bhkv->bhv', kt, S)
            delta = (vt - pred) * bt[..., None]
            S = S + jnp.einsum('bhk,bhv->bhkv', kt, delta)
            return (S, jnp.einsum('bhk,bhkv->bhv', qt, S))

        def _chunk(S, xs):
            return jax.lax.scan(_step, S, xs)
        _chunk_ckpt = jax.checkpoint(_chunk)

        def gated_delta_rule(q, k, v, g, beta):
            b, t, h, dk = q.shape
            dv = v.shape[-1]
            q = l2norm(q) * dk ** (-0.5)
            k = l2norm(k)
            nc = t // CHUNK

            def to_scan(x):
                x = x.reshape(b, nc, CHUNK, *x.shape[2:])
                return jnp.moveaxis(x, 0, 2)
            xs = tuple(map(to_scan, (q, k, v, g, beta)))
            S0 = jnp.zeros((b, h, dk, dv), q.dtype)
            _, o = jax.lax.scan(_chunk_ckpt, S0, xs)
            return jnp.moveaxis(o, 2, 0).reshape(b, t, h, dv)
        b, t, _ = hidden_states.shape
        q = short_conv(hidden_states @ Wq, conv_wq).reshape(b, t, NUM_HEADS, HEAD_K)
        k = short_conv(hidden_states @ Wk, conv_wk).reshape(b, t, NUM_HEADS, HEAD_K)
        v = short_conv(hidden_states @ Wv, conv_wv).reshape(b, t, NUM_HEADS, HEAD_V)
        beta = jax.nn.sigmoid(hidden_states @ Wb)
        g = -jnp.exp(A_log) * jax.nn.softplus(hidden_states @ Wa + dt_bias)
        o = gated_delta_rule(q, k, v, g, beta)
        gate = (hidden_states @ Wg).reshape(b, t, NUM_HEADS, HEAD_V)
        o = o * jax.lax.rsqrt(jnp.mean(o * o, -1, keepdims=True) + EPS) * norm_weight
        o = o * jax.nn.silu(gate)
        return o.reshape(b, t, VALUE_DIM) @ Wo

    def _L0_ffn_ref(x, gate_w, w1, w2, w3, sw1, sw2, sw3):
        import jax, jax.numpy as jnp
        import numpy as np
        B, S, D = (2, 256, 256)
        E, H, TOP_K = (8, 176, 2)
        SH = 176
        ROUTED_SCALE = 2.5
        b, s, d = x.shape
        xt = x.reshape(b * s, d)
        scores = jax.nn.sigmoid(xt @ gate_w.T)
        top_scores, top_idx = jax.lax.top_k(scores, TOP_K)
        top_scores = top_scores / (jnp.sum(top_scores, axis=-1, keepdims=True) + 1e-20)
        top_scores = top_scores * ROUTED_SCALE
        combine = jnp.sum(jax.nn.one_hot(top_idx, E, dtype=xt.dtype) * top_scores[..., None], axis=1)
        h = jnp.einsum('td,edh->eth', xt, w1)
        u = jnp.einsum('td,edh->eth', xt, w3)
        y = jnp.einsum('eth,ehd->etd', jax.nn.silu(h) * u, w2)
        routed = jnp.einsum('etd,te->td', y, combine)
        shared = jax.nn.silu(xt @ sw1) * (xt @ sw3) @ sw2
        return (routed + shared).reshape(b, s, d)
    x = L0_attn_hidden_states
    x = x + 0.5 * _L0_ffn_ref(_layernorm(x, axis=-1), L0_ffn_gate_w, L0_ffn_w1, L0_ffn_w2, L0_ffn_w3, L0_ffn_sw1, L0_ffn_sw2, L0_ffn_sw3)
    x = x + _L0_attn_ref(_layernorm(x, axis=-1), L0_attn_Wq, L0_attn_Wk, L0_attn_Wv, L0_attn_Wa, L0_attn_Wb, L0_attn_Wg, L0_attn_Wo, L0_attn_conv_wq, L0_attn_conv_wk, L0_attn_conv_wv, L0_attn_A_log, L0_attn_dt_bias, L0_attn_norm_weight)
    x = x + 0.5 * _L0_ffn_ref(_layernorm(x, axis=-1), L0_ffn_gate_w, L0_ffn_w1, L0_ffn_w2, L0_ffn_w3, L0_ffn_sw1, L0_ffn_sw2, L0_ffn_sw3)
    return x

_drawn_inputs = setup_inputs


def setup_inputs(seed=0):
    import zlib

    import numpy as np

    out = dict(_drawn_inputs(seed))
    spreads = {'L0_attn_norm_weight': (1.0, 0.2)}
    factors = {'L0_ffn_gate_w': 11.061,
     'L0_ffn_sw1': 4.208,
     'L0_ffn_sw2': 4.168,
     'L0_ffn_sw3': 4.177,
     'L0_ffn_w1': 3.321,
     'L0_ffn_w2': 3.29,
     'L0_ffn_w3': 3.301}
    for name, (base, spread) in spreads.items():
        noise = np.random.default_rng([zlib.crc32(name.encode()), seed]).standard_normal(out[name].shape)
        drawn = base * np.exp(spread * noise) if base else spread * noise
        out[name] = jnp.asarray(drawn.astype(out[name].dtype))
    for name, factor in factors.items():
        out[name] = (out[name] * factor).astype(out[name].dtype)
    return out
```

```python
from contextlib import ExitStack

import concourse.bass as bass
from concourse import mybir

ALU = mybir.AluOpType
ACT = mybir.ActivationFunctionType
AX_X = mybir.AxisListType.X
F32 = mybir.dt.float32
F32R = mybir.dt.float32r
BF16 = mybir.dt.bfloat16

P = 128
B, T, D = 8, 256, 256
CH = 32
NQ = P // CH
NG = B // NQ
NC = T // CH
NT = NG * NC
KD = D // P
NP = NT // 2
TOK = NT * P
E, HID = 8, 176
HT = (E * HID + HID + P - 1) // P
HF = HT * P
CHUNK = 512
NCHUNK = TOK // CHUNK
TPC = CHUNK // P
H, DK, DV = 6, 32, 64
QK, VD = H * DK, H * DV
FEAT = 2 * QK + VD
FM = FEAT // P
GAB = VD + 2 * H
KO = VD // P
INST = NT * H
IH = INST // 32
TAPS = 4
PAD = TAPS - 1
ROUTE = E + 1
EPS = 1e-5

C_ID, C_TRI, C_STR, C_BLK = 0, P, 2 * P, 3 * P
C_INC = 4 * P
C_NST = C_INC + CH
C_TIE = C_NST + CH
C_SEL = C_TIE + E * E
C_ALL = C_SEL + HF


def constants(np):
    c = np.zeros((P, C_ALL), np.float32)
    p = np.arange(P)
    same = p[:, None] // CH == p[None, :] // CH
    c[:, C_ID:C_ID + P] = np.eye(P)
    c[:, C_TRI:C_TRI + P] = same & (p[:, None] <= p[None, :])
    c[:, C_STR:C_STR + P] = same & (p[:, None] > p[None, :])
    c[:, C_BLK:C_BLK + P] = same
    t = np.arange(CH)
    c[:, C_INC:C_INC + CH] = (p % CH)[:, None] <= t[None, :]
    c[:, C_NST:C_NST + CH] = -1.0 * ((p % CH)[:, None] < t[None, :])
    e = np.arange(E)
    c[:, C_TIE:C_TIE + E * E] = (e[None, :] < e[:, None]).reshape(1, E * E)
    j = np.arange(HF)
    for r in range(3 * ROUTE):
        c[r, C_SEL:C_SEL + HF] = (j // HID == r % ROUTE) & (j < (E + 1) * HID)
    return c


def macaron(nc, x, wq, wk, wv, wg, wa, wb, wo, cwq, cwk, cwv, a_log, dt_bias, nw, gate_w,
            w1, w2, w3, sw1, sw2, sw3, consts, out):
    ctx = ExitStack()
    base = (nc.sbuf_base + 63) // 64 * 64
    room = nc.sbuf_usable_end - base

    def at(name, off, shape, dt=F32):
        size = 2 if dt == BF16 else 4
        n = size
        for s in shape[1:]:
            n *= s
        assert off + n <= room, (name, off + n, room)
        return nc.alloc_sbuf_tensor_at(name, shape, dt, offset=base + off)

    def sem(name):
        return ctx.enter_context(nc.semaphore(name))

    KB = 1024
    xres = at("xres", 0, [P, NT, D])
    xhi = at("xhi", 16 * KB, [P, KD, TOK], F32R)
    xlo = at("xlo", 32 * KB, [P, KD, TOK], F32R)
    o = 48 * KB
    ident = at("ident", o, [P, 4 * P + 2 * CH + E * E])
    o += 4 * (4 * P + 2 * CH + E * E)
    identb = at("identb", o, [P, P], BF16)
    o += 2 * P
    stats = at("stats", o, [P, NT, 6])
    o += 4 * NT * 6
    moments = at("moments", o, [P, NT, 2])
    o += 4 * NT * 2
    vareps = at("vareps", o, [P, NT])
    o += 4 * NT
    stdev = at("stdev", o, [P, NT])
    o += 4 * NT
    rstd = at("rstd", o, [P, NT])
    o += 4 * NT
    xn = at("xn", o, [P, 4, D])
    o += 16 * D
    F = (o + 63) // 64 * 64
    triu = ident[:, C_TRI:C_TRI + P]
    strict = ident[:, C_STR:C_STR + P]
    blocks = ident[:, C_BLK:C_BLK + P]
    incl = ident[:, C_INC:C_INC + CH]
    nstrict = ident[:, C_NST:C_NST + CH]
    tie = ident[:, C_TIE:C_TIE + E * E]

    WB = 4 * KD * HF
    W2B = 4 * HT * D
    assert WB == W2B
    ffn = []
    for f in range(2):
        t = {}
        for n, name in enumerate(["w1h", "w1l", "w3h", "w3l"]):
            t[name] = at(f"{name}_{f}", F + n * WB, [P, KD, HF], F32R)
        for n, name in enumerate(["w2h", "w2l"]):
            t[name] = at(f"{name}_{f}", F + (4 + n) * WB, [P, HT, D], F32R)
        r = F + 6 * WB
        t["r1"] = at(f"r1_{f}", r, [P, KD, HF])
        t["r3"] = at(f"r3_{f}", r + WB, [P, KD, HF])
        t["r2"] = at(f"r2_{f}", r + 2 * WB, [P, HT, D])
        C4 = 4 * CHUNK
        t["s"] = at(f"s_{f}", r, [P, 2, CHUNK])
        t["p"] = at(f"p_{f}", r + 2 * C4, [P, 2, CHUNK])
        t["a"] = at(f"a_{f}", r + 4 * C4, [P, 2, CHUNK])
        t["ahi"] = at(f"ahi_{f}", r + 6 * C4, [P, 3, CHUNK], F32R)
        t["alo"] = at(f"alo_{f}", r + 9 * C4, [P, 3, CHUNK], F32R)
        r += 3 * WB
        t["sel"] = at(f"sel_{f}", r, [P, HF], BF16)
        r += 2 * HF
        t["cT"] = at(f"cT_{f}", r, [P, TOK], BF16)
        r += 2 * TOK
        t["sT"] = at(f"sT_{f}", r, [P, TOK])
        t["gt"] = at(f"gt_{f}", r, [P, NT, E, E])
        t["eq"] = at(f"eq_{f}", r + 4 * NT * E * E, [P, NT, E, E])
        r += 4 * TOK
        for name in ["gr", "gh", "gl"]:
            t[name] = at(f"{name}_{f}", r, [P, KD, E], F32 if name == "gr" else F32R)
            r += 4 * KD * E
        for name in ["sc", "rank", "ss"]:
            t[name] = at(f"{name}_{f}", r, [P, NT, E])
            r += 4 * NT * E
        for name in ["cs", "cr"]:
            t[name] = at(f"{name}_{f}", r, [P, NT])
            r += 4 * NT
        t["c9"] = at(f"c9_{f}", r, [P, NT, ROUTE])
        r += 4 * NT * ROUTE
        t["c3"] = at(f"c3_{f}", r, [P, NT, 3 * ROUTE], BF16)
        r += 2 * NT * 3 * ROUTE
        ffn.append(t)
    FEND = (r + 63) // 64 * 64

    wqkv_r = at("wqkv_r", FEND, [P, KD, FEAT])
    wgab_r = at("wgab_r", FEND + 4 * KD * FEAT, [P, KD, GAB])
    o = FEND + 4 * KD * FEAT + 4 * KD * GAB
    wo_r = at("wo_r", o, [P, KO, D])
    AEND = o + 4 * KO * D
    woh = at("woh", F, [P, KO, D], F32R)
    wol = at("wol", F + 4 * KO * D, [P, KO, D], F32R)
    o = F + 8 * KO * D
    silug = at("silug", o, [P, NT, VD])
    o += 4 * NT * VD
    qkv = at("qkv", o, [P, NT, FEAT])
    o += 4 * NT * FEAT
    BR = o
    wqkvh = at("wqkvh", o, [P, KD, FEAT], F32R)
    wqkvl = at("wqkvl", o + 4 * KD * FEAT, [P, KD, FEAT], F32R)
    o += 8 * KD * FEAT
    wgabh = at("wgabh", o, [P, KD, GAB], F32R)
    wgabl = at("wgabl", o + 4 * KD * GAB, [P, KD, GAB], F32R)
    o += 8 * KD * GAB
    cb = at("cb", o, [P, 2, B, PAD + T])
    o += 8 * B * (PAD + T)
    ysum = at("ysum", o, [P, B, T])
    y = at("y", o + 4 * B * T, [P, NG, NC, NQ, CH])
    o += 8 * B * T
    assert o <= FEND, (o, FEND)
    SL = 4 * INST * CH
    kT = at("kT", BR, [P, NT, QK])
    qgT = at("qgT", BR + SL, [P, NT, QK])
    kb = at("kb", BR + SL, [P, NT, QK])
    dec = at("dec", BR + 2 * SL, [P, INST, CH])
    rhsd = at("rhsd", BR + 3 * SL, [P, INST, CH])
    ltn = at("ltn", BR + 3 * SL, [P, INST, CH])
    tt = at("tt", BR + 3 * SL, [P, INST, CH])
    o = BR + 4 * SL
    SB = 4 * NG * VD
    names = ["dlt", "tmpS", "tmpR"]
    dlt, tmpS, tmpR = (at(n, o + i * SB, [P, NG, VD]) for i, n in enumerate(names))
    tmpU = at("tmpU", o, [P, IH, 256])
    o += 3 * SB
    assert o <= room
    ab = at("ab", o, [P, NT, 2 * H])
    o += 4 * NT * 2 * H
    ss_qk = at("ss_qk", o, [P, NT, 2 * H])
    o += 4 * NT * 2 * H
    small = {}
    for n in ["z", "az", "ez", "w", "lnw", "isone", "sp", "g", "eb", "beta", "bG", "orms", "ostd"]:
        small[n] = at("sm_" + n, o, [P, NT, H])
        o += 4 * NT * H
    ge = at("ge", o, [P, 3, INST])
    o += 12 * INST
    o = max(o, AEND)
    cw = at("cw", o, [P, FM, TAPS])
    o += 4 * FM * TAPS
    alog, dtb = at("alog", o, [P, H]), at("dtb", o + 32, [P, H])
    o += 64
    nwt = at("nwt", o, [P, 1])
    o += 4
    kq = at("kq", 16 * KB, [P, 2, NT, QK])
    sq = at("sq", 16 * KB, [P, NT, 2 * QK])
    X = at("X", 16 * KB, [P, IH, CH, CH])
    U = at("U", 16 * KB + SL, [P, IH, CH, CH])
    S = at("S", 40 * KB, [P, NG, VD])
    R = at("R", 40 * KB + SB, [P, NG, VD])
    otr = 16 * KB
    oh = at("oh", otr, [P, 2, KO, P], F32R)
    ol = at("ol", otr + 8 * KO * P, [P, 2, KO, P], F32R)
    osq = at("osq", otr + 16 * KO * P, [P, NG, VD])

    ps = ctx.enter_context(nc.psum_tensor("ps", [P, 8, 512], F32))
    tri_out = nc.dram_tensor("tri_out", [NQ, INST, CH, CH], F32, kind="Internal").ap()
    inv_in = nc.dram_tensor("inv_in", [NQ, INST, CH, CH], F32, kind="Internal").ap()

    names = ("x_in const_in rw1 rw3 rw2 rgate rattn small_in x_out tri_w tri_r inv_w inv_r "
             "const_ok wh_ok wl_ok wgt_hi wgt_lo attn_hi attn_lo wo_sc "
             "ln_var ln_sd xn_ok tr_ok xhi_ok xlo_ok "
             "sc_ok sig_ok scT_ok c3_ok c3T_ok cT_ok "
             "h_ok uc_ok silu_ok p_ok a_ok ahi_ok alo_ok ystep y_ok res_ok "
             "padz cbz pj_ok pj_ev conv_ok tq_ok tq_ev gt_ok gt_ev dch "
             "l2_ss l2_sd z_ok ez_ok w_ok lnw_ok g_ok cum_ok ge_ok rhsd_ok dec_ok beta_ok kb_ok qk_ok "
             "kT_ok qT_ok mask_ok gm_ok gm_ev gm_n scaled_ok u_init inv_ok "
             "r_ok R_ok d_ok dlt_ok o_ok o_ev su_ok S_ok ost_ok osd_ok on_ok ot_ok oh_ok ol_ok wo_ok wo_ev kE_ok").split()
    s = {n: sem(n) for n in names}

    def gview(r):
        return r.rearrange("p (c b t) -> p c b t", c=TPC, b=NQ)

    def acc3(pe, dst, lh, ll, rh, rl, start, stop, **kw):
        pe.matmul(dst, ll, rh, start=start, stop=False, **kw)
        pe.matmul(dst, lh, rl, start=False, stop=False, **kw)
        return pe.matmul(dst, lh, rh, start=False, stop=stop, **kw)

    block = ctx.enter_context(nc.Block())

    @block.sync
    def _(sp):
        for b in range(B):
            g, q = divmod(b, NQ)
            sp.dma_start(xres[CH * q:CH * q + CH, g * NC:(g + 1) * NC, :],
                         x[b].rearrange("(c t) d -> t c d", t=CH)).then_inc(s["x_in"], 16)
        sp.dma_start(ident[:, :], consts[:, 0:C_SEL]).then_inc(s["const_in"], 16)
        sp.dma_start(ffn[0]["sT"][:, 0:HF], consts[:, C_SEL:C_ALL]).then_inc(s["const_in"], 16)

        def load_ffn(f):
            t = ffn[f]
            RT = E * HID
            for k in range(KD):
                sp.dma_start(t["gr"][:, k, :], gate_w[k * P:(k + 1) * P, :]).then_inc(s["rgate"], 16)
            for key, w, sw, sm in (("r1", w1, sw1, "rw1"), ("r3", w3, sw3, "rw3")):
                for k in range(KD):
                    sp.dma_start(t[key][:, k, 0:RT].rearrange("p (e h) -> p e h", e=E),
                                 w[:, k * P:(k + 1) * P, :].rearrange("e p h -> p e h")).then_inc(s[sm], 16)
                    sp.dma_start(t[key][:, k, RT:RT + HID], sw[k * P:(k + 1) * P, :]).then_inc(s[sm], 16)
            n = RT // P
            sp.dma_start(t["r2"][:, 0:n, :],
                         w2.rearrange("e h d -> (e h) d").rearrange("(n p) d -> p n d", p=P)).then_inc(s["rw2"], 16)
            sp.dma_start(t["r2"][:, n, :], sw2[0:P, :]).then_inc(s["rw2"], 16)
            sp.wait_ge(s["padz"], 3 * (f + 1))
            sp.dma_start(t["r2"][0:HID - P, n + 1, :], sw2[P:HID, :]).then_inc(s["rw2"], 16)

        load_ffn(0)
        for k in range(KD):
            r = slice(k * P, (k + 1) * P)
            sp.dma_start(wqkv_r[:, k, 0:QK], wq[r, :]).then_inc(s["rattn"], 16)
            sp.dma_start(wqkv_r[:, k, QK:2 * QK], wk[r, :]).then_inc(s["rattn"], 16)
            sp.dma_start(wqkv_r[:, k, 2 * QK:FEAT], wv[r, :]).then_inc(s["rattn"], 16)
            sp.dma_start(wgab_r[:, k, 0:VD], wg[r, :]).then_inc(s["rattn"], 16)
            sp.dma_start(wgab_r[:, k, VD:VD + H], wa[r, :]).then_inc(s["rattn"], 16)
            sp.dma_start(wgab_r[:, k, VD + H:GAB], wb[r, :]).then_inc(s["rattn"], 16)
        sp.dma_start(wo_r[:, :, :], wo.rearrange("(k p) d -> p k d", p=P)).then_inc(s["rattn"], 16)
        row = 0
        for w, rows in ((cwq, QK), (cwk, QK), (cwv, VD)):
            done = 0
            while done < rows:
                m, p0 = divmod(row, P)
                n = min(P - p0, rows - done)
                sp.dma_start(cw[p0:p0 + n, m, :], w[done:done + n, :]).then_inc(s["small_in"], 16)
                done += n
                row += n
        sp.dma_start(alog[:, :], a_log).then_inc(s["small_in"], 16)
        sp.dma_start(dtb[:, :], dt_bias).then_inc(s["small_in"], 16)
        for r in range(P // DV):
            sp.dma_start(nwt[r * DV:(r + 1) * DV, :], nw).then_inc(s["small_in"], 16)

        sp.wait_ge(s["gm_ev"], INST // 8)
        for q in range(NQ):
            sp.dma_start(tri_out[q].rearrange("n s t -> s n t"),
                         ltn[CH * q:CH * q + CH, :, :]).then_inc(s["tri_w"], 16)
        sp.wait_ge(s["tri_w"], 16 * NQ)
        sp.dma_start(X[:, :, :, :].rearrange("p h s t -> p (h s t)"),
                     tri_out.rearrange("q (n h) s t -> (q n) (h s t)", h=IH)).then_inc(s["tri_r"], 16)
        sp.wait_ge(s["inv_ok"], 1)
        sp.dma_start(inv_in.rearrange("q (n h) s t -> (q n) (h s t)", h=IH),
                     U[:, :, :, :].rearrange("p h s t -> p (h s t)")).then_inc(s["inv_w"], 16)
        sp.wait_ge(s["inv_w"], 16)
        for q in range(NQ):
            sp.dma_start(tt[CH * q:CH * q + CH, :, :],
                         inv_in[q].rearrange("n s t -> s n t")).then_inc(s["inv_r"], 16)

        sp.wait_ge(s["o_ok"], NC)
        sp.wait_ge(s["S_ok"], NC - 1)
        sp.wait_ge(s["wo_ev"], NT)
        load_ffn(1)
        sp.dma_start(ffn[1]["sT"][:, 0:HF], consts[:, C_SEL:C_ALL]).then_inc(s["const_in"], 16)

        sp.wait_ge(s["res_ok"], 1 + 2 * NCHUNK)
        for b in range(B):
            g, q = divmod(b, NQ)
            sp.dma_start(out[b].rearrange("(c t) d -> t c d", t=CH),
                         xres[CH * q:CH * q + CH, g * NC:(g + 1) * NC, :]).then_inc(s["x_out"], 16)
        sp.wait_ge(s["x_out"], 16 * B)

    @block.tensor
    def _(pe):
        def layernorm(ph):
            if ph == 0:
                pe.wait_ge(s["const_in"], 32)
            for n in range(NT):
                m = n // 2
                pe.wait_ge(s["xn_ok"], NT * ph + n + 1)
                if n % 2 == 0 and m >= 4:
                    pe.wait_ge(s["xlo_ok"], NP * ph + m - 3)
                for k in range(KD):
                    mm = pe.transpose(ps[:, m % 4, k * 2 * P + (n % 2) * P:k * 2 * P + (n % 2) * P + P],
                                      xn[:, n % 4, k * P:(k + 1) * P], ident[:, C_ID:C_ID + P])
                mm.then_inc(s["tr_ok"], 1)

        def route(f):
            t = ffn[f]
            ph = 2 * f
            pe.wait_ge(s["xlo_ok"], NP * (ph + 1))
            pe.wait_ge(s["wgt_lo"], f + 1)
            for i in range(NCHUNK):
                for k in range(KD):
                    c = slice(i * CHUNK, (i + 1) * CHUNK)
                    mm = acc3(pe, ps[0:E, i, :], t["gh"][:, k, :], t["gl"][:, k, :], xhi[:, k, c], xlo[:, k, c],
                              k == 0, k == KD - 1)
                mm.then_inc(s["sc_ok"], 1)
            pe.wait_ge(s["sig_ok"], NCHUNK * (f + 1))
            for n in range(NT):
                mm = pe.transpose(ps[:, 4, n * E:(n + 1) * E], t["sT"][0:E, n * P:(n + 1) * P],
                                  ident[0:E, C_ID:C_ID + E])
            mm.then_inc(s["scT_ok"], 1)
            pe.wait_ge(s["c3_ok"], f + 1)
            half = NT // 2
            for n in range(NT):
                v = ps[0:3 * ROUTE, 5 + n // half, :].bitcast(BF16)
                mm = pe.transpose(v[:, (n % half) * P:(n % half + 1) * P], t["c3"][:, n, :], identb[:, :])
            mm.then_inc(s["c3T_ok"], 1)
            pe.wait_ge(s["cT_ok"], 2 * (f + 1))
            pe.wait_ge(s["wl_ok"], 3 * (f + 1))

        def feed_forward(f):
            t = ffn[f]
            route(f)
            with pe.Fori(0, NCHUNK) as i:
                c = bass.ds(i * CHUNK, CHUNK)
                steps = HT * NCHUNK * f + i * HT

                def down(j):
                    pe.wait_ge(s["alo_ok"], steps + j + 2)
                    if j == 0:
                        pe.wait_ge(s["res_ok"], 1 + i + NCHUNK * f)
                    for q in range(TPC):
                        dst = ps[:, 6 + q // 2, (q % 2) * D:(q % 2 + 1) * D]
                        tok = slice(q * P, (q + 1) * P)
                        mm = acc3(pe, dst, t["ahi"][:, j % 3, tok], t["alo"][:, j % 3, tok],
                                  t["w2h"][:, j, :], t["w2l"][:, j, :],
                                  j == 0 and q % 2 == 0, j == HT - 1, skip_group_check=True)
                    mm.then_inc(s["ystep"], 1)

                for j in range(HT):
                    hid = slice(j * P, (j + 1) * P)
                    pe.wait_ge(s["silu_ok"], 1 + steps + max(j - 1, 0))
                    for k in range(KD):
                        mm = acc3(pe, ps[:, j % 2, :], t["w1h"][:, k, hid], t["w1l"][:, k, hid],
                                  xhi[:, k, c], xlo[:, k, c], k == 0, k == KD - 1)
                    mm.then_inc(s["h_ok"], 1)
                    pe.wait_ge(s["a_ok"], 1 + steps + max(j - 1, 0))
                    for k in range(KD):
                        acc3(pe, ps[:, 2 + j % 2, :], t["w3h"][:, k, hid], t["w3l"][:, k, hid],
                             xhi[:, k, c], xlo[:, k, c], k == 0, k == KD - 1)
                    pe.matmul(ps[:, 4 + j % 2, :], t["sel"][0:3 * ROUTE, hid], t["cT"][0:3 * ROUTE, c],
                              start=True, stop=True).then_inc(s["uc_ok"], 1)
                    if j >= 2:
                        down(j - 2)
                down(HT - 2)
                down(HT - 1)

        def project():
            pe.wait_ge(s["xlo_ok"], 2 * NP)
            pe.wait_ge(s["attn_lo"], 2)

            def features(m):
                for ch in range(NCHUNK):
                    n = m * NCHUNK + ch
                    if n >= 4:
                        pe.wait_ge(s["pj_ev"], n - 3)
                    c = slice(ch * CHUNK, (ch + 1) * CHUNK)
                    f = slice(m * P, (m + 1) * P)
                    for k in range(KD):
                        mm = acc3(pe, ps[:, n % 4, :], wqkvh[:, k, f], wqkvl[:, k, f], xhi[:, k, c], xlo[:, k, c],
                                  k == 0, k == KD - 1)
                    mm.then_inc(s["pj_ok"], 1)

            def turn(m):
                pe.wait_ge(s["conv_ok"], m + 1)
                for r in range(4):
                    if m > 0:
                        pe.wait_ge(s["tq_ev"], 4 * (m - 1) + r + 1)
                    for i in range(4):
                        g, c = divmod(4 * r + i, NC)
                        mm = pe.transpose(ps[:, 4 + r, i * P:(i + 1) * P],
                                          y[:, g, c, :, :].rearrange("p b t -> p (b t)"),
                                          ident[:, C_ID:C_ID + P])
                    mm.then_inc(s["tq_ok"], 1)

            features(0)
            features(1)
            for m in range(FM):
                turn(m)
                if m + 2 < FM:
                    features(m + 2)
            for n in range(NT):
                pe.wait_ge(s["pj_ev"], FM * NCHUNK)
                if n >= 4:
                    pe.wait_ge(s["gt_ev"], n - 3)
                c = slice(n * P, (n + 1) * P)
                for k in range(KD):
                    mm = acc3(pe, ps[:, n % 4, 0:GAB], xhi[:, k, c], xlo[:, k, c], wgabh[:, k, :], wgabl[:, k, :],
                              k == 0, k == KD - 1)
                mm.then_inc(s["gt_ok"], 1)

        def decays():
            pe.wait_ge(s["gt_ev"], NT)
            pe.wait_ge(s["tq_ev"], 4 * FM)
            pe.wait_ge(s["g_ok"], 1)
            gall = small["g"][:, :, :].rearrange("p n h -> p (n h)")
            for r, m in enumerate((triu, strict, blocks)):
                mm = pe.matmul(ps[:, 0, r * INST:(r + 1) * INST], m, gall, start=True, stop=True)
            mm.then_inc(s["cum_ok"], 1)
            pe.wait_ge(s["rhsd_ok"], 1)
            per = 512 // CH
            for r in range(INST // per):
                pe.matmul(ps[:, 1 + r, :], strict, rhsd[:, r * per:(r + 1) * per, :], start=True,
                          stop=True).then_inc(s["cum_ok"], 1)

        def grams():
            pe.wait_ge(s["kT_ok"], 1)
            pe.wait_ge(s["qT_ok"], 1)
            pe.wait_ge(s["dec_ok"], INST * CH // 512)
            pe.wait_ge(s["ge_ok"], 1)
            for i in range(INST):
                n, h = divmod(i, H)
                bank = (i // 8) % 8
                if i % 8 == 0 and i >= 64:
                    pe.wait_ge(s["gm_ev"], i // 8 - 7)
                f = slice(h * DK, (h + 1) * DK)
                for q in range(NQ):
                    r = slice(CH * q, CH * q + CH)
                    mm = pe.matmul(ps[r, bank, (i % 8) * 2 * CH:(i % 8 + 1) * 2 * CH], kT[r, n, f], kq[r, :, n, f],
                                   start=True, stop=True)
                if i % 8 == 7:
                    mm.then_inc(s["gm_ok"], 1)

        def chunk_steps():
            pe.wait_ge(s["inv_r"], 16 * NQ)
            pe.wait_ge(s["gm_ev"], INST // 8)
            pe.wait_ge(s["scaled_ok"], 1)
            pe.wait_ge(s["kE_ok"], 2)

            def each():
                for g in range(NG):
                    for h in range(H):
                        for q in range(NQ):
                            yield g, h, slice(CH * q, CH * q + CH), slice(h * DV, (h + 1) * DV)

            for c in range(NC):
                if c > 0:
                    pe.wait_ge(s["S_ok"], c)
                    if c > 1:
                        pe.wait_ge(s["R_ok"], c)
                    for g, h, r, v in each():
                        mm = pe.matmul(ps[r, g, v], kT[r, g * NC + c, h * DK:(h + 1) * DK], S[r, g, v],
                                       start=True, stop=True)
                    mm.then_inc(s["r_ok"], 1)
                    pe.wait_ge(s["o_ev"], c)
                    for g, h, r, v in each():
                        pe.matmul(ps[r, 4 + g, v], qgT[r, g * NC + c, h * DK:(h + 1) * DK], S[r, g, v],
                                  start=(h == 0), stop=False, skip_group_check=True)
                pe.wait_ge(s["R_ok"], c + 1)
                for g, h, r, v in each():
                    mm = pe.matmul(ps[r, 2 + g, v], tt[r, (g * NC + c) * H + h, :], R[r, g, v],
                                   start=True, stop=True)
                mm.then_inc(s["d_ok"], 1)
                pe.wait_ge(s["dlt_ok"], c + 1)
                if c < NC - 1:
                    if c > 0:
                        pe.wait_ge(s["S_ok"], c)
                    for g, h, r, v in each():
                        mm = pe.matmul(ps[r, 6 + g, v], qkv[r, g * NC + c, QK + h * DK:QK + (h + 1) * DK],
                                       dlt[r, g, v], start=True, stop=True)
                    mm.then_inc(s["su_ok"], 1)
                for g, h, r, v in each():
                    mm = pe.matmul(ps[r, 4 + g, v], dec[r, (g * NC + c) * H + h, :], dlt[r, g, v],
                                   start=(c == 0 and h == 0), stop=True, skip_group_check=True)
                mm.then_inc(s["o_ok"], 1)

        def output():
            pe.wait_ge(s["wo_sc"], 3)
            pe.wait_ge(s["dlt_ok"], NC)
            for i in range(NT + 1):
                if i < NT:
                    c, g = divmod(i, NG)
                    n = g * NC + c
                    if g == 0:
                        pe.wait_ge(s["on_ok"], c + 1)
                    if i >= 2:
                        pe.wait_ge(s["ol_ok"], i - 1)
                    for k in range(KO):
                        mm = pe.transpose(ps[:, i % 2, k * P:(k + 1) * P],
                                          qkv[:, n, 2 * QK + k * P:2 * QK + (k + 1) * P], ident[:, C_ID:C_ID + P])
                    mm.then_inc(s["ot_ok"], 1)
                if i >= 1:
                    j = i - 1
                    pe.wait_ge(s["ol_ok"], j + 1)
                    if j >= 2:
                        pe.wait_ge(s["wo_ev"], j - 1)
                    for k in range(KO):
                        mm = acc3(pe, ps[:, 2 + j % 2, 0:D], oh[:, j % 2, k, :], ol[:, j % 2, k, :],
                                  woh[:, k, :], wol[:, k, :], k == 0, k == KO - 1)
                    mm.then_inc(s["wo_ok"], 1)

        pe.sem_inc(s["ystep"], 1)
        layernorm(0)
        feed_forward(0)
        layernorm(1)
        project()
        decays()
        grams()
        chunk_steps()
        output()
        layernorm(2)
        feed_forward(1)

    @block.scalar
    def _(act):
        def layernorm(ph):
            act.wait_ge(s["ln_var"], ph + 1)
            act.activation(stdev[:, :], vareps[:, :], ACT.Sqrt).then_inc(s["ln_sd"], 1)
            for m in range(NP):
                act.wait_ge(s["tr_ok"], NT * ph + 2 * m + 2)
                act.copy(xhi[:, :, m * 2 * P:(m + 1) * 2 * P],
                         ps[:, m % 4, :].rearrange("p (k t) -> p k t", k=KD)).then_inc(s["xhi_ok"], 1)

        def split_weights(f):
            t = ffn[f]
            act.wait_ge(s["rgate"], 32 * (f + 1))
            if f == 1:
                act.wait_ge(s["wo_ev"], NT)
            act.copy(t["gh"][:, :, :], t["gr"][:, :, :]).then_inc(s["wgt_hi"], 1)
            act.wait_ge(s["padz"], 3 * (f + 1))
            act.wait_ge(s["rw1"], 64 * (f + 1))
            act.copy(t["w1h"][:, :, :], t["r1"][:, :, :]).then_inc(s["wh_ok"], 1)
            act.wait_ge(s["rw3"], 64 * (f + 1))
            act.copy(t["w3h"][:, :, :], t["r3"][:, :, :]).then_inc(s["wh_ok"], 1)
            act.wait_ge(s["rw2"], 48 * (f + 1))
            act.copy(t["w2h"][:, :, :], t["r2"][:, :, :]).then_inc(s["wh_ok"], 1)

        def feed_forward(f):
            t = ffn[f]
            for i in range(NCHUNK):
                act.wait_ge(s["sc_ok"], NCHUNK * f + i + 1)
                if i == 0:
                    act.wait_ge(s["const_ok"], 2 + f)
                act.activation(t["sT"][0:E, i * CHUNK:(i + 1) * CHUNK], ps[0:E, i, :],
                               ACT.Sigmoid).then_inc(s["sig_ok"], 1)
            act.wait_ge(s["cT_ok"], 2 * (f + 1))
            with act.Fori(0, NCHUNK) as i:
                steps = HT * NCHUNK * f + i * HT

                def high(j):
                    act.wait_ge(s["a_ok"], steps + j + 2)
                    act.wait_ge(s["ystep"], 1 + steps + max(j - 2, 0))
                    act.copy(t["ahi"][:, j % 3, :], t["a"][:, j % 2, :]).then_inc(s["ahi_ok"], 1)

                for j in range(HT):
                    act.wait_ge(s["h_ok"], steps + j + 1)
                    act.wait_ge(s["p_ok"], 1 + steps + max(j - 1, 0))
                    act.activation(t["s"][:, j % 2, :], ps[:, j % 2, :], ACT.Silu).then_inc(s["silu_ok"], 1)
                    if j >= 1:
                        high(j - 1)
                high(HT - 1)

        def project():
            act.wait_ge(s["rattn"], 16 * 13)
            act.wait_ge(s["res_ok"], 1 + NCHUNK)
            act.copy(wqkvh[:, :, :], wqkv_r[:, :, :]).then_inc(s["attn_hi"], 1)
            act.copy(wgabh[:, :, :], wgab_r[:, :, :]).then_inc(s["attn_hi"], 1)
            act.wait_ge(s["wo_sc"], 1)
            act.copy(woh[:, :, :], wo_r[:, :, :]).then_inc(s["wo_sc"], 1)

        def convolve():
            act.wait_ge(s["small_in"], 16 * 11)
            act.wait_ge(s["cbz"], 1)

            def silu_turned(m):
                for r in range(4):
                    act.wait_ge(s["tq_ok"], 4 * m + r + 1)
                    act.activation(qkv[:, 4 * r:4 * r + 4, m * P:(m + 1) * P],
                                   ps[:, 4 + r, :].rearrange("p (n f) -> p n f", n=4),
                                   ACT.Silu).then_inc(s["tq_ev"], 1)

            for m in range(FM):
                for ch in range(NCHUNK):
                    n = m * NCHUNK + ch
                    g, half = divmod(ch, 2)
                    act.wait_ge(s["pj_ok"], n + 1)
                    if m >= 2:
                        act.wait_ge(s["conv_ok"], m - 1)
                    t0 = PAD + half * TPC * CH
                    act.copy(cb[:, m % 2, g * NQ:(g + 1) * NQ, t0:t0 + TPC * CH].rearrange(
                        "p b (c t) -> p c b t", c=TPC), gview(ps[:, n % 4, :])).then_inc(s["pj_ev"], 1)
                if m >= 1:
                    silu_turned(m - 1)
            silu_turned(FM - 1)
            for n in range(NT):
                act.wait_ge(s["gt_ok"], n + 1)
                act.activation(silug[:, n, :], ps[:, n % 4, 0:VD], ACT.Silu)
                act.copy(ab[:, n, :], ps[:, n % 4, VD:GAB]).then_inc(s["gt_ev"], 1)

        def gates():
            act.wait_ge(s["l2_ss"], 1)
            act.wait_ge(s["wo_sc"], 3)
            act.activation(ss_qk[:, :, 0:H], ss_qk[:, :, 0:H], ACT.Sqrt, scale=float(DK)).then_inc(s["l2_sd"], 1)
            act.activation(ss_qk[:, :, H:2 * H], ss_qk[:, :, H:2 * H], ACT.Sqrt).then_inc(s["l2_sd"], 1)
            act.wait_ge(s["z_ok"], 1)
            act.activation(small["ez"][:, :, :], small["az"][:, :, :], ACT.Exp, scale=-1.0).then_inc(s["ez_ok"], 1)
            act.activation(small["eb"][:, :, :], ab[:, :, H:2 * H], ACT.Exp, scale=-1.0).then_inc(s["ez_ok"], 1)
            act.activation(alog[:, :], alog[:, :], ACT.Exp).then_inc(s["ez_ok"], 1)
            act.wait_ge(s["w_ok"], 1)
            act.activation(small["lnw"][:, :, :], small["w"][:, :, :], ACT.Ln).then_inc(s["lnw_ok"], 1)
            act.wait_ge(s["cum_ok"], 1)
            act.activation(ge[:, :, :].rearrange("p r i -> p (r i)"), ps[:, 0, 0:3 * INST],
                           ACT.Exp).then_inc(s["ge_ok"], 1)
            per = 512 // CH
            for r in range(INST // per):
                act.wait_ge(s["cum_ok"], r + 2)
                act.activation(dec[:, r * per:(r + 1) * per, :].rearrange("p i t -> p (i t)"), ps[:, 1 + r, :],
                               ACT.Exp).then_inc(s["dec_ok"], 1)

        def chunk_steps():
            for c in range(NC):
                act.wait_ge(s["d_ok"], c + 1)
                if c > 0:
                    act.wait_ge(s["o_ok"], c)
                act.copy(dlt[:, :, :], ps[:, 2:4, 0:VD]).then_inc(s["dlt_ok"], 1)
                act.wait_ge(s["o_ok"], c + 1)
                act.wait_ge(s["R_ok"], c + 1)
                for g in range(NG):
                    e = act.copy(qkv[:, g * NC + c, 2 * QK:FEAT], ps[:, 4 + g, 0:VD])
                e.then_inc(s["o_ev"], 1)
                act.wait_ge(s["ost_ok"], c + 1)
                act.activation(small["ostd"][:, :, :].rearrange("p n h -> p (n h)")[:, c * NG * H:(c + 1) * NG * H],
                               small["orms"][:, :, :].rearrange("p n h -> p (n h)")[:, c * NG * H:(c + 1) * NG * H],
                               ACT.Sqrt).then_inc(s["osd_ok"], 1)

        def output():
            for i in range(NT):
                act.wait_ge(s["ot_ok"], i + 1)
                if i >= 2:
                    act.wait_ge(s["wo_ok"], i - 1)
                act.copy(oh[:, i % 2, :, :].rearrange("p k t -> p (k t)"),
                         ps[:, i % 2, 0:KO * P]).then_inc(s["oh_ok"], 1)

        act.sem_inc(s["silu_ok"], 1)
        split_weights(0)
        layernorm(0)
        feed_forward(0)
        project()
        layernorm(1)
        convolve()
        gates()
        chunk_steps()
        output()
        layernorm(2)
        split_weights(1)
        feed_forward(1)

    @block.gpsimd
    def _(pool):
        def split_weights(f):
            t = ffn[f]
            RT = (E + 1) * HID
            if f == 1:
                pool.wait_ge(s["wo_ev"], NT)
            pool.memset(t["r1"][:, :, RT:HF], 0.0).then_inc(s["padz"], 1)
            pool.memset(t["r3"][:, :, RT:HF], 0.0).then_inc(s["padz"], 1)
            pool.memset(t["r2"][:, HT - 1, :], 0.0).then_inc(s["padz"], 1)
            pool.wait_ge(s["rgate"], 32 * (f + 1))
            pool.wait_ge(s["wgt_hi"], f + 1)
            pool.tensor_tensor(t["gl"][:, :, :], t["gr"][:, :, :], t["gh"][:, :, :].bitcast(F32),
                               ALU.subtract).then_inc(s["wgt_lo"], 1)
            for r, (raw, hi, lo) in enumerate((("r1", "w1h", "w1l"), ("r3", "w3h", "w3l"), ("r2", "w2h", "w2l"))):
                pool.wait_ge(s["wh_ok"], 3 * f + r + 1)
                pool.tensor_tensor(t[lo][:, :, :], t[raw][:, :, :], t[hi][:, :, :].bitcast(F32),
                                   ALU.subtract).then_inc(s["wl_ok"], 1)

        def feed_forward(f):
            t = ffn[f]
            pool.wait_ge(s["cT_ok"], 2 * (f + 1))
            with pool.Fori(0, NCHUNK) as i:
                steps = HT * NCHUNK * f + i * HT
                for j in range(HT):
                    pool.wait_ge(s["ahi_ok"], steps + j + 1)
                    pool.tensor_tensor(t["alo"][:, j % 3, :], t["a"][:, j % 2, :],
                                       t["ahi"][:, j % 3, :].bitcast(F32), ALU.subtract).then_inc(s["alo_ok"], 1)

        def attention():
            pool.wait_ge(s["res_ok"], 1 + NCHUNK)
            pool.memset(cb[:, :, :, 0:PAD], 0.0).then_inc(s["cbz"], 1)
            pool.wait_ge(s["attn_hi"], 2)
            pool.tensor_tensor(wqkvl[:, :, :], wqkv_r[:, :, :], wqkvh[:, :, :].bitcast(F32),
                               ALU.subtract).then_inc(s["attn_lo"], 1)
            pool.tensor_tensor(wgabl[:, :, :], wgab_r[:, :, :], wgabh[:, :, :].bitcast(F32),
                               ALU.subtract).then_inc(s["attn_lo"], 1)
            pool.wait_ge(s["wo_sc"], 2)
            pool.tensor_tensor(wol[:, :, :], wo_r[:, :, :], woh[:, :, :].bitcast(F32),
                               ALU.subtract).then_inc(s["wo_sc"], 1)
            pool.wait_ge(s["g_ok"], 1)
            pool.wait_ge(s["tq_ev"], 4 * FM)
            gall = small["g"][:, :, :].rearrange("p n h -> p (n h)")
            pool.tensor_tensor(rhsd[:, :, :], gall.unsqueeze(2).broadcast_to((P, INST, CH)),
                               incl.unsqueeze(1).broadcast_to((P, INST, CH)), ALU.mult).then_inc(s["rhsd_ok"], 1)
            pool.wait_ge(s["beta_ok"], 1)
            pool.wait_ge(s["qk_ok"], 1)
            pool.tensor_tensor(kb[:, :, :].rearrange("p n (h d) -> p n h d", h=H),
                               qkv[:, :, QK:2 * QK].rearrange("p n (h d) -> p n h d", h=H),
                               small["beta"][:, :, :].unsqueeze(3).broadcast_to((P, NT, H, DK)),
                               ALU.mult).then_inc(s["kb_ok"], 1)
            pool.wait_ge(s["cum_ok"], 1 + INST * CH // 512)
            pool.wait_ge(s["dec_ok"], INST * CH // 512)
            pool.tensor_tensor(ltn[:, :, :], dec[:, :, :], nstrict.unsqueeze(1).broadcast_to((P, INST, CH)),
                               ALU.mult).then_inc(s["mask_ok"], 1)
            pool.wait_ge(s["mask_ok"], 1)
            pool.tensor_tensor(dec[:, :, :], dec[:, :, :], incl.unsqueeze(1).broadcast_to((P, INST, CH)),
                               ALU.mult).then_inc(s["mask_ok"], 1)
            pool.wait_ge(s["kT_ok"], 1)
            pool.wait_ge(s["kb_ok"], 1)
            pool.wait_ge(s["ge_ok"], 1)
            kv = qkv[:, :, QK:2 * QK].rearrange("p n (h d) -> p n h d", h=H)
            pool.tensor_tensor(kv, kv, ge[:, 1, :].rearrange("p (n h) -> p n h", h=H).unsqueeze(3).broadcast_to(
                (P, NT, H, DK)), ALU.mult).then_inc(s["kE_ok"], 1)
            vv = qkv[:, :, 2 * QK:FEAT].rearrange("p n (h d) -> p n h d", h=H)
            pool.tensor_tensor(vv, vv, small["beta"][:, :, :].unsqueeze(3).broadcast_to((P, NT, H, DV)),
                               ALU.mult).then_inc(s["kE_ok"], 1)
            pool.wait_ge(s["gm_ok"], INST // 8)
            pool.memset(U[:, :, :, :], 0.0).then_inc(s["u_init"], 1)
            pool.wait_ge(s["u_init"], 1)
            pool.memset(U[:, :, :, :].rearrange("p h s t -> p h (s t)")[:, :, 0:CH * CH:CH + 1],
                        1.0).then_inc(s["u_init"], 1)

        pool.sem_inc(s["alo_ok"], 1)
        split_weights(0)
        feed_forward(0)
        attention()
        split_weights(1)
        feed_forward(1)

    @block.vector
    def _(v):
        chain = [0]

        def link(ins):
            chain[0] += 1
            ins.then_inc(s["dch"], 1)
            v.wait_ge(s["dch"], chain[0])

        def layernorm(ph):
            if ph == 0:
                v.wait_ge(s["x_in"], 16 * B)
            for n in range(NT):
                e = v.bn_stats(stats[:, n, :], xres[:, n, :])
            link(e)
            for n in range(NT):
                e = v.bn_aggr(moments[:, n, :], stats[:, n, :])
            link(e)
            v.tensor_scalar(vareps[:, :], moments[:, :, 1], EPS, None, ALU.add).then_inc(s["ln_var"], 1)
            v.wait_ge(s["ln_sd"], ph + 1)
            link(v.reciprocal(rstd[:, :], stdev[:, :]))

            def normal(n):
                if n >= 4:
                    v.wait_ge(s["tr_ok"], NT * ph + n - 3)
                v.tensor_scalar(xn[:, n % 4, :], xres[:, n, :], moments[:, n, 0:1], rstd[:, n:n + 1],
                                ALU.subtract, ALU.mult).then_inc(s["xn_ok"], 1)

            for n in range(4):
                normal(n)
            for m in range(NP):
                v.wait_ge(s["xhi_ok"], NP * ph + m + 1)
                c = slice(m * 2 * P, (m + 1) * 2 * P)
                v.tensor_tensor(xlo[:, :, c], ps[:, m % 4, :].rearrange("p (k t) -> p k t", k=KD),
                                xhi[:, :, c].bitcast(F32), ALU.subtract).then_inc(s["xlo_ok"], 1)
                for n in (2 * m + 4, 2 * m + 5):
                    if n < NT:
                        normal(n)

        def route(f):
            t = ffn[f]
            v.wait_ge(s["scT_ok"], f + 1)
            link(v.tensor_copy(t["sc"][:, :, :], ps[:, 4, 0:NT * E].rearrange("p (n e) -> p n e", e=E)))
            over = t["sc"][:, :, :].unsqueeze(2).broadcast_to((P, NT, E, E))
            mine = t["sc"][:, :, :].unsqueeze(3).broadcast_to((P, NT, E, E))
            v.tensor_tensor(t["gt"][:, :, :, :], over, mine, ALU.is_gt)
            link(v.tensor_tensor(t["eq"][:, :, :, :], over, mine, ALU.is_equal))
            eqf = t["eq"][:, :, :, :].rearrange("p n a b -> p n (a b)")
            link(v.tensor_tensor(eqf, eqf, tie.unsqueeze(1).broadcast_to((P, NT, E * E)), ALU.mult))
            link(v.tensor_tensor(t["gt"][:, :, :, :], t["gt"][:, :, :, :], t["eq"][:, :, :, :], ALU.add))
            link(v.tensor_reduce(t["rank"][:, :, :], t["gt"][:, :, :, :], AX_X, ALU.add))
            link(v.tensor_scalar(t["rank"][:, :, :], t["rank"][:, :, :], 1.5, None, ALU.is_lt))
            link(v.tensor_tensor(t["ss"][:, :, :], t["rank"][:, :, :], t["sc"][:, :, :], ALU.mult))
            link(v.tensor_reduce(t["cs"][:, :], t["ss"][:, :, :], AX_X, ALU.add))
            link(v.tensor_scalar(t["cs"][:, :], t["cs"][:, :], 1e-20, None, ALU.add))
            link(v.reciprocal(t["cr"][:, :], t["cs"][:, :]))
            link(v.tensor_scalar(t["cr"][:, :], t["cr"][:, :], 2.5 * 0.5, None, ALU.mult))
            v.memset(t["c9"][:, :, E:ROUTE], 0.5)
            link(v.tensor_tensor(t["c9"][:, :, 0:E], t["ss"][:, :, :],
                                 t["cr"][:, :].unsqueeze(2).broadcast_to((P, NT, E)), ALU.mult))
            for r in range(3):
                part = t["c3"][:, :, r * ROUTE:(r + 1) * ROUTE]
                e = v.tensor_copy(part, t["c9"][:, :, :])
                if r < 2:
                    link(e)
                    link(v.tensor_tensor(t["c9"][:, :, :], t["c9"][:, :, :], part, ALU.subtract))
            e.then_inc(s["c3_ok"], 1)
            v.wait_ge(s["c3T_ok"], f + 1)
            for r in range(2):
                v.tensor_copy(t["cT"][0:3 * ROUTE, r * TOK // 2:(r + 1) * TOK // 2],
                              ps[0:3 * ROUTE, 5 + r, :].bitcast(BF16)).then_inc(s["cT_ok"], 1)

        def feed_forward(f):
            t = ffn[f]
            if f == 0:
                v.wait_ge(s["const_in"], 32)
                v.tensor_copy(identb[:, :], ident[:, C_ID:C_ID + P]).then_inc(s["const_ok"], 1)
                v.tensor_copy(t["sel"][0:3 * ROUTE, :], t["sT"][0:3 * ROUTE, 0:HF]).then_inc(s["const_ok"], 1)
            else:
                v.wait_ge(s["const_in"], 48)
                v.tensor_copy(t["sel"][0:3 * ROUTE, :], t["sT"][0:3 * ROUTE, 0:HF]).then_inc(s["const_ok"], 1)
            route(f)
            with v.Fori(0, NCHUNK) as i:
                steps = HT * NCHUNK * f + i * HT
                for j in range(HT):
                    v.wait_ge(s["silu_ok"], steps + j + 2)
                    v.wait_ge(s["uc_ok"], steps + j + 1)
                    v.wait_ge(s["a_ok"], 1 + steps + max(j - 1, 0))
                    v.tensor_tensor(t["p"][:, j % 2, :], t["s"][:, j % 2, :], ps[:, 2 + j % 2, :],
                                    ALU.mult).then_inc(s["p_ok"], 1)
                    v.wait_ge(s["p_ok"], steps + j + 2)
                    v.wait_ge(s["alo_ok"], 1 + steps + max(j - 1, 0))
                    v.tensor_tensor(t["a"][:, j % 2, :], t["p"][:, j % 2, :], ps[:, 4 + j % 2, :],
                                    ALU.mult).then_inc(s["a_ok"], 1)
                v.wait_ge(s["ystep"], 1 + steps + HT)
                xr = xres[:, bass.ds(i * TPC, TPC), :]
                v.tensor_tensor(xr, xr, ps[:, 6:8, :].rearrange("p b (q d) -> p (b q) d", d=D),
                                ALU.add).then_inc(s["res_ok"], 1)

        def convolve():
            for m in range(FM):
                v.wait_ge(s["pj_ev"], (m + 1) * NCHUNK)
                v.wait_ge(s["cbz"], 1)
                if m > 0:
                    v.wait_ge(s["conv_ok"], m)
                link(v.tensor_scalar(ysum[:, :, :], cb[:, m % 2, :, PAD:PAD + T], cw[:, m, PAD:PAD + 1], None,
                                     ALU.mult))
                for i in range(1, PAD):
                    link(v.scalar_tensor_tensor(out=ysum[:, :, :], in0=cb[:, m % 2, :, i:i + T],
                                                scalar=cw[:, m, i:i + 1], in1=ysum[:, :, :],
                                                op0=ALU.mult, op1=ALU.add))
                if m > 0:
                    v.wait_ge(s["tq_ok"], 4 * m)
                for b in range(B):
                    g, q = divmod(b, NQ)
                    e = v.scalar_tensor_tensor(out=y[:, g, :, q, :],
                                               in0=cb[:, m % 2, b, 0:T].rearrange("p (c t) -> p c t", t=CH),
                                               scalar=cw[:, m, 0:1],
                                               in1=ysum[:, b, :].rearrange("p (c t) -> p c t", t=CH),
                                               op0=ALU.mult, op1=ALU.add)
                e.then_inc(s["conv_ok"], 1)

        def gates():
            m_ = small
            v.wait_ge(s["gt_ev"], NT)
            v.wait_ge(s["tq_ev"], 4 * FM)
            v.tensor_tensor(m_["z"][:, :, :], ab[:, :, 0:H], dtb[:, :].unsqueeze(1).broadcast_to((P, NT, H)),
                            ALU.add).then_inc(s["dch"], 1)
            chain[0] += 1
            link(v.tensor_tensor(sq[:, :, :], qkv[:, :, 0:2 * QK], qkv[:, :, 0:2 * QK], ALU.mult))
            v.scalar_tensor_tensor(out=m_["az"][:, :, :], in0=m_["z"][:, :, :], scalar=-1.0, in1=m_["z"][:, :, :],
                                   op0=ALU.mult, op1=ALU.max).then_inc(s["z_ok"], 1)
            v.tensor_reduce(ss_qk[:, :, :], sq[:, :, :].rearrange("p n (h d) -> p n h d", d=DK), AX_X,
                            ALU.add).then_inc(s["l2_ss"], 1)
            v.wait_ge(s["ez_ok"], 3)
            link(v.tensor_scalar(m_["w"][:, :, :], m_["ez"][:, :, :], 1.0, None, ALU.add))
            v.tensor_scalar(m_["isone"][:, :, :], m_["w"][:, :, :], 1.0, None, ALU.is_equal).then_inc(s["w_ok"], 1)
            v.tensor_scalar(m_["eb"][:, :, :], m_["eb"][:, :, :], 1.0, None, ALU.add).then_inc(s["dch"], 1)
            chain[0] += 1
            v.wait_ge(s["lnw_ok"], 1)
            v.wait_ge(s["w_ok"], 1)
            v.wait_ge(s["dch"], chain[0])
            v.tensor_tensor(m_["lnw"][:, :, :], m_["lnw"][:, :, :], m_["isone"][:, :, :], ALU.add)
            link(v.scalar_tensor_tensor(out=m_["w"][:, :, :], in0=m_["w"][:, :, :], scalar=-1.0,
                                        in1=m_["isone"][:, :, :], op0=ALU.add, op1=ALU.add))
            v.reciprocal(m_["beta"][:, :, :], m_["eb"][:, :, :]).then_inc(s["beta_ok"], 1)
            link(v.reciprocal(m_["w"][:, :, :], m_["w"][:, :, :]))
            link(v.tensor_tensor(m_["lnw"][:, :, :], m_["lnw"][:, :, :], m_["ez"][:, :, :], ALU.mult))
            link(v.tensor_tensor(m_["lnw"][:, :, :], m_["lnw"][:, :, :], m_["w"][:, :, :], ALU.mult))
            link(v.scalar_tensor_tensor(out=m_["sp"][:, :, :], in0=m_["z"][:, :, :], scalar=0.0,
                                        in1=m_["lnw"][:, :, :], op0=ALU.max, op1=ALU.add))
            v.scalar_tensor_tensor(out=m_["g"][:, :, :], in0=m_["sp"][:, :, :], scalar=-1.0,
                                   in1=alog[:, :].unsqueeze(1).broadcast_to((P, NT, H)),
                                   op0=ALU.mult, op1=ALU.mult).then_inc(s["g_ok"], 1)
            v.wait_ge(s["l2_sd"], 2)
            link(v.reciprocal(ss_qk[:, :, :], ss_qk[:, :, :]))
            qk4 = qkv[:, :, 0:2 * QK].rearrange("p n (h d) -> p n h d", d=DK)
            link(v.tensor_tensor(qk4, qk4, ss_qk[:, :, :].unsqueeze(3).broadcast_to((P, NT, 2 * H, DK)), ALU.mult))
            v.transpose(kT[:, :, :], qkv[:, :, QK:2 * QK]).then_inc(s["kT_ok"], 1)
            v.wait_ge(s["kT_ok"], 1)
            v.transpose(kq[:, 1, :, :], qkv[:, :, 0:QK]).then_inc(s["qk_ok"], 1)
            v.wait_ge(s["qk_ok"], 1)
            v.wait_ge(s["kb_ok"], 1)
            v.transpose(kq[:, 0, :, :], kb[:, :, :]).then_inc(s["qT_ok"], 1)
            v.wait_ge(s["qT_ok"], 1)
            v.wait_ge(s["ge_ok"], 1)
            q4 = qkv[:, :, 0:QK].rearrange("p n (h d) -> p n h d", d=DK)
            G4 = ge[:, 0, :].rearrange("p (n h) -> p n h", h=H)
            link(v.tensor_tensor(m_["bG"][:, :, :], m_["beta"][:, :, :], G4, ALU.mult))
            link(v.tensor_tensor(q4, q4, G4.unsqueeze(3).broadcast_to((P, NT, H, DK)), ALU.mult))
            v.transpose(qgT[:, :, :], qkv[:, :, 0:QK]).then_inc(s["scaled_ok"], 1)

        def triangles():
            v.wait_ge(s["mask_ok"], 2)
            for r in range(INST // 8):
                v.wait_ge(s["gm_ok"], r + 1)
                b = ps[:, r % 8, :].rearrange("p (i w t) -> p i w t", i=8, w=2)
                c = slice(8 * r, 8 * r + 8)
                v.tensor_tensor(ltn[:, c, :], ltn[:, c, :], b[:, :, 0, :], ALU.mult)
                v.tensor_tensor(dec[:, c, :], dec[:, c, :], b[:, :, 1, :], ALU.mult).then_inc(s["gm_ev"], 1)
            v.wait_ge(s["u_init"], 2)
            v.wait_ge(s["tri_r"], 16)
            for c in range(CH - 1):
                rows, cols = c + 1, CH - 1 - c
                tmp = tmpU[:, :, 0:rows * cols].rearrange("p h (j i) -> p h j i", j=rows)
                link(v.tensor_tensor(tmp, X[:, :, c:c + 1, c + 1:CH].broadcast_to((P, IH, rows, cols)),
                                     U[:, :, 0:rows, c:c + 1].broadcast_to((P, IH, rows, cols)), ALU.mult))
                dst = U[:, :, 0:rows, c + 1:CH]
                e = v.tensor_tensor(dst, dst, tmp, ALU.add)
                if c < CH - 2:
                    link(e)
            e.then_inc(s["inv_ok"], 1)

        def chunk_steps():
            Rv = R[:, :, :].rearrange("p g (h d) -> p g h d", h=H)
            v.wait_ge(s["kE_ok"], 2)
            for c in range(NC):
                vb = qkv[:, c:NT:NC, 2 * QK:FEAT]
                if c == 0:
                    v.tensor_copy(R[:, :, :], vb).then_inc(s["R_ok"], 1)
                else:
                    v.wait_ge(s["r_ok"], c)
                    bg = small["bG"][:, c:NT:NC, :].unsqueeze(3).broadcast_to((P, NG, H, DV))
                    link(v.tensor_tensor(tmpR[:, :, :].rearrange("p g (h d) -> p g h d", h=H),
                                         ps[:, 0:2, 0:VD].rearrange("p g (h d) -> p g h d", h=H), bg, ALU.mult))
                    v.tensor_tensor(R[:, :, :], vb, tmpR[:, :, :], ALU.subtract).then_inc(s["R_ok"], 1)
                    if c < NC - 1:
                        gt = ge[:, 2, :].rearrange("p (n h) -> p n h", h=H)[:, c:NT:NC, :].unsqueeze(3).broadcast_to(
                            (P, NG, H, DV))
                        link(v.tensor_tensor(tmpS[:, :, :].rearrange("p g (h d) -> p g h d", h=H),
                                             S[:, :, :].rearrange("p g (h d) -> p g h d", h=H), gt, ALU.mult))
                if c < NC - 1:
                    v.wait_ge(s["su_ok"], c + 1)
                    if c == 0:
                        v.tensor_copy(S[:, :, :], ps[:, 6:8, 0:VD]).then_inc(s["S_ok"], 1)
                    else:
                        v.tensor_tensor(S[:, :, :], tmpS[:, :, :], ps[:, 6:8, 0:VD], ALU.add).then_inc(s["S_ok"], 1)
                v.wait_ge(s["o_ev"], c + 1)
                ov = qkv[:, c:NT:NC, 2 * QK:FEAT]
                ov4 = ov.rearrange("p g (h d) -> p g h d", h=H)
                link(v.tensor_tensor(osq[:, :, :], ov, ov, ALU.mult))
                cs = slice(c * NG * H, (c + 1) * NG * H)
                rms = small["orms"][:, :, :].rearrange("p n h -> p (n h)")[:, cs]
                std = small["ostd"][:, :, :].rearrange("p n h -> p (n h)")[:, cs]
                link(v.tensor_reduce(rms, osq[:, :, :].rearrange("p g (h d) -> p (g h) d", h=H), AX_X, ALU.add))
                v.tensor_scalar(rms, rms, 1.0 / DV, EPS, ALU.mult, ALU.add).then_inc(s["ost_ok"], 1)
                v.wait_ge(s["osd_ok"], c + 1)
                link(v.reciprocal(std, std))
                r4 = std.rearrange("p (g h) -> p g h", g=NG).unsqueeze(3).broadcast_to((P, NG, H, DV))
                link(v.tensor_tensor(ov4, ov4, r4, ALU.mult))
                v.tensor_tensor(ov, ov, silug[:, c:NT:NC, :], ALU.mult).then_inc(s["on_ok"], 1)

        def output():
            for i in range(NT + 1):
                if i < NT:
                    v.wait_ge(s["oh_ok"], i + 1)
                    v.tensor_tensor(ol[:, i % 2, :, :].rearrange("p k t -> p (k t)"), ps[:, i % 2, 0:KO * P],
                                    oh[:, i % 2, :, :].rearrange("p k t -> p (k t)").bitcast(F32),
                                    ALU.subtract).then_inc(s["ol_ok"], 1)
                if i >= 1:
                    c, g = divmod(i - 1, NG)
                    n = g * NC + c
                    v.wait_ge(s["wo_ok"], i)
                    v.tensor_tensor(xres[:, n, :], xres[:, n, :], ps[:, 2 + (i - 1) % 2, 0:D],
                                    ALU.add).then_inc(s["wo_ev"], 1)
            v.wait_ge(s["wo_ev"], NT)

        for n in ("p_ok", "a_ok", "res_ok"):
            v.sem_inc(s[n], 1)
        layernorm(0)
        feed_forward(0)
        v.wait_ge(s["res_ok"], 1 + NCHUNK)
        v.wait_ge(s["small_in"], 16 * 11)
        v.wait_ge(s["rattn"], 16 * 13)
        v.tensor_scalar(wo_r[:, :, :], wo_r[:, :, :], nwt[:, 0:1], None, ALU.mult).then_inc(s["wo_sc"], 1)
        layernorm(1)
        convolve()
        gates()
        triangles()
        chunk_steps()
        output()
        layernorm(2)
        feed_forward(1)

    ctx.close()


_INS = ["hidden_states", "Wq", "Wk", "Wv", "Wg", "Wa", "Wb", "Wo", "conv_wq", "conv_wk", "conv_wv",
        "A_log", "dt_bias", "norm_weight"]
_FFN = ["gate_w", "w1", "w2", "w3", "sw1", "sw2", "sw3"]


def kernel(**inputs):
    import numpy as _np
    import concourse.bacc as _bacc
    from concourse import mybir as _mybir
    from concourse.bass_utils import run_bass_kernel_spmd as _run

    nc = _bacc.Bacc("TRN2", target_bir_lowering=False, num_devices=1)
    arrays, args = {}, []
    for name in [f"L0_attn_{n}" for n in _INS] + [f"L0_ffn_{n}" for n in _FFN] + ["constants"]:
        a = constants(_np) if name == "constants" else _np.asarray(inputs[name])
        if name in ("L0_attn_A_log", "L0_attn_dt_bias"):
            a = _np.broadcast_to(a[None, :], (P, H))
        if name == "L0_attn_norm_weight":
            a = a.reshape(DV, 1)
        if name == "L0_ffn_gate_w":
            a = a.T
        a = _np.ascontiguousarray(a)
        arrays[f"in_{name}_dram"] = a
        args.append(nc.dram_tensor(f"in_{name}_dram", a.shape, _mybir.dt.from_np(a.dtype), kind="ExternalInput").ap())
    args.append(nc.dram_tensor("out_0_dram", (B, T, D), _mybir.dt.float32, kind="ExternalOutput").ap())
    macaron(nc, *args)
    r = _run(nc, [arrays], core_ids=[0])
    return r.results[0]["out_0_dram"]
```

```python
from contextlib import ExitStack

import concourse.bass as bass
from concourse import mybir

ALU = mybir.AluOpType
ACT = mybir.ActivationFunctionType
AX_X = mybir.AxisListType.X
F32 = mybir.dt.float32
F32R = mybir.dt.float32r
BF16 = mybir.dt.bfloat16

P = 128
B, T, D = 8, 256, 256
CH = 32
NQ = P // CH
NG = B // NQ
NC = T // CH
NT = NG * NC
KD = D // P
NP = NT // 2
TOK = NT * P
E, HID = 8, 176
HT = (E * HID + HID + P - 1) // P
HF = HT * P
CHUNK = 512
NCHUNK = TOK // CHUNK
TPC = CHUNK // P
H, DK, DV = 6, 32, 64
QK, VD = H * DK, H * DV
FEAT = 2 * QK + VD
FM = FEAT // P
GAB = VD + 2 * H
KO = VD // P
INST = NT * H
IH = INST // 32
TAPS = 4
PAD = TAPS - 1
EARLY = 2
POOL_ROWS = 3
ROUTE = E + 1
EPS = 1e-5

C_ID, C_TRI, C_STR, C_BLK = 0, P, 2 * P, 3 * P
C_INC = 4 * P
C_NST = C_INC + CH
C_TIE = C_NST + CH
C_THR = C_TIE + E * E
C_SEL = C_THR + E
C_ALL = C_SEL + HF


def constants(np):
    c = np.zeros((P, C_ALL), np.float32)
    p = np.arange(P)
    same = p[:, None] // CH == p[None, :] // CH
    c[:, C_ID:C_ID + P] = np.eye(P)
    c[:, C_TRI:C_TRI + P] = same & (p[:, None] <= p[None, :])
    c[:, C_STR:C_STR + P] = same & (p[:, None] > p[None, :])
    c[:, C_BLK:C_BLK + P] = same
    t = np.arange(CH)
    c[:, C_INC:C_INC + CH] = (p % CH)[:, None] <= t[None, :]
    c[:, C_NST:C_NST + CH] = -1.0 * ((p % CH)[:, None] < t[None, :])
    e = np.arange(E)
    c[:, C_TIE:C_TIE + E * E] = (e[None, :] < e[:, None]).reshape(1, E * E)
    c[:, C_THR:C_THR + E] = e + 0.5 - (E - 2)
    j = np.arange(HF)
    for r in range(3 * ROUTE):
        c[r, C_SEL:C_SEL + HF] = (j // HID == r % ROUTE) & (j < (E + 1) * HID)
    return c


def macaron(nc, x, wq, wk, wv, wg, wa, wb, wo, cwq, cwk, cwv, a_log, dt_bias, nw, gate_w,
            w1, w2, w3, sw1, sw2, sw3, consts, out):
    ctx = ExitStack()
    base = (nc.sbuf_base + 63) // 64 * 64
    room = nc.sbuf_usable_end - base

    def at(name, off, shape, dt=F32):
        size = 2 if dt == BF16 else 4
        n = size
        for s in shape[1:]:
            n *= s
        assert off + n <= room, (name, off + n, room)
        return nc.alloc_sbuf_tensor_at(name, shape, dt, offset=base + off)

    def sem(name):
        return ctx.enter_context(nc.semaphore(name))

    KB = 1024
    xres = at("xres", 0, [P, NT, D])
    xhi = at("xhi", 16 * KB, [P, KD, TOK], F32R)
    xlo = at("xlo", 32 * KB, [P, KD, TOK], F32R)
    o = 48 * KB
    ident = at("ident", o, [P, C_SEL])
    o += 4 * C_SEL
    identb = at("identb", o, [P, P], BF16)
    o += 2 * P
    stats = at("stats", o, [P, NT, 6])
    o += 4 * NT * 6
    moments = at("moments", o, [P, NT, 2])
    o += 4 * NT * 2
    vareps = at("vareps", o, [P, NT])
    o += 4 * NT
    stdev = at("stdev", o, [P, NT])
    o += 4 * NT
    rstd = at("rstd", o, [P, NT])
    o += 4 * NT
    XN = o
    xn = at("xn", o, [P, 4, D])
    o += 16 * D
    F = (o + 63) // 64 * 64
    triu = ident[:, C_TRI:C_TRI + P]
    strict = ident[:, C_STR:C_STR + P]
    blocks = ident[:, C_BLK:C_BLK + P]
    incl = ident[:, C_INC:C_INC + CH]
    nstrict = ident[:, C_NST:C_NST + CH]
    tie = ident[:, C_TIE:C_TIE + E * E]
    places = ident[:, C_THR:C_THR + E]

    WB = 4 * KD * HF
    W2B = 4 * HT * D
    assert WB == W2B
    ffn = []
    for f in range(2):
        t = {}
        for n, name in enumerate(["w1h", "w1l", "w3h", "w3l"]):
            t[name] = at(f"{name}_{f}", F + n * WB, [P, KD, HF], F32R)
        for n, name in enumerate(["w2h", "w2l"]):
            t[name] = at(f"{name}_{f}", F + (4 + n) * WB, [P, HT, D], F32R)
        r = F + 6 * WB
        early = r if f == 0 else 16 * KB
        t["r1"] = at(f"r1_{f}", early, [P, KD, HF])
        t["r3"] = at(f"r3_{f}", early + WB, [P, KD, HF])
        t["r2"] = at(f"r2_{f}", r + 2 * WB, [P, HT, D])
        C4 = 4 * CHUNK
        t["s"] = at(f"s_{f}", r, [P, 2, CHUNK])
        t["p"] = at(f"p_{f}", r + 2 * C4, [P, 2, CHUNK])
        t["a"] = at(f"a_{f}", r + 4 * C4, [P, 2, CHUNK])
        t["ahi"] = at(f"ahi_{f}", r + 6 * C4, [P, 3, CHUNK], F32R)
        t["alo"] = at(f"alo_{f}", r + 9 * C4, [P, 3, CHUNK], F32R)
        r += 3 * WB
        t["sel"] = at(f"sel_{f}", r, [P, HF], BF16)
        r += 2 * HF
        t["cT"] = at(f"cT_{f}", r, [P, TOK], BF16)
        r += 2 * TOK
        t["sT"] = at(f"sT_{f}", r, [P, TOK])
        t["gt"] = at(f"gt_{f}", r, [P, NT, E, E])
        r += 4 * TOK
        for name in ["gr", "gh", "gl"]:
            t[name] = at(f"{name}_{f}", r, [P, KD, E], F32 if name == "gr" else F32R)
            r += 4 * KD * E
        for name in ["sc", "rank", "less", "ss"]:
            t[name] = at(f"{name}_{f}", r, [P, NT, E])
            r += 4 * NT * E
        for name in ["cs", "cr"]:
            t[name] = at(f"{name}_{f}", r, [P, NT])
            r += 4 * NT
        t["c9"] = at(f"c9_{f}", r, [P, NT, ROUTE])
        r += 4 * NT * ROUTE
        t["c3"] = at(f"c3_{f}", r, [P, NT, 3 * ROUTE], BF16)
        r += 2 * NT * 3 * ROUTE
        ffn.append(t)
    FEND = (r + 63) // 64 * 64

    wqkv_r = at("wqkv_r", FEND, [P, KD, FEAT])
    wgab_r = at("wgab_r", FEND + 4 * KD * FEAT, [P, KD, GAB])
    o = FEND + 4 * KD * FEAT + 4 * KD * GAB
    wo_r = at("wo_r", o, [P, KO, D])
    AEND = o + 4 * KO * D
    woh = at("woh", F, [P, KO, D], F32R)
    wol = at("wol", F + 4 * KO * D, [P, KO, D], F32R)
    o = F + 8 * KO * D
    silug = at("silug", o, [P, NT, VD])
    o += 4 * NT * VD
    qkv = at("qkv", o, [P, NT, FEAT])
    o += 4 * NT * FEAT
    BR = o
    wqkvh = at("wqkvh", o, [P, KD, FEAT], F32R)
    wqkvl = at("wqkvl", o + 4 * KD * FEAT, [P, KD, FEAT], F32R)
    o += 8 * KD * FEAT
    wgabh = at("wgabh", o, [P, KD, GAB], F32R)
    wgabl = at("wgabl", o + 4 * KD * GAB, [P, KD, GAB], F32R)
    o += 8 * KD * GAB
    cb = at("cb", o, [P, 2, B, PAD + T])
    o += 8 * B * (PAD + T)
    YS = o
    ysum0 = at("ysum0", YS, [P, B, T])
    y = at("y", o + 4 * B * T, [P, NG, NC, NQ, CH])
    o += 8 * B * T
    assert o <= FEND, (o, FEND)
    SL = 4 * INST * CH
    assert 12 * KD * FEAT >= SL and 2 * SL <= 8 * KD * (FEAT + GAB) + 4 * B * (PAD + T)
    dec = at("dec", BR, [P, INST, CH])
    kT = at("kT", BR + SL, [P, NT, QK])
    qgT = at("qgT", BR + 2 * SL, [P, NT, QK])
    kb = at("kb", YS, [P, NT // 2, QK])
    tt = at("tt", BR + 3 * SL, [P, INST, CH])
    assert o >= BR + 4 * SL
    ab = at("ab", o, [P, NT, 2 * H])
    o += 4 * NT * 2 * H
    ss_qk = at("ss_qk", o, [P, NT, 2 * H])
    o += 4 * NT * 2 * H
    small = {}
    for n in ["z", "az", "ez", "w", "lnw", "isone", "sp", "g", "eb", "beta", "bG", "orms", "ostd"]:
        small[n] = at("sm_" + n, o, [P, NT, H])
        o += 4 * NT * H
    ge = at("ge", o, [P, 3, INST])
    o += 12 * INST
    TL = o
    SB = 4 * NG * VD
    dlt, tmpS, tmpR = (at(n, TL + i * SB, [P, NG, VD]) for i, n in enumerate(["dlt", "tmpS", "tmpR"]))
    osq = tmpR
    assert 4 * IH * 256 <= SB
    tmpU = at("tmpU", TL, [P, IH, 256])
    tmpP = at("tmpP", TL + SB, [P, IH, POOL_ROWS * CH])
    oh = at("oh", TL + 3 * SB, [P, NG, KO, P], F32R)
    ol = at("ol", TL + 4 * SB, [P, NG, KO, P], F32R)
    R = at("R", XN, [P, NG, VD])
    rhsd = at("rhsd", TL, [P, INST, CH])
    ltn = at("ltn", TL, [P, INST, CH])
    sqs = [at("sq0", XN, [P, NT // 2, P]), at("sq1", TL + 4 * TOK, [P, NT // 2, P])]
    ysums = [ysum0, at("ysum1", TL, [P, B, T])] * (FM // 2)
    ysums[FM - 1] = at("ysum5", 40 * KB, [P, B, T])
    o = TL + 5 * SB
    assert o >= AEND and o >= TL + SL
    cw = at("cw", o, [P, FM, TAPS])
    o += 4 * FM * TAPS
    alog, dtb = at("alog", o, [P, H]), at("dtb", o + 32, [P, H])
    o += 64
    nwt = at("nwt", o, [P, 1])
    kq = at("kq", 16 * KB, [P, 2, NT, QK])
    X = at("X", 16 * KB, [P, IH, CH, CH])
    U = at("U", 16 * KB + SL, [P, IH, CH, CH])
    S = at("S", 42 * KB, [P, 2, NG, VD])

    ps = ctx.enter_context(nc.psum_tensor("ps", [P, 8, 512], F32))
    tri_out = nc.dram_tensor("tri_out", [NQ, INST, CH, CH], F32, kind="Internal").ap()
    inv_in = nc.dram_tensor("inv_in", [NQ, INST, CH, CH], F32, kind="Internal").ap()

    names = ("x_in0 x_in1 const_in rw1 rw3 rw2 rgate rattn small_in x_out tri_w tri_r inv_w inv_a inv_r "
             "const_ok w1h_ok w3h_ok w2h_ok w1l_ok w3l_ok w2l_ok wgt_hi wgt_lo attn_hi attn_lo wo_sc "
             "st_ok ln_var ln_sd xn_ok tr_ok xhi_ok xlo_ok "
             "sc_ok sig_ok scT_ok c3_ok c3T_ok cT_ok "
             "h_ok uc_ok silu_ok p_ok a_ok ahi_ok alo_ok ystep y_ok res_ok "
             "padz cbz pj_ok pj_ev tap_ok conv_ok sq_ok tq_ok tq_ev dch "
             "l2_ss l2_sd z_ok ez_ok w_ok lnw_ok g_ok cum_ok ge_ok rhsd_ok dec_ok beta_ok kb_ok qk_ok "
             "kT_ok qT_ok mask_ok gm_ok gm_ev gm_n scaled_ok u_init row_ok inv_ok "
             "r_ok R_ok d_ok dlt_ok o_ok o_ev su_ok S_ok ost_ok osd_ok on_ok ot_ok oh_ok ol_ok wo_ok wo_ev kE_ok").split()
    s = {n: sem(n) for n in names}

    def gview(r):
        return r.rearrange("p (c b t) -> p c b t", c=TPC, b=NQ)

    def acc3(pe, dst, lh, ll, rh, rl, start, stop, **kw):
        pe.matmul(dst, ll, rh, start=start, stop=False, **kw)
        pe.matmul(dst, lh, rl, start=False, stop=False, **kw)
        return pe.matmul(dst, lh, rh, start=False, stop=stop, **kw)

    block = ctx.enter_context(nc.Block())

    @block.sync
    def _(sp):
        def load_selector(f):
            sp.dma_start(ffn[f]["sT"][0:3 * ROUTE, 0:HF],
                         consts[0:3 * ROUTE, C_SEL:C_ALL]).then_inc(s["const_in"], 16)

        RT = E * HID

        def load_up(f):
            t = ffn[f]
            for key, w, sw, sm in (("r1", w1, sw1, "rw1"), ("r3", w3, sw3, "rw3")):
                for k in range(KD):
                    sp.dma_start(t[key][:, k, 0:RT].rearrange("p (e h) -> p e h", e=E),
                                 w[:, k * P:(k + 1) * P, :].rearrange("e p h -> p e h")).then_inc(s[sm], 16)
                    sp.dma_start(t[key][:, k, RT:RT + HID], sw[k * P:(k + 1) * P, :]).then_inc(s[sm], 16)

        def load_gate(f):
            for k in range(KD):
                sp.dma_start(ffn[f]["gr"][:, k, :], gate_w[k * P:(k + 1) * P, :]).then_inc(s["rgate"], 16)

        def load_down(f):
            t = ffn[f]
            n = RT // P
            sp.dma_start(t["r2"][:, 0:n, :],
                         w2.rearrange("e h d -> (e h) d").rearrange("(n p) d -> p n d", p=P)).then_inc(s["rw2"], 16)
            sp.dma_start(t["r2"][:, n, :], sw2[0:P, :]).then_inc(s["rw2"], 16)
            sp.wait_ge(s["padz"], 3 * (f + 1))
            sp.dma_start(t["r2"][0:HID - P, n + 1, :], sw2[P:HID, :]).then_inc(s["rw2"], 16)

        sp.dma_start(ident[:, :], consts[:, 0:C_SEL]).then_inc(s["const_in"], 16)
        load_selector(0)
        load_gate(0)
        for b in range(B):
            g, q = divmod(b, NQ)
            sp.dma_start(xres[CH * q:CH * q + CH, g * NC:(g + 1) * NC, :],
                         x[b].rearrange("(c t) d -> t c d", t=CH)).then_inc(s[f"x_in{g}"], 16)
        load_up(0)
        load_down(0)
        for k in range(KD):
            r = slice(k * P, (k + 1) * P)
            sp.dma_start(wqkv_r[:, k, 0:QK], wq[r, :]).then_inc(s["rattn"], 16)
            sp.dma_start(wqkv_r[:, k, QK:2 * QK], wk[r, :]).then_inc(s["rattn"], 16)
            sp.dma_start(wqkv_r[:, k, 2 * QK:FEAT], wv[r, :]).then_inc(s["rattn"], 16)
            sp.dma_start(wgab_r[:, k, 0:VD], wg[r, :]).then_inc(s["rattn"], 16)
            sp.dma_start(wgab_r[:, k, VD:VD + H], wa[r, :]).then_inc(s["rattn"], 16)
            sp.dma_start(wgab_r[:, k, VD + H:GAB], wb[r, :]).then_inc(s["rattn"], 16)
        sp.dma_start(wo_r[:, :, :], wo.rearrange("(k p) d -> p k d", p=P)).then_inc(s["rattn"], 16)
        row = 0
        for w, rows in ((cwq, QK), (cwk, QK), (cwv, VD)):
            done = 0
            while done < rows:
                m, p0 = divmod(row, P)
                n = min(P - p0, rows - done)
                sp.dma_start(cw[p0:p0 + n, m, :], w[done:done + n, :]).then_inc(s["small_in"], 16)
                done += n
                row += n
        sp.dma_start(alog[:, :], a_log).then_inc(s["small_in"], 16)
        sp.dma_start(dtb[:, :], dt_bias).then_inc(s["small_in"], 16)
        for r in range(P // DV):
            sp.dma_start(nwt[r * DV:(r + 1) * DV, :], nw).then_inc(s["small_in"], 16)

        for g in range(NG):
            n = slice(g * INST // NG, (g + 1) * INST // NG)
            sp.wait_ge(s["gm_ev"], (g + 1) * INST // 8 // NG)
            for q in range(NQ):
                sp.dma_start(tri_out[q, n].rearrange("n s t -> s n t"),
                             ltn[CH * q:CH * q + CH, n, :]).then_inc(s["tri_w"], 16)
        sp.wait_ge(s["tri_w"], 16 * NQ * NG)
        sp.dma_start(X[:, :, :, :].rearrange("p h s t -> p (h s t)"),
                     tri_out.rearrange("q (n h) s t -> (q n) (h s t)", h=IH)).then_inc(s["tri_r"], 16)
        sp.wait_ge(s["inv_ok"], 2)
        sp.dma_start(inv_in.rearrange("q (n h) s t -> (q n) (h s t)", h=IH),
                     U[:, :, :, :].rearrange("p h s t -> p (h s t)")).then_inc(s["inv_w"], 16)
        sp.wait_ge(s["inv_w"], 16)
        for sm, c in (("inv_a", slice(0, EARLY)), ("inv_r", slice(EARLY, NC))):
            for g in range(NG):
                n = slice((g * NC + c.start) * H, (g * NC + c.stop) * H)
                for q in range(NQ):
                    sp.dma_start(tt[CH * q:CH * q + CH, n, :],
                                 inv_in[q, n].rearrange("n s t -> s n t")).then_inc(s[sm], 16)

        load_up(1)
        sp.wait_ge(s["o_ok"], NC)
        load_down(1)
        sp.wait_ge(s["wo_ev"], NT)
        load_gate(1)
        load_selector(1)

        for i in range(NCHUNK):
            sp.wait_ge(s["res_ok"], 1 + NCHUNK + i + 1)
            g, half = divmod(i, NCHUNK // NG)
            for q in range(NQ):
                tok = slice(half * TPC * CH, (half + 1) * TPC * CH)
                sp.dma_start(out[g * NQ + q, tok].rearrange("(c t) d -> t c d", t=CH),
                             xres[CH * q:CH * q + CH, i * TPC:(i + 1) * TPC, :]).then_inc(s["x_out"], 16)
        sp.wait_ge(s["x_out"], 16 * NQ * NCHUNK)

    @block.tensor
    def _(pe):
        def layernorm(ph):
            if ph == 0:
                pe.wait_ge(s["const_in"], 16)
            f, route = divmod(ph, 2)

            def scores(i):
                t = ffn[f]
                if i == 0:
                    pe.wait_ge(s["wgt_lo"], f + 1)
                pe.wait_ge(s["xlo_ok"], NP * ph + (i + 1) * TPC // 2)
                for k in range(KD):
                    c = slice(i * CHUNK, (i + 1) * CHUNK)
                    mm = acc3(pe, ps[0:E, 4 + i, :], t["gh"][:, k, :], t["gl"][:, k, :], xhi[:, k, c], xlo[:, k, c],
                              k == 0, k == KD - 1)
                mm.then_inc(s["sc_ok"], 1)

            for n in range(NT):
                m = n // 2
                if route == 0 and n in (6, 10, 14):
                    scores((n - 6) // 4)
                pe.wait_ge(s["xn_ok"], NT * ph + n + 1)
                if n % 2 == 0 and m >= 4:
                    pe.wait_ge(s["xlo_ok"], NP * ph + m - 3)
                for k in range(KD):
                    mm = pe.transpose(ps[:, m % 4, k * 2 * P + (n % 2) * P:k * 2 * P + (n % 2) * P + P],
                                      xn[:, n % 4, k * P:(k + 1) * P], ident[:, C_ID:C_ID + P])
                mm.then_inc(s["tr_ok"], 1)
            if route == 0:
                scores(NCHUNK - 1)

        def route(f):
            t = ffn[f]
            pe.wait_ge(s["sig_ok"], NCHUNK * (f + 1))
            for n in range(NT):
                mm = pe.transpose(ps[:, 0, n * E:(n + 1) * E], t["sT"][0:E, n * P:(n + 1) * P],
                                  ident[0:E, C_ID:C_ID + E])
            mm.then_inc(s["scT_ok"], 1)
            pe.wait_ge(s["c3_ok"], f + 1)
            half = NT // 2
            for n in range(NT):
                v = ps[0:3 * ROUTE, 5 + n // half, :].bitcast(BF16)
                mm = pe.transpose(v[:, (n % half) * P:(n % half + 1) * P], t["c3"][:, n, :], identb[:, :])
            mm.then_inc(s["c3T_ok"], 1)
            pe.wait_ge(s["cT_ok"], 2 * (f + 1))
            for w, n in (("1", KD), ("3", 1), ("2", 1)):
                pe.wait_ge(s[f"w{w}l_ok"], n * (f + 1))

        def feed_forward(f):
            t = ffn[f]
            route(f)
            with pe.Fori(0, NCHUNK) as i:
                c = bass.ds(i * CHUNK, CHUNK)
                steps = HT * NCHUNK * f + i * HT

                def down(j):
                    pe.wait_ge(s["alo_ok"], steps + j + 2)
                    if j == 0:
                        pe.wait_ge(s["res_ok"], 1 + i + NCHUNK * f)
                    for q in range(TPC):
                        dst = ps[:, 6 + q // 2, (q % 2) * D:(q % 2 + 1) * D]
                        tok = slice(q * P, (q + 1) * P)
                        mm = acc3(pe, dst, t["ahi"][:, j % 3, tok], t["alo"][:, j % 3, tok],
                                  t["w2h"][:, j, :], t["w2l"][:, j, :],
                                  j == 0 and q % 2 == 0, j == HT - 1, skip_group_check=True)
                    mm.then_inc(s["ystep"], 1)

                for j in range(HT):
                    hid = slice(j * P, (j + 1) * P)
                    pe.wait_ge(s["silu_ok"], 1 + steps + max(j - 1, 0))
                    for k in range(KD):
                        mm = acc3(pe, ps[:, j % 2, :], t["w1h"][:, k, hid], t["w1l"][:, k, hid],
                                  xhi[:, k, c], xlo[:, k, c], k == 0, k == KD - 1)
                    mm.then_inc(s["h_ok"], 1)
                    pe.wait_ge(s["a_ok"], 1 + steps + max(j - 1, 0))
                    for k in range(KD):
                        acc3(pe, ps[:, 2 + j % 2, :], t["w3h"][:, k, hid], t["w3l"][:, k, hid],
                             xhi[:, k, c], xlo[:, k, c], k == 0, k == KD - 1)
                    pe.matmul(ps[:, 4 + j % 2, :], t["sel"][0:3 * ROUTE, hid], t["cT"][0:3 * ROUTE, c],
                              start=True, stop=True).then_inc(s["uc_ok"], 1)
                    if j >= 2:
                        down(j - 2)
                down(HT - 2)
                down(HT - 1)

        def project():
            pe.wait_ge(s["xlo_ok"], 2 * NP)
            pe.wait_ge(s["attn_lo"], 2)

            job = [0]

            def bank():
                n = job[0]
                job[0] += 1
                if n >= 4:
                    pe.wait_ge(s["pj_ev"], n - 3)
                return n % 4

            def features(m):
                for ch in range(NCHUNK):
                    n = bank()
                    c = slice(ch * CHUNK, (ch + 1) * CHUNK)
                    f = slice(m * P, (m + 1) * P)
                    for k in range(KD):
                        mm = acc3(pe, ps[:, n, :], wqkvh[:, k, f], wqkvl[:, k, f], xhi[:, k, c], xlo[:, k, c],
                                  k == 0, k == KD - 1)
                    mm.then_inc(s["pj_ok"], 1)

            def gate_tiles(r):
                for i in range(4 * r, 4 * r + 4):
                    n = bank()
                    c = slice(i * P, (i + 1) * P)
                    for k in range(KD):
                        mm = acc3(pe, ps[:, n, 0:GAB], xhi[:, k, c], xlo[:, k, c], wgabh[:, k, :], wgabl[:, k, :],
                                  k == 0, k == KD - 1)
                    mm.then_inc(s["pj_ok"], 1)

            def turn(m):
                pe.wait_ge(s["conv_ok"], m + 1)
                for r in range(4):
                    if m > 0:
                        pe.wait_ge(s["tq_ev"], 4 * (m - 1) + r + 1)
                    for i in range(4):
                        g, c = divmod(4 * r + i, NC)
                        mm = pe.transpose(ps[:, 4 + r, i * P:(i + 1) * P],
                                          y[:, g, c, :, :].rearrange("p b t -> p (b t)"),
                                          ident[:, C_ID:C_ID + P])
                    mm.then_inc(s["tq_ok"], 1)

            features(0)
            features(1)
            gate_tiles(0)
            for m in range(FM - 2):
                turn(m)
                features(m + 2)
                if m < 3:
                    gate_tiles(m + 1)
            decays()
            turn(FM - 2)
            grams(turn)

        def decays():
            pe.wait_ge(s["pj_ev"], FM * NCHUNK + NT)
            pe.wait_ge(s["g_ok"], 1)
            gall = small["g"][:, :, :].rearrange("p n h -> p (n h)")
            for r, m in enumerate((triu, strict, blocks)):
                mm = pe.matmul(ps[:, 0, r * INST:(r + 1) * INST], m, gall, start=True, stop=True)
            mm.then_inc(s["cum_ok"], 1)
            pe.wait_ge(s["rhsd_ok"], 1)
            per = 512 // CH
            for r in range(INST // per):
                if r == 3:
                    pe.wait_ge(s["ge_ok"], 1)
                if r > 3:
                    pe.wait_ge(s["dec_ok"], r - 3)
                pe.matmul(ps[:, (1 + r) % 4, :], strict, rhsd[:, r * per:(r + 1) * per, :], start=True,
                          stop=True).then_inc(s["cum_ok"], 1)

        def grams(turn):
            pe.wait_ge(s["kT_ok"], 1)
            pe.wait_ge(s["qk_ok"], 1)
            pe.wait_ge(s["dec_ok"], INST * CH // 512)
            pe.wait_ge(s["ge_ok"], 1)
            for i in range(INST):
                n, h = divmod(i, H)
                bank = (i // 8) % 4
                if i % (INST // 2) == 0:
                    pe.wait_ge(s["qT_ok"], 1 + i // (INST // 2))
                if i == 3 * 8:
                    turn(FM - 1)
                if i % 8 == 0 and i >= 4 * 8:
                    pe.wait_ge(s["gm_ev"], i // 8 - 3)
                f = slice(h * DK, (h + 1) * DK)
                for q in range(NQ):
                    r = slice(CH * q, CH * q + CH)
                    mm = pe.matmul(ps[r, bank, (i % 8) * 2 * CH:(i % 8 + 1) * 2 * CH], kT[r, n, f], kq[r, :, n, f],
                                   start=True, stop=True)
                if i % 8 == 7:
                    mm.then_inc(s["gm_ok"], 1)

        def chunk_steps():
            pe.wait_ge(s["inv_a"], 16 * NQ * NG)
            pe.wait_ge(s["gm_ev"], INST // 8)
            pe.wait_ge(s["tq_ev"], 4 * FM)
            pe.wait_ge(s["scaled_ok"], 1)
            pe.wait_ge(s["kE_ok"], 2)
            pe.wait_ge(s["wo_sc"], 3)

            def each(groups=range(NG)):
                for g in groups:
                    for h in range(H):
                        for q in range(NQ):
                            yield g, h, slice(CH * q, CH * q + CH), slice(h * DV, (h + 1) * DV)

            def predict(c):
                pe.wait_ge(s["S_ok"], c)
                for g, h, r, v in each():
                    mm = pe.matmul(ps[r, g, v], kT[r, g * NC + c, h * DK:(h + 1) * DK], S[r, c % 2, g, v],
                                   start=True, stop=True)
                mm.then_inc(s["r_ok"], 1)

            def within(c):
                for g, h, r, v in each():
                    mm = pe.matmul(ps[r, 4 + g, v], dec[r, (g * NC + c) * H + h, :], dlt[r, g, v],
                                   start=(c == 0 and h == 0), stop=True, skip_group_check=True)
                mm.then_inc(s["o_ok"], 1)

            def turn(c):
                pe.wait_ge(s["on_ok"], c + 1)
                for g in range(NG):
                    if c > 0:
                        pe.wait_ge(s["wo_ev"], NG * (c - 1) + g + 1)
                    for k in range(KO):
                        mm = pe.transpose(ps[:, 6 + g, k * P:(k + 1) * P],
                                          qkv[:, g * NC + c, 2 * QK + k * P:2 * QK + (k + 1) * P],
                                          ident[:, C_ID:C_ID + P])
                    mm.then_inc(s["ot_ok"], 1)

            def deltas(c):
                pe.wait_ge(s["R_ok"], c + 1)
                if c == EARLY:
                    pe.wait_ge(s["inv_r"], 16 * NQ * NG)
                for g, h, r, v in each():
                    mm = pe.matmul(ps[r, 2 + g, v], tt[r, (g * NC + c) * H + h, :], R[r, g, v],
                                   start=True, stop=True)
                mm.then_inc(s["d_ok"], 1)

            def across(c, g):
                pe.wait_ge(s["o_ev"], c)
                for g, h, r, v in each([g]):
                    pe.matmul(ps[r, 4 + g, v], qgT[r, g * NC + c, h * DK:(h + 1) * DK], S[r, c % 2, g, v],
                              start=(h == 0), stop=False, skip_group_check=True)

            def update(c):
                for g, h, r, v in each():
                    mm = pe.matmul(ps[r, g, v], qkv[r, g * NC + c, QK + h * DK:QK + (h + 1) * DK],
                                   dlt[r, g, v], start=True, stop=True)
                mm.then_inc(s["su_ok"], 1)

            def project_out(c):
                for g in range(NG):
                    pe.wait_ge(s["ol_ok"], NG * c + g + 1)
                    for k in range(KO):
                        mm = acc3(pe, ps[:, 6 + g, 0:D], oh[:, g, k, :], ol[:, g, k, :],
                                  woh[:, k, :], wol[:, k, :], k == 0, k == KO - 1)
                    mm.then_inc(s["wo_ok"], 1)

            for c in range(NC + 2):
                if 0 < c < NC:
                    predict(c)
                if 0 < c <= NC:
                    within(c - 1)
                if c >= 2:
                    turn(c - 2)
                if c < NC:
                    deltas(c)
                    if c > 0:
                        across(c, 0)
                    pe.wait_ge(s["dlt_ok"], c + 1)
                if c < NC - 1:
                    update(c)
                if c >= 2:
                    project_out(c - 2)
                if 0 < c < NC:
                    across(c, 1)

        pe.sem_inc(s["ystep"], 1)
        layernorm(0)
        feed_forward(0)
        layernorm(1)
        project()
        chunk_steps()
        layernorm(2)
        feed_forward(1)

    @block.scalar
    def _(act):
        def layernorm(ph):
            act.wait_ge(s["ln_var"], ph + 1)
            act.activation(stdev[:, :], vareps[:, :], ACT.Sqrt).then_inc(s["ln_sd"], 1)
            if ph == 2:
                high_part(1, "2")
                act.wait_ge(s["w1l_ok"], 2 * KD)
                act.wait_ge(s["w3l_ok"], 2)
            for m in range(NP):
                if ph == 0 and m in (NP - 3, NP - 2):
                    high_part(0, "1", m - (NP - 3))
                act.wait_ge(s["tr_ok"], NT * ph + 2 * m + 2)
                act.copy(xhi[:, :, m * 2 * P:(m + 1) * 2 * P],
                         ps[:, m % 4, :].rearrange("p (k t) -> p k t", k=KD)).then_inc(s["xhi_ok"], 1)
                if ph != 1 and m in (3, 5, 7):
                    sigmoid(ph // 2, (m - 3) // 2)
            if ph != 1:
                sigmoid(ph // 2, NCHUNK - 1)

        def sigmoid(f, i):
            act.wait_ge(s["sc_ok"], NCHUNK * f + i + 1)
            if i == 0:
                act.wait_ge(s["const_ok"], 2 + f)
            act.activation(ffn[f]["sT"][0:E, i * CHUNK:(i + 1) * CHUNK], ps[0:E, 4 + i, :],
                           ACT.Sigmoid).then_inc(s["sig_ok"], 1)

        def high_part(f, w, k=None):
            t = ffn[f]
            if f == 1:
                act.wait_ge(s["wo_ev"], NT)
            act.wait_ge(s["padz"], 3 * (f + 1))
            act.wait_ge(s["rw" + w], (48 if w == "2" else 64) * (f + 1))
            part = slice(None) if k is None else slice(k, k + 1)
            act.copy(t[f"w{w}h"][:, part, :], t["r" + w][:, part, :]).then_inc(s[f"w{w}h_ok"], 1)

        def high_gate(f):
            t = ffn[f]
            act.wait_ge(s["rgate"], 32 * (f + 1))
            act.copy(t["gh"][:, :, :], t["gr"][:, :, :]).then_inc(s["wgt_hi"], 1)

        def feed_forward(f):
            t = ffn[f]
            if f == 0:
                high_part(0, "3")
                high_part(0, "2")
            act.wait_ge(s["cT_ok"], 2 * (f + 1))
            with act.Fori(0, NCHUNK) as i:
                steps = HT * NCHUNK * f + i * HT

                def high(j):
                    act.wait_ge(s["a_ok"], steps + j + 2)
                    act.wait_ge(s["ystep"], 1 + steps + max(j - 2, 0))
                    act.copy(t["ahi"][:, j % 3, :], t["a"][:, j % 2, :]).then_inc(s["ahi_ok"], 1)

                for j in range(HT):
                    act.wait_ge(s["h_ok"], steps + j + 1)
                    act.wait_ge(s["p_ok"], 1 + steps + max(j - 1, 0))
                    act.activation(t["s"][:, j % 2, :], ps[:, j % 2, :], ACT.Silu).then_inc(s["silu_ok"], 1)
                    if j >= 1:
                        high(j - 1)
                high(HT - 1)

        def project():
            act.wait_ge(s["rattn"], 16 * 13)
            act.wait_ge(s["res_ok"], 1 + NCHUNK)
            act.copy(wqkvh[:, :, :], wqkv_r[:, :, :]).then_inc(s["attn_hi"], 1)
            act.copy(wgabh[:, :, :], wgab_r[:, :, :]).then_inc(s["attn_hi"], 1)
            act.wait_ge(s["wo_sc"], 1)
            act.copy(woh[:, :, :], wo_r[:, :, :]).then_inc(s["wo_sc"], 1)

        def convolve():
            act.wait_ge(s["small_in"], 16 * 11)
            act.wait_ge(s["cbz"], 1)

            def silu_turned(m):
                for r in range(4):
                    act.wait_ge(s["tq_ok"], 4 * m + r + 1)
                    act.activation(qkv[:, 4 * r:4 * r + 4, m * P:(m + 1) * P],
                                   ps[:, 4 + r, :].rearrange("p (n f) -> p n f", n=4),
                                   ACT.Silu).then_inc(s["tq_ev"], 1)

            job = [0]

            def features(m):
                for ch in range(NCHUNK):
                    n = job[0]
                    job[0] += 1
                    g, half = divmod(ch, 2)
                    act.wait_ge(s["pj_ok"], n + 1)
                    if m >= 2:
                        act.wait_ge(s["conv_ok"], m - 1)
                    t0 = PAD + half * TPC * CH
                    act.copy(cb[:, m % 2, g * NQ:(g + 1) * NQ, t0:t0 + TPC * CH].rearrange(
                        "p b (c t) -> p c b t", c=TPC), gview(ps[:, n % 4, :])).then_inc(s["pj_ev"], 1)
                if m == 1:
                    act.wait_ge(s["attn_lo"], 2)
                    act.wait_ge(s["wo_sc"], 3)
                act.wait_ge(s["pj_ev"], job[0])
                act.activation(ysums[m][:, :, :], cb[:, m % 2, :, PAD:PAD + T], ACT.Copy,
                               scale=cw[:, m, PAD:PAD + 1]).then_inc(s["tap_ok"], 1)

            def gate_tiles(r):
                for i in range(4 * r, 4 * r + 4):
                    n = job[0]
                    job[0] += 1
                    act.wait_ge(s["pj_ok"], n + 1)
                    act.activation(silug[:, i, :], ps[:, n % 4, 0:VD], ACT.Silu)
                    act.copy(ab[:, i, :], ps[:, n % 4, VD:GAB]).then_inc(s["pj_ev"], 1)

            def squares(m):
                for r in range(2):
                    n = 2 * m + r
                    act.wait_ge(s["tq_ev"], 4 * m + 2 * r + 2)
                    if n >= 2:
                        act.wait_ge(s["l2_ss"], n - 1)
                    act.activation(sqs[r][:, :, :], qkv[:, r * NT // 2:(r + 1) * NT // 2, m * P:(m + 1) * P],
                                   ACT.Square).then_inc(s["sq_ok"], 1)

            def decay_and_beta():
                act.wait_ge(s["z_ok"], 1)
                act.activation(small["ez"][:, :, :], small["az"][:, :, :], ACT.Exp, scale=-1.0).then_inc(s["ez_ok"], 1)
                act.activation(small["eb"][:, :, :], ab[:, :, H:2 * H], ACT.Exp, scale=-1.0).then_inc(s["ez_ok"], 1)
                act.activation(alog[:, :], alog[:, :], ACT.Exp).then_inc(s["ez_ok"], 1)
                act.wait_ge(s["w_ok"], 1)
                act.activation(small["lnw"][:, :, :], small["w"][:, :, :], ACT.Ln).then_inc(s["lnw_ok"], 1)
                act.wait_ge(s["l2_ss"], 6)
                act.activation(ss_qk[:, :, 0:H], ss_qk[:, :, 0:H], ACT.Sqrt, scale=float(DK)).then_inc(s["l2_sd"], 1)
                act.activation(ss_qk[:, :, H:2 * H], ss_qk[:, :, H:2 * H], ACT.Sqrt).then_inc(s["l2_sd"], 1)

            features(0)
            features(1)
            gate_tiles(0)
            for m in range(3):
                silu_turned(m)
                features(m + 2)
                gate_tiles(m + 1)
                squares(m)
            decay_and_beta()
            silu_turned(3)
            features(5)
            act.wait_ge(s["cum_ok"], 1)
            act.activation(ge[:, :, :].rearrange("p r i -> p (r i)"), ps[:, 0, 0:3 * INST],
                           ACT.Exp).then_inc(s["ge_ok"], 1)
            per = 512 // CH
            for r in range(INST // per):
                act.wait_ge(s["cum_ok"], r + 2)
                act.activation(dec[:, r * per:(r + 1) * per, :].rearrange("p i t -> p (i t)"), ps[:, (1 + r) % 4, :],
                               ACT.Exp).then_inc(s["dec_ok"], 1)
            silu_turned(FM - 2)
            silu_turned(FM - 1)

        def chunk_steps():
            flat = "p n h -> p (n h)"

            def outputs(c):
                act.wait_ge(s["o_ok"], c + 1)
                act.wait_ge(s["R_ok"], c + 1)
                for g in range(NG):
                    e = act.copy(qkv[:, g * NC + c, 2 * QK:FEAT], ps[:, 4 + g, 0:VD])
                e.then_inc(s["o_ev"], 1)

            def high(c):
                for g in range(NG):
                    act.wait_ge(s["ot_ok"], NG * c + g + 1)
                    if c > 0:
                        act.wait_ge(s["wo_ok"], NG * (c - 1) + g + 1)
                    act.copy(oh[:, g, :, :].rearrange("p k t -> p (k t)"),
                             ps[:, 6 + g, 0:KO * P]).then_inc(s["oh_ok"], 1)

            def deltas(c):
                act.wait_ge(s["d_ok"], c + 1)
                act.copy(dlt[:, :, :], ps[:, 2:4, 0:VD]).then_inc(s["dlt_ok"], 1)

            def deviation(c):
                cs = slice(c * NG * H, (c + 1) * NG * H)
                act.wait_ge(s["ost_ok"], c + 1)
                act.activation(small["ostd"][:, :, :].rearrange(flat)[:, cs],
                               small["orms"][:, :, :].rearrange(flat)[:, cs], ACT.Sqrt).then_inc(s["osd_ok"], 1)

            for c in range(NC + 2):
                if 0 < c <= NC:
                    outputs(c - 1)
                if c >= 2:
                    high(c - 2)
                if c < NC:
                    deltas(c)
                if 0 < c <= NC:
                    deviation(c - 1)

        act.sem_inc(s["silu_ok"], 1)
        high_gate(0)
        layernorm(0)
        feed_forward(0)
        project()
        layernorm(1)
        convolve()
        chunk_steps()
        for k in range(KD):
            high_part(1, "1", k)
        high_part(1, "3")
        high_gate(1)
        layernorm(2)
        feed_forward(1)

    @block.gpsimd
    def _(pool):
        def split_weights(f):
            t = ffn[f]
            RT = (E + 1) * HID
            for raw in ("r1", "r3"):
                pool.memset(t[raw][:, :, RT:HF], 0.0).then_inc(s["padz"], 1)
            if f == 1:
                pool.wait_ge(s["o_ok"], NC)
            pool.memset(t["r2"][:, HT - 1, :], 0.0).then_inc(s["padz"], 1)

            def low(w, k=None):
                pool.wait_ge(s[f"w{w}h_ok"], f + 1 if k is None else KD * f + k + 1)
                part = slice(None) if k is None else slice(k, k + 1)
                pool.tensor_tensor(t[f"w{w}l"][:, part, :], t["r" + w][:, part, :],
                                   t[f"w{w}h"][:, part, :].bitcast(F32), ALU.subtract).then_inc(s[f"w{w}l_ok"], 1)

            def low_gate():
                pool.wait_ge(s["wgt_hi"], f + 1)
                pool.tensor_tensor(t["gl"][:, :, :], t["gr"][:, :, :], t["gh"][:, :, :].bitcast(F32),
                                   ALU.subtract).then_inc(s["wgt_lo"], 1)

            if f == 0:
                low_gate()
                low("1", 0)
            low("1", 1)
            if f == 1:
                low_gate()
            low("2")

        def feed_forward(f):
            t = ffn[f]
            pool.wait_ge(s["cT_ok"], 2 * (f + 1))
            with pool.Fori(0, NCHUNK) as i:
                steps = HT * NCHUNK * f + i * HT
                for j in range(HT):
                    pool.wait_ge(s["ahi_ok"], steps + j + 1)
                    pool.tensor_tensor(t["alo"][:, j % 3, :], t["a"][:, j % 2, :],
                                       t["ahi"][:, j % 3, :].bitcast(F32), ALU.subtract).then_inc(s["alo_ok"], 1)

        def attention():
            pool.wait_ge(s["res_ok"], 1 + NCHUNK)
            pool.memset(cb[:, :, :, 0:PAD], 0.0).then_inc(s["cbz"], 1)
            pool.wait_ge(s["attn_hi"], 2)
            pool.tensor_tensor(wqkvl[:, :, :], wqkv_r[:, :, :], wqkvh[:, :, :].bitcast(F32),
                               ALU.subtract).then_inc(s["attn_lo"], 1)
            pool.tensor_tensor(wgabl[:, :, :], wgab_r[:, :, :], wgabh[:, :, :].bitcast(F32),
                               ALU.subtract).then_inc(s["attn_lo"], 1)
            pool.wait_ge(s["wo_sc"], 2)
            pool.tensor_tensor(wol[:, :, :], wo_r[:, :, :], woh[:, :, :].bitcast(F32),
                               ALU.subtract).then_inc(s["wo_sc"], 1)
            pool.wait_ge(s["g_ok"], 1)
            pool.wait_ge(s["conv_ok"], 4)
            pool.wait_ge(s["l2_ss"], 6)
            gall = small["g"][:, :, :].rearrange("p n h -> p (n h)")
            pool.tensor_tensor(rhsd[:, :, :], gall.unsqueeze(2).broadcast_to((P, INST, CH)),
                               incl.unsqueeze(1).broadcast_to((P, INST, CH)), ALU.mult).then_inc(s["rhsd_ok"], 1)
            pool.wait_ge(s["cum_ok"], 1 + INST * CH // 512)
            pool.wait_ge(s["dec_ok"], INST * CH // 512)
            pool.tensor_tensor(ltn[:, :, :], dec[:, :, :], nstrict.unsqueeze(1).broadcast_to((P, INST, CH)),
                               ALU.mult).then_inc(s["mask_ok"], 1)
            pool.wait_ge(s["mask_ok"], 1)
            pool.tensor_tensor(dec[:, :, :], dec[:, :, :], incl.unsqueeze(1).broadcast_to((P, INST, CH)),
                               ALU.mult).then_inc(s["mask_ok"], 1)
            pool.wait_ge(s["kT_ok"], 1)
            pool.wait_ge(s["kb_ok"], 2)
            pool.wait_ge(s["ge_ok"], 1)
            kv = qkv[:, :, QK:2 * QK].rearrange("p n (h d) -> p n h d", h=H)
            pool.tensor_tensor(kv, kv, ge[:, 1, :].rearrange("p (n h) -> p n h", h=H).unsqueeze(3).broadcast_to(
                (P, NT, H, DK)), ALU.mult).then_inc(s["kE_ok"], 1)
            pool.wait_ge(s["gm_ok"], INST // 8)
            pool.memset(U[:, :, :, :], 0.0).then_inc(s["u_init"], 1)
            pool.wait_ge(s["u_init"], 1)
            pool.memset(U[:, :, :, :].rearrange("p h s t -> p h (s t)")[:, :, 0:CH * CH:CH + 1],
                        1.0).then_inc(s["u_init"], 1)
            pool.wait_ge(s["tq_ev"], 4 * FM)
            vv = qkv[:, :, 2 * QK:FEAT].rearrange("p n (h d) -> p n h d", h=H)
            pool.tensor_tensor(vv, vv, small["beta"][:, :, :].unsqueeze(3).broadcast_to((P, NT, H, DV)),
                               ALU.mult).then_inc(s["kE_ok"], 1)

        def first_rows():
            pool.wait_ge(s["u_init"], 2)
            pool.wait_ge(s["tri_r"], 16)
            done = 0
            for c in range(CH - 1):
                rows, cols = min(c + 1, POOL_ROWS), CH - 1 - c
                tmp = tmpP[:, :, 0:rows * cols].rearrange("p h (j i) -> p h j i", j=rows)
                pool.tensor_tensor(tmp, X[:, :, c:c + 1, c + 1:CH].broadcast_to((P, IH, rows, cols)),
                                   U[:, :, 0:rows, c:c + 1].broadcast_to((P, IH, rows, cols)),
                                   ALU.mult).then_inc(s["row_ok"], 1)
                done += 1
                pool.wait_ge(s["row_ok"], done)
                dst = U[:, :, 0:rows, c + 1:CH]
                e = pool.tensor_tensor(dst, dst, tmp, ALU.add)
                if c < CH - 2:
                    e.then_inc(s["row_ok"], 1)
                    done += 1
                    pool.wait_ge(s["row_ok"], done)
            e.then_inc(s["inv_ok"], 1)

        pool.sem_inc(s["alo_ok"], 1)
        split_weights(0)
        feed_forward(0)
        attention()
        first_rows()
        pool.wait_ge(s["inv_w"], 16)
        split_weights(1)
        feed_forward(1)

    @block.vector
    def _(v):
        chain = [0]

        def link(ins):
            chain[0] += 1
            ins.then_inc(s["dch"], 1)
            v.wait_ge(s["dch"], chain[0])

        def layernorm(ph):
            if ph == 0:
                for n in range(NT):
                    if n % NC == 0:
                        v.wait_ge(s[f"x_in{n // NC}"], 16 * NQ)
                    e = v.bn_stats(stats[:, n, :], xres[:, n, :])
                e.then_inc(s["st_ok"], 1)
            v.wait_ge(s["st_ok"], (1, 1 + NCHUNK, 1 + NCHUNK + NC)[ph])
            for n in range(NT):
                e = v.bn_aggr(moments[:, n, :], stats[:, n, :])
            link(e)
            v.tensor_scalar(vareps[:, :], moments[:, :, 1], EPS, None, ALU.add).then_inc(s["ln_var"], 1)
            if ph == 2:
                low_part(1)
                selector(1)
                v.wait_ge(s["w1l_ok"], 2 * KD)
            v.wait_ge(s["ln_sd"], ph + 1)
            link(v.reciprocal(rstd[:, :], stdev[:, :]))

            def normal(n):
                if n >= 4:
                    v.wait_ge(s["tr_ok"], NT * ph + n - 3)
                v.tensor_scalar(xn[:, n % 4, :], xres[:, n, :], moments[:, n, 0:1], rstd[:, n:n + 1],
                                ALU.subtract, ALU.mult).then_inc(s["xn_ok"], 1)

            for n in range(4):
                normal(n)
            for m in range(NP):
                v.wait_ge(s["xhi_ok"], NP * ph + m + 1)
                c = slice(m * 2 * P, (m + 1) * 2 * P)
                v.tensor_tensor(xlo[:, :, c], ps[:, m % 4, :].rearrange("p (k t) -> p k t", k=KD),
                                xhi[:, :, c].bitcast(F32), ALU.subtract).then_inc(s["xlo_ok"], 1)
                for n in (2 * m + 4, 2 * m + 5):
                    if n < NT:
                        normal(n)

        def selector(f):
            v.wait_ge(s["const_in"], 32 + 16 * f)
            if f == 0:
                v.tensor_copy(identb[:, :], ident[:, C_ID:C_ID + P]).then_inc(s["const_ok"], 1)
            v.tensor_copy(ffn[f]["sel"][0:3 * ROUTE, :],
                          ffn[f]["sT"][0:3 * ROUTE, 0:HF]).then_inc(s["const_ok"], 1)

        def low_part(f):
            t = ffn[f]
            if f == 1:
                v.wait_ge(s["w1h_ok"], KD + 1)
                v.tensor_tensor(t["w1l"][:, 0, :], t["r1"][:, 0, :], t["w1h"][:, 0, :].bitcast(F32),
                                ALU.subtract).then_inc(s["w1l_ok"], 1)
            v.wait_ge(s["w3h_ok"], f + 1)
            v.tensor_tensor(t["w3l"][:, :, :], t["r3"][:, :, :], t["w3h"][:, :, :].bitcast(F32),
                            ALU.subtract).then_inc(s["w3l_ok"], 1)

        def route(f):
            t = ffn[f]
            v.wait_ge(s["scT_ok"], f + 1)
            link(v.tensor_copy(t["sc"][:, :, :], ps[:, 0, 0:NT * E].rearrange("p (n e) -> p n e", e=E)))
            over = t["sc"][:, :, :].unsqueeze(2).broadcast_to((P, NT, E, E))
            mine = t["sc"][:, :, :].unsqueeze(3).broadcast_to((P, NT, E, E))
            link(v.tensor_tensor(t["gt"][:, :, :, :], over, mine, ALU.is_ge))
            gtf = t["gt"][:, :, :, :].rearrange("p n a b -> p n (a b)")
            link(v.tensor_tensor(gtf, gtf, tie.unsqueeze(1).broadcast_to((P, NT, E * E)), ALU.mult))
            v.tensor_reduce(t["rank"][:, :, :], t["gt"][:, :, :, :], AX_X, ALU.add)
            link(v.tensor_reduce(t["less"][:, :, :], t["gt"][:, :, :, :].rearrange("p n a b -> p n b a"), AX_X,
                                 ALU.add))
            link(v.tensor_tensor(t["rank"][:, :, :], t["rank"][:, :, :], t["less"][:, :, :], ALU.subtract))
            link(v.tensor_tensor(t["rank"][:, :, :], t["rank"][:, :, :],
                                 places.unsqueeze(1).broadcast_to((P, NT, E)), ALU.is_lt))
            link(v.tensor_tensor(t["ss"][:, :, :], t["rank"][:, :, :], t["sc"][:, :, :], ALU.mult))
            link(v.tensor_reduce(t["cs"][:, :], t["ss"][:, :, :], AX_X, ALU.add))
            link(v.tensor_scalar(t["cs"][:, :], t["cs"][:, :], 1e-20, None, ALU.add))
            link(v.reciprocal(t["cr"][:, :], t["cs"][:, :]))
            v.memset(t["c9"][:, :, E:ROUTE], 0.5)
            link(v.scalar_tensor_tensor(out=t["c9"][:, :, 0:E], in0=t["ss"][:, :, :], scalar=2.5 * 0.5,
                                        in1=t["cr"][:, :].unsqueeze(2).broadcast_to((P, NT, E)),
                                        op0=ALU.mult, op1=ALU.mult))
            for r in range(3):
                part = t["c3"][:, :, r * ROUTE:(r + 1) * ROUTE]
                e = v.tensor_copy(part, t["c9"][:, :, :])
                if r < 2:
                    link(e)
                    link(v.tensor_tensor(t["c9"][:, :, :], t["c9"][:, :, :], part, ALU.subtract))
            e.then_inc(s["c3_ok"], 1)
            if f == 0:
                low_part(0)
            v.wait_ge(s["c3T_ok"], f + 1)
            for r in range(2):
                v.tensor_copy(t["cT"][0:3 * ROUTE, r * TOK // 2:(r + 1) * TOK // 2],
                              ps[0:3 * ROUTE, 5 + r, :].bitcast(BF16)).then_inc(s["cT_ok"], 1)

        def feed_forward(f):
            t = ffn[f]
            route(f)
            with v.Fori(0, NCHUNK) as i:
                steps = HT * NCHUNK * f + i * HT
                for j in range(HT):
                    v.wait_ge(s["silu_ok"], steps + j + 2)
                    v.wait_ge(s["uc_ok"], steps + j + 1)
                    v.wait_ge(s["a_ok"], 1 + steps + max(j - 1, 0))
                    v.tensor_tensor(t["p"][:, j % 2, :], t["s"][:, j % 2, :], ps[:, 2 + j % 2, :],
                                    ALU.mult).then_inc(s["p_ok"], 1)
                    v.wait_ge(s["p_ok"], steps + j + 2)
                    v.wait_ge(s["alo_ok"], 1 + steps + max(j - 1, 0))
                    v.tensor_tensor(t["a"][:, j % 2, :], t["p"][:, j % 2, :], ps[:, 4 + j % 2, :],
                                    ALU.mult).then_inc(s["a_ok"], 1)
                v.wait_ge(s["ystep"], 1 + steps + HT)
                xr = xres[:, bass.ds(i * TPC, TPC), :]
                v.tensor_tensor(xr, xr, ps[:, 6:8, :].rearrange("p b (q d) -> p (b q) d", d=D),
                                ALU.add).then_inc(s["res_ok"], 1)
                if f == 0:
                    v.wait_ge(s["res_ok"], i + 2)
                    for q in range(TPC):
                        e = v.bn_stats(stats[:, bass.ds(i * TPC + q, 1), :].rearrange("p n c -> p (n c)"),
                                       xres[:, bass.ds(i * TPC + q, 1), :].rearrange("p n d -> p (n d)"))
                    e.then_inc(s["st_ok"], 1)

        def convolve():
            m_ = small

            def taps(m):
                v.wait_ge(s["tap_ok"], m + 1)
                v.wait_ge(s["cbz"], 1)
                for i in range(1, PAD):
                    link(v.scalar_tensor_tensor(out=ysums[m][:, :, :], in0=cb[:, m % 2, :, i:i + T],
                                                scalar=cw[:, m, i:i + 1], in1=ysums[m][:, :, :],
                                                op0=ALU.mult, op1=ALU.add))

            def last_tap(m):
                if m > 0:
                    v.wait_ge(s["tq_ok"], 4 * m)
                for b in range(B):
                    g, q = divmod(b, NQ)
                    e = v.scalar_tensor_tensor(out=y[:, g, :, q, :],
                                               in0=cb[:, m % 2, b, 0:T].rearrange("p (c t) -> p c t", t=CH),
                                               scalar=cw[:, m, 0:1],
                                               in1=ysums[m][:, b, :].rearrange("p (c t) -> p c t", t=CH),
                                               op0=ALU.mult, op1=ALU.add)
                e.then_inc(s["conv_ok"], 1)

            def square_sums(m):
                per = P // DK
                for r in range(2):
                    v.wait_ge(s["sq_ok"], 2 * m + r + 1)
                    v.tensor_reduce(ss_qk[:, r * NT // 2:(r + 1) * NT // 2, m * per:(m + 1) * per],
                                    sqs[r][:, :, :].rearrange("p n (h d) -> p n h d", d=DK), AX_X,
                                    ALU.add).then_inc(s["l2_ss"], 1)

            def softplus_in():
                v.wait_ge(s["pj_ev"], (FM - 1) * NCHUNK + NT)
                v.tensor_tensor(m_["z"][:, :, :], ab[:, :, 0:H], dtb[:, :].unsqueeze(1).broadcast_to((P, NT, H)),
                                ALU.add).then_inc(s["dch"], 1)
                chain[0] += 1
                v.wait_ge(s["dch"], chain[0])
                v.scalar_tensor_tensor(out=m_["az"][:, :, :], in0=m_["z"][:, :, :], scalar=-1.0,
                                       in1=m_["z"][:, :, :], op0=ALU.mult, op1=ALU.max).then_inc(s["z_ok"], 1)

            def softplus_mid():
                v.wait_ge(s["ez_ok"], 3)
                link(v.tensor_scalar(m_["w"][:, :, :], m_["ez"][:, :, :], 1.0, None, ALU.add))
                v.tensor_scalar(m_["isone"][:, :, :], m_["w"][:, :, :], 1.0, None, ALU.is_equal).then_inc(s["w_ok"], 1)
                link(v.tensor_scalar(m_["eb"][:, :, :], m_["eb"][:, :, :], 1.0, None, ALU.add))
                v.reciprocal(m_["beta"][:, :, :], m_["eb"][:, :, :]).then_inc(s["beta_ok"], 1)

            def decay():
                v.wait_ge(s["lnw_ok"], 1)
                v.wait_ge(s["w_ok"], 1)
                v.tensor_tensor(m_["lnw"][:, :, :], m_["lnw"][:, :, :], m_["isone"][:, :, :], ALU.add)
                link(v.scalar_tensor_tensor(out=m_["w"][:, :, :], in0=m_["w"][:, :, :], scalar=-1.0,
                                            in1=m_["isone"][:, :, :], op0=ALU.add, op1=ALU.add))
                link(v.reciprocal(m_["w"][:, :, :], m_["w"][:, :, :]))
                link(v.tensor_tensor(m_["lnw"][:, :, :], m_["lnw"][:, :, :], m_["ez"][:, :, :], ALU.mult))
                link(v.tensor_tensor(m_["lnw"][:, :, :], m_["lnw"][:, :, :], m_["w"][:, :, :], ALU.mult))
                link(v.scalar_tensor_tensor(out=m_["sp"][:, :, :], in0=m_["z"][:, :, :], scalar=0.0,
                                            in1=m_["lnw"][:, :, :], op0=ALU.max, op1=ALU.add))
                v.scalar_tensor_tensor(out=m_["g"][:, :, :], in0=m_["sp"][:, :, :], scalar=-1.0,
                                       in1=alog[:, :].unsqueeze(1).broadcast_to((P, NT, H)),
                                       op0=ALU.mult, op1=ALU.mult).then_inc(s["g_ok"], 1)

            for m in range(4):
                taps(m)
                last_tap(m)
                if 0 < m < 3:
                    square_sums(m - 1)
            softplus_in()
            square_sums(2)
            softplus_mid()
            taps(4)
            decay()
            last_tap(4)
            v.wait_ge(s["l2_sd"], 2)
            link(v.reciprocal(ss_qk[:, :, :], ss_qk[:, :, :]))
            qk4 = qkv[:, :, 0:2 * QK].rearrange("p n (h d) -> p n h d", d=DK)
            link(v.tensor_tensor(qk4, qk4, ss_qk[:, :, :].unsqueeze(3).broadcast_to((P, NT, 2 * H, DK)), ALU.mult))
            v.wait_ge(s["pj_ev"], FM * NCHUNK + NT)
            v.transpose(kT[:, :, :], qkv[:, :, QK:2 * QK]).then_inc(s["kT_ok"], 1)
            v.transpose(kq[:, 1, :, :], qkv[:, :, 0:QK]).then_inc(s["qk_ok"], 1)
            v.wait_ge(s["conv_ok"], 5)
            v.wait_ge(s["beta_ok"], 1)
            for r in range(2):
                half = slice(r * NT // 2, (r + 1) * NT // 2)
                if r > 0:
                    v.wait_ge(s["qT_ok"], r)
                v.tensor_tensor(kb[:, :, :].rearrange("p n (h d) -> p n h d", h=H),
                                qkv[:, half, QK:2 * QK].rearrange("p n (h d) -> p n h d", h=H),
                                small["beta"][:, half, :].unsqueeze(3).broadcast_to((P, NT // 2, H, DK)),
                                ALU.mult).then_inc(s["kb_ok"], 1)
                v.wait_ge(s["kb_ok"], r + 1)
                v.transpose(kq[:, 0, half, :], kb[:, :, :]).then_inc(s["qT_ok"], 1)
            taps(5)
            last_tap(5)

        def from_start():
            v.wait_ge(s["ge_ok"], 1)
            v.wait_ge(s["conv_ok"], FM)
            q4 = qkv[:, :, 0:QK].rearrange("p n (h d) -> p n h d", d=DK)
            G4 = ge[:, 0, :].rearrange("p (n h) -> p n h", h=H)
            v.wait_ge(s["qk_ok"], 1)
            link(v.tensor_tensor(small["bG"][:, :, :], small["beta"][:, :, :], G4, ALU.mult))
            link(v.tensor_tensor(q4, q4, G4.unsqueeze(3).broadcast_to((P, NT, H, DK)), ALU.mult))
            v.transpose(qgT[:, :, :], qkv[:, :, 0:QK]).then_inc(s["scaled_ok"], 1)

        def triangles():
            v.wait_ge(s["mask_ok"], 2)
            for r in range(INST // 8):
                v.wait_ge(s["gm_ok"], r + 1)
                b = ps[:, r % 4, :].rearrange("p (i w t) -> p i w t", i=8, w=2)
                c = slice(8 * r, 8 * r + 8)
                v.tensor_tensor(ltn[:, c, :], ltn[:, c, :], b[:, :, 0, :], ALU.mult)
                v.tensor_tensor(dec[:, c, :], dec[:, c, :], b[:, :, 1, :], ALU.mult).then_inc(s["gm_ev"], 1)
            from_start()
            v.wait_ge(s["u_init"], 2)
            v.wait_ge(s["tri_r"], 16)
            for c in range(POOL_ROWS, CH - 1):
                rows, cols = c + 1 - POOL_ROWS, CH - 1 - c
                tmp = tmpU[:, :, 0:rows * cols].rearrange("p h (j i) -> p h j i", j=rows)
                mine = slice(POOL_ROWS, c + 1)
                link(v.tensor_tensor(tmp, X[:, :, c:c + 1, c + 1:CH].broadcast_to((P, IH, rows, cols)),
                                     U[:, :, mine, c:c + 1].broadcast_to((P, IH, rows, cols)), ALU.mult))
                dst = U[:, :, mine, c + 1:CH]
                e = v.tensor_tensor(dst, dst, tmp, ALU.add)
                if c < CH - 2:
                    link(e)
            e.then_inc(s["inv_ok"], 1)

        def chunk_steps():
            v.wait_ge(s["kE_ok"], 2)
            heads = "p g (h d) -> p g h d"
            flat = "p n h -> p (n h)"

            def residues(c):
                vb = qkv[:, c:NT:NC, 2 * QK:FEAT]
                if c == 0:
                    v.tensor_copy(R[:, :, :], vb).then_inc(s["R_ok"], 1)
                    return
                v.wait_ge(s["r_ok"], c)
                bg = small["bG"][:, c:NT:NC, :].unsqueeze(3).broadcast_to((P, NG, H, DV))
                link(v.tensor_tensor(tmpR[:, :, :].rearrange(heads, h=H),
                                     ps[:, 0:2, 0:VD].rearrange(heads, h=H), bg, ALU.mult))
                v.tensor_tensor(R[:, :, :], vb, tmpR[:, :, :], ALU.subtract).then_inc(s["R_ok"], 1)
                if c < NC - 1:
                    gt = ge[:, 2, :].rearrange("p (n h) -> p n h", h=H)[:, c:NT:NC, :].unsqueeze(3).broadcast_to(
                        (P, NG, H, DV))
                    link(v.tensor_tensor(tmpS[:, :, :].rearrange(heads, h=H), S[:, c % 2, :, :].rearrange(heads, h=H), gt,
                                         ALU.mult))

            def low(c):
                for g in range(NG):
                    v.wait_ge(s["oh_ok"], NG * c + g + 1)
                    v.tensor_tensor(ol[:, g, :, :].rearrange("p k t -> p (k t)"), ps[:, 6 + g, 0:KO * P],
                                    oh[:, g, :, :].rearrange("p k t -> p (k t)").bitcast(F32),
                                    ALU.subtract).then_inc(s["ol_ok"], 1)

            def mean_square(c):
                cs = slice(c * NG * H, (c + 1) * NG * H)
                ov = qkv[:, c:NT:NC, 2 * QK:FEAT]
                rms = small["orms"][:, :, :].rearrange(flat)[:, cs]
                v.wait_ge(s["o_ev"], c + 1)
                v.wait_ge(s["R_ok"], min(c + 2, NC))
                link(v.tensor_tensor(osq[:, :, :], ov, ov, ALU.mult))
                link(v.tensor_reduce(rms, osq[:, :, :].rearrange("p g (h d) -> p (g h) d", h=H), AX_X, ALU.add))
                v.tensor_scalar(rms, rms, 1.0 / DV, EPS, ALU.mult, ALU.add).then_inc(s["ost_ok"], 1)

            def state(c):
                v.wait_ge(s["su_ok"], c + 1)
                if c == 0:
                    v.tensor_copy(S[:, 1, :, :], ps[:, 0:2, 0:VD]).then_inc(s["S_ok"], 1)
                else:
                    v.tensor_tensor(S[:, (c + 1) % 2, :, :], tmpS[:, :, :], ps[:, 0:2, 0:VD], ALU.add).then_inc(s["S_ok"], 1)

            def normalize(c):
                ov = qkv[:, c:NT:NC, 2 * QK:FEAT]
                ov4 = ov.rearrange(heads, h=H)
                std = small["ostd"][:, :, :].rearrange(flat)[:, c * NG * H:(c + 1) * NG * H]
                v.wait_ge(s["osd_ok"], c + 1)
                link(v.reciprocal(std, std))
                r4 = std.rearrange("p (g h) -> p g h", g=NG).unsqueeze(3).broadcast_to((P, NG, H, DV))
                link(v.tensor_tensor(ov4, ov4, r4, ALU.mult))
                v.tensor_tensor(ov, ov, silug[:, c:NT:NC, :], ALU.mult).then_inc(s["on_ok"], 1)

            def residual(c):
                for g in range(NG):
                    n = g * NC + c
                    v.wait_ge(s["wo_ok"], NG * c + g + 1)
                    v.tensor_tensor(xres[:, n, :], xres[:, n, :], ps[:, 6 + g, 0:D], ALU.add).then_inc(s["wo_ev"], 1)

            def statistics(c):
                v.wait_ge(s["wo_ev"], NG * (c + 1))
                for g in range(NG):
                    n = g * NC + c
                    e = v.bn_stats(stats[:, n, :], xres[:, n, :])
                e.then_inc(s["st_ok"], 1)

            for c in range(NC + 2):
                if c < NC:
                    residues(c)
                if c >= 3:
                    statistics(c - 3)
                if c >= 2:
                    low(c - 2)
                if 0 < c <= NC:
                    mean_square(c - 1)
                if c < NC - 1:
                    state(c)
                if 0 < c <= NC:
                    normalize(c - 1)
                if c >= 2:
                    residual(c - 2)
            statistics(NC - 1)

        for n in ("p_ok", "a_ok", "res_ok"):
            v.sem_inc(s[n], 1)
        selector(0)
        layernorm(0)
        feed_forward(0)
        v.wait_ge(s["res_ok"], 1 + NCHUNK)
        v.wait_ge(s["small_in"], 16 * 11)
        v.wait_ge(s["rattn"], 16 * 13)
        v.tensor_scalar(wo_r[:, :, :], wo_r[:, :, :], nwt[:, 0:1], None, ALU.mult).then_inc(s["wo_sc"], 1)
        layernorm(1)
        convolve()
        triangles()
        chunk_steps()
        layernorm(2)
        feed_forward(1)

    ctx.close()


_INS = ["hidden_states", "Wq", "Wk", "Wv", "Wg", "Wa", "Wb", "Wo", "conv_wq", "conv_wk", "conv_wv",
        "A_log", "dt_bias", "norm_weight"]
_FFN = ["gate_w", "w1", "w2", "w3", "sw1", "sw2", "sw3"]


def kernel(**inputs):
    import numpy as _np
    import concourse.bacc as _bacc
    from concourse import mybir as _mybir
    from concourse.bass_utils import run_bass_kernel_spmd as _run

    nc = _bacc.Bacc("TRN2", target_bir_lowering=False, num_devices=1)
    arrays, args = {}, []
    for name in [f"L0_attn_{n}" for n in _INS] + [f"L0_ffn_{n}" for n in _FFN] + ["constants"]:
        a = constants(_np) if name == "constants" else _np.asarray(inputs[name])
        if name in ("L0_attn_A_log", "L0_attn_dt_bias"):
            a = _np.broadcast_to(a[None, :], (P, H))
        if name == "L0_attn_norm_weight":
            a = a.reshape(DV, 1)
        if name == "L0_ffn_gate_w":
            a = a.T
        a = _np.ascontiguousarray(a)
        arrays[f"in_{name}_dram"] = a
        args.append(nc.dram_tensor(f"in_{name}_dram", a.shape, _mybir.dt.from_np(a.dtype), kind="ExternalInput").ap())
    args.append(nc.dram_tensor("out_0_dram", (B, T, D), _mybir.dt.float32, kind="ExternalOutput").ap())
    macaron(nc, *args)
    r = _run(nc, [arrays], core_ids=[0])
    return r.results[0]["out_0_dram"]
```

```python
from contextlib import ExitStack

import concourse.bass as bass
from concourse import mybir

ALU = mybir.AluOpType
ACT = mybir.ActivationFunctionType
AX_X = mybir.AxisListType.X
F32 = mybir.dt.float32
F32R = mybir.dt.float32r

P = 128
B, T, D = 8, 256, 256
CH = 32
NQ = P // CH
NG = B // NQ
NC = T // CH
NT = NG * NC
KD = D // P
NP = NT // 2
TOK = NT * P
E, HID = 8, 176
HT = (E * HID + HID + P - 1) // P
HF = HT * P
FULL = HT - 1
REST = (E + 1) * HID - FULL * P
HALF = P // 2
assert 0 < REST <= HALF and FULL * P >= E * HID
UF = FULL * P
CHUNK = 512
NCHUNK = TOK // CHUNK
TPC = CHUNK // P
H, DK, DV = 6, 32, 64
QK, VD = H * DK, H * DV
FEAT = 2 * QK + VD
FM = FEAT // P
GAB = VD + 2 * H
KO = VD // P
INST = NT * H
IH = INST // 32
TAPS = 4
PAD = TAPS - 1
EARLY = 2
POOL_ROWS = 3
ROUTE = E + 1
EPS = 1e-5

RING = 4
LAG = 3
assert (HT - 1) % RING == 0


def slot(j):
    return j % RING if j < HT - 1 else RING


def pieces(j):
    if j == FULL:
        return [(0, HALF, E)]
    out, p = [], 0
    while p < P:
        e = min((j * P + p) // HID, E)
        q = P if e == E else min(P, (e + 1) * HID - j * P)
        out.append((p, q, e))
        p = q
    return out


def arrived(j, upto=None):
    return 16 * sum(len(pieces(m)) for m in range(HT if upto is None else upto + 1) if slot(m) == slot(j))


C_ID, C_TRI, C_STR, C_BLK = 0, P, 2 * P, 3 * P
C_INC = 4 * P
C_NST = C_INC + CH
C_TIE = C_NST + CH
C_THR = C_TIE + E * E
C_ALL = C_THR + E


def constants(np):
    c = np.zeros((P, C_ALL), np.float32)
    p = np.arange(P)
    same = p[:, None] // CH == p[None, :] // CH
    c[:, C_ID:C_ID + P] = np.eye(P)
    c[:, C_TRI:C_TRI + P] = same & (p[:, None] <= p[None, :])
    c[:, C_STR:C_STR + P] = same & (p[:, None] > p[None, :])
    c[:, C_BLK:C_BLK + P] = same
    t = np.arange(CH)
    c[:, C_INC:C_INC + CH] = (p % CH)[:, None] <= t[None, :]
    c[:, C_NST:C_NST + CH] = -1.0 * ((p % CH)[:, None] < t[None, :])
    e = np.arange(E)
    c[:, C_TIE:C_TIE + E * E] = (e[None, :] < e[:, None]).reshape(1, E * E)
    c[:, C_THR:C_THR + E] = e + 0.5 - (E - 2)
    return c


def macaron(nc, x, wq, wk, wv, wg, wa, wb, wo, cwq, cwk, cwv, a_log, dt_bias, nw, gate_w,
            w1, w2, w3, sw1, sw2, sw3, consts, out):
    ctx = ExitStack()
    base = (nc.sbuf_base + 63) // 64 * 64
    room = nc.sbuf_usable_end - base

    def at(name, off, shape, dt=F32):
        n = 4
        for s in shape[1:]:
            n *= s
        assert off + n <= room, (name, off + n, room)
        return nc.alloc_sbuf_tensor_at(name, shape, dt, offset=base + off)

    def sem(name):
        return ctx.enter_context(nc.semaphore(name))

    KB = 1024
    xres = at("xres", 0, [P, NT, D])
    xhi = at("xhi", 16 * KB, [P, KD, TOK], F32R)
    xlo = at("xlo", 32 * KB, [P, KD, TOK], F32R)
    o = 48 * KB
    ident = at("ident", o, [P, C_ALL])
    o += 4 * C_ALL
    stats = at("stats", o, [P, NT, 6])
    o += 4 * NT * 6
    moments = at("moments", o, [P, NT, 2])
    o += 4 * NT * 2
    vareps = at("vareps", o, [P, NT])
    o += 4 * NT
    stdev = at("stdev", o, [P, NT])
    o += 4 * NT
    rstd = at("rstd", o, [P, NT])
    o += 4 * NT
    offset = at("offset", o, [P, NT])
    o += 4 * NT
    XN = o
    xn = at("xn", o, [P, 4, D])
    o += 16 * D
    F = (o + 63) // 64 * 64
    triu = ident[:, C_TRI:C_TRI + P]
    strict = ident[:, C_STR:C_STR + P]
    blocks = ident[:, C_BLK:C_BLK + P]
    incl = ident[:, C_INC:C_INC + CH]
    nstrict = ident[:, C_NST:C_NST + CH]
    tie = ident[:, C_TIE:C_TIE + E * E]
    places = ident[:, C_THR:C_THR + E]

    WB = 4 * KD * HF
    W2B = 4 * HT * D
    assert WB == W2B
    ffn = []
    for f in range(2):
        t = {}
        for n, name in enumerate(["w1h", "w1l", "w3h", "w3l"]):
            t[name] = at(f"{name}_{f}", F + n * WB, [P, KD, HF if name[1] == "1" else UF], F32R)
        for n, name in enumerate(["w2h", "w2l"]):
            t[name] = at(f"{name}_{f}", F + (4 + n) * WB, [P, HT, D], F32R)
        r = F + 6 * WB
        early = r if f == 0 else 16 * KB
        t["r1"] = at(f"r1_{f}", early, [P, KD, HF])
        t["r3"] = at(f"r3_{f}", early + WB, [P, KD, UF])
        t["r2"] = at(f"r2_{f}", r + 2 * WB, [P, HT, D])
        C4 = 4 * CHUNK
        t["s"] = at(f"s_{f}", r, [P, 2, CHUNK])
        t["p"] = at(f"p_{f}", r + 2 * C4, [P, 2, CHUNK])
        t["a"] = at(f"a_{f}", r + 4 * C4, [P, 2, CHUNK])
        t["ahi"] = at(f"ahi_{f}", r + 6 * C4, [P, LAG + 1, CHUNK], F32R)
        t["alo"] = at(f"alo_{f}", r + (7 + LAG) * C4, [P, LAG + 1, CHUNK], F32R)
        assert (8 + 2 * LAG) * C4 <= 3 * WB
        r += 3 * WB
        t["cring"] = at(f"cring_{f}", r, [P, RING + 1, CHUNK])
        r += 4 * (RING + 1) * CHUNK
        t["sT"] = at(f"sT_{f}", r, [P, TOK])
        t["gt"] = at(f"gt_{f}", r, [P, NT, E, E])
        t["cT"] = at(f"cT_{f}", r, [P, TOK])
        r += 4 * TOK
        for name in ["gr", "gh", "gl"]:
            t[name] = at(f"{name}_{f}", r, [P, KD, E], F32 if name == "gr" else F32R)
            r += 4 * KD * E
        for name in ["sc", "rank", "less", "ss"]:
            t[name] = at(f"{name}_{f}", r, [P, NT, E])
            r += 4 * NT * E
        for name in ["cs", "cr"]:
            t[name] = at(f"{name}_{f}", r, [P, NT])
            r += 4 * NT
        t["c9"] = at(f"c9_{f}", r, [P, NT, ROUTE])
        r += 4 * NT * ROUTE
        ffn.append(t)
    FEND = (r + 63) // 64 * 64

    wqkv_r = at("wqkv_r", FEND, [P, KD, FEAT])
    wgab_r = at("wgab_r", FEND + 4 * KD * FEAT, [P, KD, GAB])
    o = FEND + 4 * KD * FEAT + 4 * KD * GAB
    wo_r = at("wo_r", o, [P, KO, D])
    AEND = o + 4 * KO * D
    woh = at("woh", F, [P, KO, D], F32R)
    wol = at("wol", F + 4 * KO * D, [P, KO, D], F32R)
    o = F + 8 * KO * D
    silug = at("silug", o, [P, NT, VD])
    o += 4 * NT * VD
    qkv = at("qkv", o, [P, NT, FEAT])
    o += 4 * NT * FEAT
    BR = o
    wqkvh = at("wqkvh", o, [P, KD, FEAT], F32R)
    wqkvl = at("wqkvl", o + 4 * KD * FEAT, [P, KD, FEAT], F32R)
    o += 8 * KD * FEAT
    wgabh = at("wgabh", o, [P, KD, GAB], F32R)
    wgabl = at("wgabl", o + 4 * KD * GAB, [P, KD, GAB], F32R)
    o += 8 * KD * GAB
    cb = at("cb", o, [P, 2, B, PAD + T])
    o += 8 * B * (PAD + T)
    YS = o
    ysum0 = at("ysum0", YS, [P, B, T])
    y = at("y", o + 4 * B * T, [P, NG, NC, NQ, CH])
    o += 8 * B * T
    assert o <= FEND, (o, FEND)
    SL = 4 * INST * CH
    assert 12 * KD * FEAT >= SL and 2 * SL <= 8 * KD * (FEAT + GAB) + 4 * B * (PAD + T)
    dec = at("dec", BR, [P, INST, CH])
    kT = at("kT", BR + SL, [P, NT, QK])
    qgT = at("qgT", BR + 2 * SL, [P, NT, QK])
    kb = at("kb", YS, [P, NT // 2, QK])
    tt = at("tt", BR + 3 * SL, [P, INST, CH])
    assert o >= BR + 4 * SL
    ab = at("ab", o, [P, NT, 2 * H])
    o += 4 * NT * 2 * H
    ss_qk = at("ss_qk", o, [P, NT, 2 * H])
    o += 4 * NT * 2 * H
    small = {}
    for n in ["z", "az", "ez", "w", "lnw", "isone", "sp", "g", "eb", "beta", "bG", "orms", "ostd"]:
        small[n] = at("sm_" + n, o, [P, NT, H])
        o += 4 * NT * H
    ge = at("ge", o, [P, 3, INST])
    o += 12 * INST
    TL = o
    SB = 4 * NG * VD
    dlt, tmpS, tmpR = (at(n, TL + i * SB, [P, NG, VD]) for i, n in enumerate(["dlt", "tmpS", "tmpR"]))
    osq = tmpR
    assert 4 * IH * 256 <= SB
    tmpU = at("tmpU", TL, [P, IH, 256])
    tmpP = at("tmpP", TL + SB, [P, IH, POOL_ROWS * CH])
    oh = at("oh", TL + 3 * SB, [P, NG, KO, P], F32R)
    ol = at("ol", TL + 4 * SB, [P, NG, KO, P], F32R)
    R = at("R", XN, [P, NG, VD])
    rhsd = at("rhsd", TL, [P, INST, CH])
    ltn = at("ltn", TL, [P, INST, CH])
    sqs = [at("sq0", XN, [P, NT // 2, P]), at("sq1", TL + 4 * TOK, [P, NT // 2, P])]
    ysums = [ysum0, at("ysum1", TL, [P, B, T])] * (FM // 2)
    ysums[FM - 1] = at("ysum5", 40 * KB, [P, B, T])
    o = TL + 5 * SB
    assert o >= AEND and o >= TL + SL
    cw = at("cw", o, [P, FM, TAPS])
    o += 4 * FM * TAPS
    alog, dtb = at("alog", o, [P, H]), at("dtb", o + 32, [P, H])
    o += 64
    nwt = at("nwt", o, [P, 1])
    kq = at("kq", 16 * KB, [P, 2, NT, QK])
    X = at("X", 16 * KB, [P, IH, CH, CH])
    U = at("U", 16 * KB + SL, [P, IH, CH, CH])
    S = at("S", 42 * KB, [P, 2, NG, VD])

    ps = ctx.enter_context(nc.psum_tensor("ps", [P, 8, 512], F32))
    comb = [nc.dram_tensor(f"comb_{f}", [ROUTE, TOK], F32, kind="Internal").ap() for f in range(2)]
    tri_out = nc.dram_tensor("tri_out", [NQ, INST, CH, CH], F32, kind="Internal").ap()
    inv_in = nc.dram_tensor("inv_in", [NQ, INST, CH, CH], F32, kind="Internal").ap()

    names = ("x_in0 x_in1 const_in rw1 rw3 rw2 rgate rattn small_in x_out tri_w tri_r inv_w inv_a inv_r "
             "w1h_ok w3h_ok w2h_ok w1l_ok w3l_ok w2l_ok wgt_hi wgt_lo attn_hi attn_lo wo_sc "
             "st_ok ln_var ln_sd offset_ok xn_even xn_odd tr_ok xhi_ok xlo_ok "
             "sc_ok sig_ok scT_ok c9_ok c9T_ok cTa_ok cTb_ok comb_w "
             "h_ok u_ok silu_ok p_ok a_ok ahi_ok alo_ok ystep y_ok res_ok "
             "padz cbz pj_ok pj_ev tap_ok unit_ok q_unit conv_ok sq_ok tq_ok tq_ev dch "
             "l2_ss l2_sd z_ok ez_ok w_ok lnw_ok g_ok cum_ok ge_ok rhsd_ok dec_ok beta_ok kb_ok qk_ok "
             "kT_ok qT_ok mask_ok gm_ok gm_ev gm_n scaled_ok u_init row_ok inv_ok "
             "r_ok R_ok d_ok dlt_ok o_ok o_ev su_ok S_ok ost_ok osd_ok on_ok ot_ok oh_ok ol_ok wo_ok wo_ev kE_ok").split()
    s = {n: sem(n) for n in names + [f"cr{r}" for r in range(RING + 1)]}

    def gview(r):
        return r.rearrange("p (c b t) -> p c b t", c=TPC, b=NQ)

    def acc3(pe, dst, lh, ll, rh, rl, start, stop, **kw):
        pe.matmul(dst, ll, rh, start=start, stop=False, **kw)
        pe.matmul(dst, lh, rl, start=False, stop=False, **kw)
        return pe.matmul(dst, lh, rh, start=False, stop=stop, **kw)

    block = ctx.enter_context(nc.Block())

    @block.sync
    def _(sp):
        RT = E * HID

        def load_up(f):
            t = ffn[f]
            for key, w, sw, sm in (("r1", w1, sw1, "rw1"), ("r3", w3, sw3, "rw3")):
                for k in range(KD):
                    r = slice(k * P, (k + 1) * P)
                    sp.dma_start(t[key][:, k, 0:RT].rearrange("p (e h) -> p e h", e=E),
                                 w[:, r, :].rearrange("e p h -> p e h")).then_inc(s[sm], 16)
                    sp.dma_start(t[key][:, k, RT:UF], sw[r, 0:UF - RT]).then_inc(s[sm], 16)
                    if key == "r1":
                        sp.dma_start(t[key][:, k, UF:UF + REST], sw3[r, UF - RT:HID]).then_inc(s[sm], 16)
                        sp.dma_start(t[key][:, k, UF + HALF:UF + HALF + REST],
                                     sw1[r, UF - RT:HID]).then_inc(s[sm], 16)

        def load_gate(f):
            for k in range(KD):
                sp.dma_start(ffn[f]["gr"][:, k, :], gate_w[k * P:(k + 1) * P, :]).then_inc(s["rgate"], 16)

        def load_down(f):
            t = ffn[f]
            n = RT // P
            sp.dma_start(t["r2"][:, 0:n, :],
                         w2.rearrange("e h d -> (e h) d").rearrange("(n p) d -> p n d", p=P)).then_inc(s["rw2"], 16)
            sp.dma_start(t["r2"][:, n, :], sw2[0:P, :]).then_inc(s["rw2"], 16)
            sp.wait_ge(s["padz"], 3 * (f + 1))
            sp.dma_start(t["r2"][0:REST, FULL, :], sw2[HID - REST:HID, :]).then_inc(s["rw2"], 16)

        sp.dma_start(ident[:, :], consts[:, :]).then_inc(s["const_in"], 16)
        def expert_weights(f):
            t = ffn[f]

            def tile(i, j):
                for p0, p1, e in pieces(j):
                    sp.dma_start(t["cring"][p0:p1, slot(j), :],
                                 comb[f][e:e + 1, bass.ds(i * CHUNK, CHUNK)].broadcast_to((p1 - p0, CHUNK))
                                 ).then_inc(s[f"cr{slot(j)}"], 16)

            for r in range(2):
                half = slice(r * TOK // 2, (r + 1) * TOK // 2)
                sp.wait_ge(s[("cTa_ok", "cTb_ok")[r]], f + 1)
                sp.dma_start(comb[f][:, half], t["cT"][0:ROUTE, half]).then_inc(s["comb_w"], 16)
            sp.wait_ge(s["comb_w"], 32 * (f + 1))
            first = list(range(RING)) + [HT - 1]
            for j in first:
                tile(0, j)
            with sp.Fori(0, NCHUNK - 1) as i:
                for j in range(HT):
                    sp.wait_ge(s["a_ok"], HT * NCHUNK * f + i * HT + j + 2)
                    if j < HT - 1 - RING:
                        tile(i, j + RING)
                    else:
                        tile(i + 1, slot(j) if j < HT - 1 else j)
            for j in range(HT - 1 - RING):
                sp.wait_ge(s["a_ok"], HT * (NCHUNK * (f + 1) - 1) + j + 2)
                tile(NCHUNK - 1, j + RING)

        load_gate(0)
        for b in range(B):
            g, q = divmod(b, NQ)
            sp.dma_start(xres[CH * q:CH * q + CH, g * NC:(g + 1) * NC, :],
                         x[b].rearrange("(c t) d -> t c d", t=CH)).then_inc(s[f"x_in{g}"], 16)
        load_up(0)
        load_down(0)
        for k in range(KD):
            r = slice(k * P, (k + 1) * P)
            sp.dma_start(wqkv_r[:, k, 0:QK], wq[r, :]).then_inc(s["rattn"], 16)
            sp.dma_start(wqkv_r[:, k, QK:2 * QK], wk[r, :]).then_inc(s["rattn"], 16)
            sp.dma_start(wqkv_r[:, k, 2 * QK:FEAT], wv[r, :]).then_inc(s["rattn"], 16)
            sp.dma_start(wgab_r[:, k, 0:VD], wg[r, :]).then_inc(s["rattn"], 16)
            sp.dma_start(wgab_r[:, k, VD:VD + H], wa[r, :]).then_inc(s["rattn"], 16)
            sp.dma_start(wgab_r[:, k, VD + H:GAB], wb[r, :]).then_inc(s["rattn"], 16)
        sp.dma_start(wo_r[:, :, :], wo.rearrange("(k p) d -> p k d", p=P)).then_inc(s["rattn"], 16)
        row = 0
        for w, rows in ((cwq, QK), (cwk, QK), (cwv, VD)):
            done = 0
            while done < rows:
                m, p0 = divmod(row, P)
                n = min(P - p0, rows - done)
                sp.dma_start(cw[p0:p0 + n, m, :], w[done:done + n, :]).then_inc(s["small_in"], 16)
                done += n
                row += n
        sp.dma_start(alog[:, :], a_log).then_inc(s["small_in"], 16)
        sp.dma_start(dtb[:, :], dt_bias).then_inc(s["small_in"], 16)
        for r in range(P // DV):
            sp.dma_start(nwt[r * DV:(r + 1) * DV, :], nw).then_inc(s["small_in"], 16)

        expert_weights(0)

        for g in range(NG):
            n = slice(g * INST // NG, (g + 1) * INST // NG)
            sp.wait_ge(s["gm_ev"], (g + 1) * INST // 8 // NG)
            for q in range(NQ):
                sp.dma_start(tri_out[q, n].rearrange("n s t -> s n t"),
                             ltn[CH * q:CH * q + CH, n, :]).then_inc(s["tri_w"], 16)
        sp.wait_ge(s["tri_w"], 16 * NQ * NG)
        sp.dma_start(X[:, :, :, :].rearrange("p h s t -> p (h s t)"),
                     tri_out.rearrange("q (n h) s t -> (q n) (h s t)", h=IH)).then_inc(s["tri_r"], 16)
        sp.wait_ge(s["inv_ok"], 2)
        sp.dma_start(inv_in.rearrange("q (n h) s t -> (q n) (h s t)", h=IH),
                     U[:, :, :, :].rearrange("p h s t -> p (h s t)")).then_inc(s["inv_w"], 16)
        sp.wait_ge(s["inv_w"], 16)
        for sm, c in (("inv_a", slice(0, EARLY)), ("inv_r", slice(EARLY, NC))):
            for g in range(NG):
                n = slice((g * NC + c.start) * H, (g * NC + c.stop) * H)
                for q in range(NQ):
                    sp.dma_start(tt[CH * q:CH * q + CH, n, :],
                                 inv_in[q, n].rearrange("n s t -> s n t")).then_inc(s[sm], 16)

        load_up(1)
        sp.wait_ge(s["o_ok"], NC)
        load_down(1)
        sp.wait_ge(s["wo_ev"], NT)
        load_gate(1)
        expert_weights(1)

        for i in range(NCHUNK):
            sp.wait_ge(s["res_ok"], 1 + NCHUNK + i + 1)
            g, half = divmod(i, NCHUNK // NG)
            for q in range(NQ):
                tok = slice(half * TPC * CH, (half + 1) * TPC * CH)
                sp.dma_start(out[g * NQ + q, tok].rearrange("(c t) d -> t c d", t=CH),
                             xres[CH * q:CH * q + CH, i * TPC:(i + 1) * TPC, :]).then_inc(s["x_out"], 16)
        sp.wait_ge(s["x_out"], 16 * NQ * NCHUNK)

    @block.tensor
    def _(pe):
        def layernorm(ph):
            if ph == 0:
                pe.wait_ge(s["const_in"], 16)
            f, route = divmod(ph, 2)

            def scores(i):
                t = ffn[f]
                if i == 0:
                    pe.wait_ge(s["wgt_lo"], f + 1)
                pe.wait_ge(s["xlo_ok"], NP * ph + (i + 1) * TPC // 2)
                for k in range(KD):
                    c = slice(i * CHUNK, (i + 1) * CHUNK)
                    mm = acc3(pe, ps[0:E, 4 + i, :], t["gh"][:, k, :], t["gl"][:, k, :], xhi[:, k, c], xlo[:, k, c],
                              k == 0, k == KD - 1)
                mm.then_inc(s["sc_ok"], 1)

            for n in range(NT):
                m = n // 2
                if route == 0 and n in (6, 10, 14):
                    scores((n - 6) // 4)
                pe.wait_ge(s[("xn_even", "xn_odd")[n % 2]], NP * ph + m + 1)
                if n % 2 == 0 and m >= 4:
                    pe.wait_ge(s["xlo_ok"], NP * ph + m - 3)
                for k in range(KD):
                    mm = pe.transpose(ps[:, m % 4, k * 2 * P + (n % 2) * P:k * 2 * P + (n % 2) * P + P],
                                      xn[:, n % 4, k * P:(k + 1) * P], ident[:, C_ID:C_ID + P])
                mm.then_inc(s["tr_ok"], 1)
            if route == 0:
                scores(NCHUNK - 1)

        def route(f):
            t = ffn[f]
            pe.wait_ge(s["sig_ok"], NCHUNK * (f + 1))
            for n in range(NT):
                mm = pe.transpose(ps[:, 0, n * E:(n + 1) * E], t["sT"][0:E, n * P:(n + 1) * P],
                                  ident[0:E, C_ID:C_ID + E])
            mm.then_inc(s["scT_ok"], 1)
            pe.wait_ge(s["c9_ok"], f + 1)
            for n in range(NT):
                mm = pe.transpose(ps[0:ROUTE, 4 + n // TPC, (n % TPC) * P:(n % TPC + 1) * P], t["c9"][:, n, :],
                                  ident[:, C_ID:C_ID + P])
                if n % (NT // 2) == NT // 2 - 1:
                    mm.then_inc(s["c9T_ok"], 1)
            pe.wait_ge(s["w1l_ok"], KD * (f + 1))

        def feed_forward(f):
            t = ffn[f]
            route(f)
            with pe.Fori(0, NCHUNK) as i:
                c = bass.ds(i * CHUNK, CHUNK)
                steps = HT * NCHUNK * f + i * HT

                def down(j):
                    pe.wait_ge(s["alo_ok"], steps + j + 2)
                    if j == 0:
                        pe.wait_ge(s["res_ok"], 1 + i + NCHUNK * f)
                        pe.wait_ge(s["w2l_ok"], f + 1)
                        pe.wait_ge(s["cTb_ok"], f + 1)
                    rows = slice(0, P) if j < FULL else slice(0, HALF)
                    for q in range(TPC):
                        dst = ps[:, 6 + q // 2, (q % 2) * D:(q % 2 + 1) * D]
                        tok = slice(q * P, (q + 1) * P)
                        mm = acc3(pe, dst, t["ahi"][rows, j % (LAG + 1), tok], t["alo"][rows, j % (LAG + 1), tok],
                                  t["w2h"][rows, j, :], t["w2l"][rows, j, :],
                                  j == 0 and q % 2 == 0, j == HT - 1, skip_group_check=True)
                    mm.then_inc(s["ystep"], 1)

                pe.wait_ge(s["p_ok"], 1 + steps)
                for j in range(HT):
                    hid = slice(j * P, (j + 1) * P)
                    pe.wait_ge(s["silu_ok"], 1 + steps + max(j - 1, 0))
                    for k in range(KD):
                        mm = acc3(pe, ps[:, j % 2, :], t["w1h"][:, k, hid], t["w1l"][:, k, hid],
                                  xhi[:, k, c], xlo[:, k, c], k == 0, k == KD - 1)
                    mm.then_inc(s["h_ok"], 1)
                    if j < FULL:
                        pe.wait_ge(s["p_ok"], 1 + steps + max(j - 1, 0))
                        if j == 0:
                            pe.wait_ge(s["w3l_ok"], f + 1)
                        for k in range(KD):
                            mm = acc3(pe, ps[:, 2 + j % 2, :], t["w3h"][:, k, hid], t["w3l"][:, k, hid],
                                      xhi[:, k, c], xlo[:, k, c], k == 0, k == KD - 1)
                        mm.then_inc(s["u_ok"], 1)
                    if j >= LAG:
                        down(j - LAG)
                for j in range(HT - LAG, HT):
                    down(j)

        def project():
            pe.wait_ge(s["xlo_ok"], 2 * NP)
            pe.wait_ge(s["attn_lo"], 2)

            job = [0]

            def bank():
                n = job[0]
                job[0] += 1
                if n >= 4:
                    pe.wait_ge(s["pj_ev"], n - 3)
                return n % 4

            def features(m):
                for ch in range(NCHUNK):
                    n = bank()
                    c = slice(ch * CHUNK, (ch + 1) * CHUNK)
                    f = slice(m * P, (m + 1) * P)
                    for k in range(KD):
                        mm = acc3(pe, ps[:, n, :], wqkvh[:, k, f], wqkvl[:, k, f], xhi[:, k, c], xlo[:, k, c],
                                  k == 0, k == KD - 1)
                    mm.then_inc(s["pj_ok"], 1)

            def gate_tiles(r):
                for i in range(4 * r, 4 * r + 4):
                    n = bank()
                    c = slice(i * P, (i + 1) * P)
                    for k in range(KD):
                        mm = acc3(pe, ps[:, n, 0:GAB], xhi[:, k, c], xlo[:, k, c], wgabh[:, k, :], wgabl[:, k, :],
                                  k == 0, k == KD - 1)
                    mm.then_inc(s["pj_ok"], 1)

            def turn(m):
                pe.wait_ge(s["conv_ok"], m + 1)
                for r in range(4):
                    if m > 0:
                        pe.wait_ge(s["tq_ev"], 4 * (m - 1) + r + 1)
                    for i in range(4):
                        g, c = divmod(4 * r + i, NC)
                        mm = pe.transpose(ps[:, 4 + r, i * P:(i + 1) * P],
                                          y[:, g, c, :, :].rearrange("p b t -> p (b t)"),
                                          ident[:, C_ID:C_ID + P])
                    mm.then_inc(s["tq_ok"], 1)

            features(0)
            features(1)
            gate_tiles(0)
            for m in range(FM - 2):
                turn(m)
                features(m + 2)
                if m < 3:
                    gate_tiles(m + 1)
            decays()
            turn(FM - 2)
            grams(turn)

        def decays():
            pe.wait_ge(s["pj_ev"], FM * NCHUNK + NT)
            pe.wait_ge(s["g_ok"], 1)
            gall = small["g"][:, :, :].rearrange("p n h -> p (n h)")
            for r, m in enumerate((triu, strict, blocks)):
                mm = pe.matmul(ps[:, 0, r * INST:(r + 1) * INST], m, gall, start=True, stop=True)
            mm.then_inc(s["cum_ok"], 1)
            pe.wait_ge(s["rhsd_ok"], 1)
            per = 512 // CH
            for r in range(INST // per):
                if r == 3:
                    pe.wait_ge(s["ge_ok"], 1)
                if r > 3:
                    pe.wait_ge(s["dec_ok"], r - 3)
                pe.matmul(ps[:, (1 + r) % 4, :], strict, rhsd[:, r * per:(r + 1) * per, :], start=True,
                          stop=True).then_inc(s["cum_ok"], 1)

        def grams(turn):
            pe.wait_ge(s["kT_ok"], 1)
            pe.wait_ge(s["qk_ok"], 1)
            pe.wait_ge(s["dec_ok"], INST * CH // 512)
            pe.wait_ge(s["ge_ok"], 1)
            for i in range(INST):
                n, h = divmod(i, H)
                bank = (i // 8) % 4
                if i % (INST // 2) == 0:
                    pe.wait_ge(s["qT_ok"], 1 + i // (INST // 2))
                if i == 3 * 8:
                    turn(FM - 1)
                if i % 8 == 0 and i >= 4 * 8:
                    pe.wait_ge(s["gm_ev"], i // 8 - 3)
                f = slice(h * DK, (h + 1) * DK)
                for q in range(NQ):
                    r = slice(CH * q, CH * q + CH)
                    mm = pe.matmul(ps[r, bank, (i % 8) * 2 * CH:(i % 8 + 1) * 2 * CH], kT[r, n, f], kq[r, :, n, f],
                                   start=True, stop=True)
                if i % 8 == 7:
                    mm.then_inc(s["gm_ok"], 1)

        def chunk_steps():
            pe.wait_ge(s["inv_a"], 16 * NQ * NG)
            pe.wait_ge(s["gm_ev"], INST // 8)
            pe.wait_ge(s["tq_ev"], 4 * FM)
            pe.wait_ge(s["scaled_ok"], 1)
            pe.wait_ge(s["kE_ok"], 2)
            pe.wait_ge(s["wo_sc"], 3)

            def each(groups=range(NG)):
                for g in groups:
                    for h in range(H):
                        for q in range(NQ):
                            yield g, h, slice(CH * q, CH * q + CH), slice(h * DV, (h + 1) * DV)

            def predict(c):
                pe.wait_ge(s["S_ok"], c)
                for g, h, r, v in each():
                    mm = pe.matmul(ps[r, g, v], kT[r, g * NC + c, h * DK:(h + 1) * DK], S[r, c % 2, g, v],
                                   start=True, stop=True)
                mm.then_inc(s["r_ok"], 1)

            def within(c):
                for g, h, r, v in each():
                    mm = pe.matmul(ps[r, 4 + g, v], dec[r, (g * NC + c) * H + h, :], dlt[r, g, v],
                                   start=(c == 0 and h == 0), stop=True, skip_group_check=True)
                mm.then_inc(s["o_ok"], 1)

            def turn(c):
                pe.wait_ge(s["on_ok"], c + 1)
                for g in range(NG):
                    if c > 0:
                        pe.wait_ge(s["wo_ev"], NG * (c - 1) + g + 1)
                    for k in range(KO):
                        mm = pe.transpose(ps[:, 6 + g, k * P:(k + 1) * P],
                                          qkv[:, g * NC + c, 2 * QK + k * P:2 * QK + (k + 1) * P],
                                          ident[:, C_ID:C_ID + P])
                    mm.then_inc(s["ot_ok"], 1)

            def deltas(c):
                pe.wait_ge(s["R_ok"], c + 1)
                if c == EARLY:
                    pe.wait_ge(s["inv_r"], 16 * NQ * NG)
                for g, h, r, v in each():
                    mm = pe.matmul(ps[r, 2 + g, v], tt[r, (g * NC + c) * H + h, :], R[r, g, v],
                                   start=True, stop=True)
                mm.then_inc(s["d_ok"], 1)

            def across(c, g):
                pe.wait_ge(s["o_ev"], c)
                for g, h, r, v in each([g]):
                    pe.matmul(ps[r, 4 + g, v], qgT[r, g * NC + c, h * DK:(h + 1) * DK], S[r, c % 2, g, v],
                              start=(h == 0), stop=False, skip_group_check=True)

            def update(c):
                for g, h, r, v in each():
                    mm = pe.matmul(ps[r, g, v], qkv[r, g * NC + c, QK + h * DK:QK + (h + 1) * DK],
                                   dlt[r, g, v], start=True, stop=True)
                mm.then_inc(s["su_ok"], 1)

            def project_out(c):
                for g in range(NG):
                    pe.wait_ge(s["ol_ok"], NG * c + g + 1)
                    for k in range(KO):
                        mm = acc3(pe, ps[:, 6 + g, 0:D], oh[:, g, k, :], ol[:, g, k, :],
                                  woh[:, k, :], wol[:, k, :], k == 0, k == KO - 1)
                    mm.then_inc(s["wo_ok"], 1)

            for c in range(NC + 2):
                if 0 < c < NC:
                    predict(c)
                if 0 < c <= NC:
                    within(c - 1)
                if c >= 2:
                    turn(c - 2)
                if c < NC:
                    deltas(c)
                    if c > 0:
                        across(c, 0)
                    pe.wait_ge(s["dlt_ok"], c + 1)
                if c < NC - 1:
                    update(c)
                if c >= 2:
                    project_out(c - 2)
                if 0 < c < NC:
                    across(c, 1)

        pe.sem_inc(s["ystep"], 1)
        layernorm(0)
        feed_forward(0)
        layernorm(1)
        project()
        chunk_steps()
        layernorm(2)
        feed_forward(1)

    @block.scalar
    def _(act):
        def layernorm(ph):
            act.wait_ge(s["ln_var"], ph + 1)
            act.activation(stdev[:, :], vareps[:, :], ACT.Sqrt).then_inc(s["ln_sd"], 1)
            if ph == 2:
                high_part(1, "2")
                act.wait_ge(s["w1l_ok"], 2 * KD)
                act.wait_ge(s["w3l_ok"], 2)

            def normal(n):
                if n >= 4:
                    act.wait_ge(s["tr_ok"], NT * ph + n - 3)
                act.activation(xn[:, n % 4, :], xres[:, n, :], ACT.Identity, bias=offset[:, n:n + 1],
                               scale=rstd[:, n:n + 1]).then_inc(s["xn_odd"], 1)

            act.wait_ge(s["offset_ok"], ph + 1)
            if ph == 1:
                act.wait_ge(s["res_ok"], 1 + NCHUNK)
            if ph == 2:
                act.wait_ge(s["wo_ev"], NT)
            for n in (1, 3):
                normal(n)
            for m in range(NP):
                if ph == 0 and m in (NP - 3, NP - 2):
                    high_part(0, "1", m - (NP - 3))
                act.wait_ge(s["tr_ok"], NT * ph + 2 * m + 2)
                act.copy(xhi[:, :, m * 2 * P:(m + 1) * 2 * P],
                         ps[:, m % 4, :].rearrange("p (k t) -> p k t", k=KD)).then_inc(s["xhi_ok"], 1)
                if 2 * m + 5 < NT:
                    normal(2 * m + 5)
                if ph != 1 and m in (3, 5, 7):
                    sigmoid(ph // 2, (m - 3) // 2)
            if ph != 1:
                sigmoid(ph // 2, NCHUNK - 1)

        def sigmoid(f, i):
            act.wait_ge(s["sc_ok"], NCHUNK * f + i + 1)
            act.activation(ffn[f]["sT"][0:E, i * CHUNK:(i + 1) * CHUNK], ps[0:E, 4 + i, :],
                           ACT.Sigmoid).then_inc(s["sig_ok"], 1)

        def high_part(f, w, k=None):
            t = ffn[f]
            if f == 1:
                act.wait_ge(s["wo_ev"], NT)
            act.wait_ge(s["padz"], 3 * (f + 1))
            act.wait_ge(s["rw" + w], {"1": 128, "3": 64, "2": 48}[w] * (f + 1))
            part = slice(None) if k is None else slice(k, k + 1)
            act.copy(t[f"w{w}h"][:, part, :], t["r" + w][:, part, :]).then_inc(s[f"w{w}h_ok"], 1)

        def high_gate(f):
            t = ffn[f]
            act.wait_ge(s["rgate"], 32 * (f + 1))
            act.copy(t["gh"][:, :, :], t["gr"][:, :, :]).then_inc(s["wgt_hi"], 1)

        def feed_forward(f):
            t = ffn[f]
            if f == 0:
                high_part(0, "3")
                high_part(0, "2")
            act.wait_ge(s["c9T_ok"], 2 * (f + 1))
            act.copy(t["cT"][0:ROUTE, TOK // 2:TOK],
                     ps[0:ROUTE, 6:8, :].rearrange("p b t -> p (b t)")).then_inc(s["cTb_ok"], 1)
            with act.Fori(0, NCHUNK) as i:
                steps = HT * NCHUNK * f + i * HT

                def high(j):
                    act.wait_ge(s["a_ok"], steps + j + 2)
                    act.wait_ge(s["ystep"], 1 + steps + max(j - LAG, 0))
                    rows = slice(0, P) if j < FULL else slice(0, HALF)
                    act.copy(t["ahi"][rows, j % (LAG + 1), :], t["a"][rows, j % 2, :]).then_inc(s["ahi_ok"], 1)

                for j in range(HT):
                    act.wait_ge(s["h_ok"], steps + j + 1)
                    act.wait_ge(s["p_ok"], 1 + steps + max(j - 1, 0))
                    src, dst = (slice(0, P),) * 2 if j < FULL else (slice(HALF, P), slice(0, HALF))
                    act.activation(t["s"][dst, j % 2, :], ps[src, j % 2, :], ACT.Silu).then_inc(s["silu_ok"], 1)
                    if j >= 1:
                        high(j - 1)
                high(HT - 1)

        def project():
            act.wait_ge(s["rattn"], 16 * 13)
            act.wait_ge(s["res_ok"], 1 + NCHUNK)
            act.copy(wqkvh[:, :, :], wqkv_r[:, :, :]).then_inc(s["attn_hi"], 1)
            act.copy(wgabh[:, :, :], wgab_r[:, :, :]).then_inc(s["attn_hi"], 1)
            act.wait_ge(s["wo_sc"], 1)
            act.copy(woh[:, :, :], wo_r[:, :, :]).then_inc(s["wo_sc"], 1)

        def convolve():
            act.wait_ge(s["small_in"], 16 * 11)
            act.wait_ge(s["cbz"], 1)

            def silu_turned(m):
                for r in range(4):
                    act.wait_ge(s["tq_ok"], 4 * m + r + 1)
                    act.activation(qkv[:, 4 * r:4 * r + 4, m * P:(m + 1) * P],
                                   ps[:, 4 + r, :].rearrange("p (n f) -> p n f", n=4),
                                   ACT.Silu).then_inc(s["tq_ev"], 1)

            job = [0]

            def features(m):
                for ch in range(NCHUNK):
                    n = job[0]
                    job[0] += 1
                    g, half = divmod(ch, 2)
                    act.wait_ge(s["pj_ok"], n + 1)
                    if m >= 2:
                        act.wait_ge(s["conv_ok"], m - 1)
                    t0 = PAD + half * TPC * CH
                    act.copy(cb[:, m % 2, g * NQ:(g + 1) * NQ, t0:t0 + TPC * CH].rearrange(
                        "p b (c t) -> p c b t", c=TPC), gview(ps[:, n % 4, :])).then_inc(s["pj_ev"], 1)
                if m == 1:
                    act.wait_ge(s["attn_lo"], 2)
                    act.wait_ge(s["wo_sc"], 3)
                act.wait_ge(s["pj_ev"], job[0])
                act.activation(ysums[m][:, :, :], cb[:, m % 2, :, PAD:PAD + T], ACT.Copy,
                               scale=cw[:, m, PAD:PAD + 1]).then_inc(s["tap_ok"], 1)

            def gate_tiles(r):
                for i in range(4 * r, 4 * r + 4):
                    n = job[0]
                    job[0] += 1
                    act.wait_ge(s["pj_ok"], n + 1)
                    act.activation(silug[:, i, :], ps[:, n % 4, 0:VD], ACT.Silu)
                    act.copy(ab[:, i, :], ps[:, n % 4, VD:GAB]).then_inc(s["pj_ev"], 1)

            def squares(m):
                for r in range(2):
                    n = 2 * m + r
                    act.wait_ge(s["tq_ev"], 4 * m + 2 * r + 2)
                    if n >= 2:
                        act.wait_ge(s["l2_ss"], n - 1)
                    act.activation(sqs[r][:, :, :], qkv[:, r * NT // 2:(r + 1) * NT // 2, m * P:(m + 1) * P],
                                   ACT.Square).then_inc(s["sq_ok"], 1)

            def decay_and_beta():
                act.wait_ge(s["z_ok"], 1)
                act.activation(small["ez"][:, :, :], small["az"][:, :, :], ACT.Exp, scale=-1.0).then_inc(s["ez_ok"], 1)
                act.activation(small["eb"][:, :, :], ab[:, :, H:2 * H], ACT.Exp, scale=-1.0).then_inc(s["ez_ok"], 1)
                act.activation(alog[:, :], alog[:, :], ACT.Exp).then_inc(s["ez_ok"], 1)
                act.wait_ge(s["w_ok"], 1)
                act.activation(small["lnw"][:, :, :], small["w"][:, :, :], ACT.Ln).then_inc(s["lnw_ok"], 1)
                act.wait_ge(s["l2_ss"], 6)
                act.activation(ss_qk[:, :, 0:H], ss_qk[:, :, 0:H], ACT.Sqrt, scale=float(DK)).then_inc(s["l2_sd"], 1)
                act.activation(ss_qk[:, :, H:2 * H], ss_qk[:, :, H:2 * H], ACT.Sqrt).then_inc(s["l2_sd"], 1)

            features(0)
            features(1)
            gate_tiles(0)
            for m in range(3):
                silu_turned(m)
                features(m + 2)
                gate_tiles(m + 1)
                squares(m)
            decay_and_beta()
            silu_turned(3)
            features(5)
            act.wait_ge(s["cum_ok"], 1)
            act.activation(ge[:, :, :].rearrange("p r i -> p (r i)"), ps[:, 0, 0:3 * INST],
                           ACT.Exp).then_inc(s["ge_ok"], 1)
            per = 512 // CH
            for r in range(INST // per):
                act.wait_ge(s["cum_ok"], r + 2)
                act.activation(dec[:, r * per:(r + 1) * per, :].rearrange("p i t -> p (i t)"), ps[:, (1 + r) % 4, :],
                               ACT.Exp).then_inc(s["dec_ok"], 1)
            silu_turned(FM - 2)
            silu_turned(FM - 1)

        def chunk_steps():
            flat = "p n h -> p (n h)"

            def outputs(c):
                act.wait_ge(s["o_ok"], c + 1)
                act.wait_ge(s["R_ok"], c + 1)
                for g in range(NG):
                    e = act.copy(qkv[:, g * NC + c, 2 * QK:FEAT], ps[:, 4 + g, 0:VD])
                e.then_inc(s["o_ev"], 1)

            def high(c):
                for g in range(NG):
                    act.wait_ge(s["ot_ok"], NG * c + g + 1)
                    if c > 0:
                        act.wait_ge(s["wo_ok"], NG * (c - 1) + g + 1)
                    act.copy(oh[:, g, :, :].rearrange("p k t -> p (k t)"),
                             ps[:, 6 + g, 0:KO * P]).then_inc(s["oh_ok"], 1)

            def deltas(c):
                act.wait_ge(s["d_ok"], c + 1)
                act.copy(dlt[:, :, :], ps[:, 2:4, 0:VD]).then_inc(s["dlt_ok"], 1)

            def deviation(c):
                cs = slice(c * NG * H, (c + 1) * NG * H)
                act.wait_ge(s["ost_ok"], c + 1)
                act.activation(small["ostd"][:, :, :].rearrange(flat)[:, cs],
                               small["orms"][:, :, :].rearrange(flat)[:, cs], ACT.Sqrt).then_inc(s["osd_ok"], 1)

            for c in range(NC + 2):
                if 0 < c <= NC:
                    outputs(c - 1)
                if c >= 2:
                    high(c - 2)
                if c < NC:
                    deltas(c)
                if 0 < c <= NC:
                    deviation(c - 1)

        act.sem_inc(s["silu_ok"], 1)
        high_gate(0)
        layernorm(0)
        feed_forward(0)
        project()
        layernorm(1)
        convolve()
        chunk_steps()
        for k in range(KD):
            high_part(1, "1", k)
        high_part(1, "3")
        high_gate(1)
        layernorm(2)
        feed_forward(1)

    @block.gpsimd
    def _(pool):
        def split_weights(f):
            t = ffn[f]
            for c in (UF, UF + HALF):
                pool.memset(t["r1"][:, :, c + REST:c + HALF], 0.0).then_inc(s["padz"], 1)
            if f == 1:
                pool.wait_ge(s["o_ok"], NC)
            pool.memset(t["r2"][:, HT - 1, :], 0.0).then_inc(s["padz"], 1)

            def low(w, k=None):
                pool.wait_ge(s[f"w{w}h_ok"], f + 1 if k is None else KD * f + k + 1)
                part = slice(None) if k is None else slice(k, k + 1)
                pool.tensor_tensor(t[f"w{w}l"][:, part, :], t["r" + w][:, part, :],
                                   t[f"w{w}h"][:, part, :].bitcast(F32), ALU.subtract).then_inc(s[f"w{w}l_ok"], 1)

            def low_gate():
                pool.wait_ge(s["wgt_hi"], f + 1)
                pool.tensor_tensor(t["gl"][:, :, :], t["gr"][:, :, :], t["gh"][:, :, :].bitcast(F32),
                                   ALU.subtract).then_inc(s["wgt_lo"], 1)

            if f == 0:
                low_gate()
                low("1", 0)
            low("1", 1)
            if f == 1:
                low_gate()
            low("2")

        def feed_forward(f):
            t = ffn[f]
            with pool.Fori(0, NCHUNK) as i:
                steps = HT * NCHUNK * f + i * HT
                for j in range(HT):
                    pool.wait_ge(s["ahi_ok"], steps + j + 1)
                    rows = slice(0, P) if j < FULL else slice(0, HALF)
                    pool.tensor_tensor(t["alo"][rows, j % (LAG + 1), :], t["a"][rows, j % 2, :],
                                       t["ahi"][rows, j % (LAG + 1), :].bitcast(F32),
                                       ALU.subtract).then_inc(s["alo_ok"], 1)

        def attention():
            pool.wait_ge(s["res_ok"], 1 + NCHUNK)
            pool.memset(cb[:, :, :, 0:PAD], 0.0).then_inc(s["cbz"], 1)
            pool.wait_ge(s["attn_hi"], 2)
            pool.tensor_tensor(wqkvl[:, :, :], wqkv_r[:, :, :], wqkvh[:, :, :].bitcast(F32),
                               ALU.subtract).then_inc(s["attn_lo"], 1)
            pool.tensor_tensor(wgabl[:, :, :], wgab_r[:, :, :], wgabh[:, :, :].bitcast(F32),
                               ALU.subtract).then_inc(s["attn_lo"], 1)
            pool.wait_ge(s["wo_sc"], 2)
            pool.tensor_tensor(wol[:, :, :], wo_r[:, :, :], woh[:, :, :].bitcast(F32),
                               ALU.subtract).then_inc(s["wo_sc"], 1)
            pool.wait_ge(s["g_ok"], 1)
            pool.wait_ge(s["conv_ok"], 4)
            pool.wait_ge(s["l2_ss"], 6)
            gall = small["g"][:, :, :].rearrange("p n h -> p (n h)")
            pool.tensor_tensor(rhsd[:, :, :], gall.unsqueeze(2).broadcast_to((P, INST, CH)),
                               incl.unsqueeze(1).broadcast_to((P, INST, CH)), ALU.mult).then_inc(s["rhsd_ok"], 1)
            pool.wait_ge(s["unit_ok"], 1)
            q4 = qkv[:, :, 0:QK].rearrange("p n (h d) -> p n h d", d=DK)
            pool.tensor_tensor(q4, q4, ss_qk[:, :, 0:H].unsqueeze(3).broadcast_to((P, NT, H, DK)),
                               ALU.mult).then_inc(s["q_unit"], 1)
            pool.wait_ge(s["cum_ok"], 1 + INST * CH // 512)
            pool.wait_ge(s["dec_ok"], INST * CH // 512)
            pool.tensor_tensor(ltn[:, :, :], dec[:, :, :], nstrict.unsqueeze(1).broadcast_to((P, INST, CH)),
                               ALU.mult).then_inc(s["mask_ok"], 1)
            pool.wait_ge(s["mask_ok"], 1)
            pool.tensor_tensor(dec[:, :, :], dec[:, :, :], incl.unsqueeze(1).broadcast_to((P, INST, CH)),
                               ALU.mult).then_inc(s["mask_ok"], 1)
            pool.wait_ge(s["kT_ok"], 1)
            pool.wait_ge(s["kb_ok"], 2)
            pool.wait_ge(s["ge_ok"], 1)
            kv = qkv[:, :, QK:2 * QK].rearrange("p n (h d) -> p n h d", h=H)
            pool.tensor_tensor(kv, kv, ge[:, 1, :].rearrange("p (n h) -> p n h", h=H).unsqueeze(3).broadcast_to(
                (P, NT, H, DK)), ALU.mult).then_inc(s["kE_ok"], 1)
            pool.wait_ge(s["gm_ok"], INST // 8)
            pool.memset(U[:, :, :, :], 0.0).then_inc(s["u_init"], 1)
            pool.wait_ge(s["u_init"], 1)
            pool.memset(U[:, :, :, :].rearrange("p h s t -> p h (s t)")[:, :, 0:CH * CH:CH + 1],
                        1.0).then_inc(s["u_init"], 1)
            pool.wait_ge(s["tq_ev"], 4 * FM)
            vv = qkv[:, :, 2 * QK:FEAT].rearrange("p n (h d) -> p n h d", h=H)
            pool.tensor_tensor(vv, vv, small["beta"][:, :, :].unsqueeze(3).broadcast_to((P, NT, H, DV)),
                               ALU.mult).then_inc(s["kE_ok"], 1)

        def first_rows():
            pool.wait_ge(s["u_init"], 2)
            pool.wait_ge(s["tri_r"], 16)
            done = 0
            for c in range(CH - 1):
                rows, cols = min(c + 1, POOL_ROWS), CH - 1 - c
                tmp = tmpP[:, :, 0:rows * cols].rearrange("p h (j i) -> p h j i", j=rows)
                pool.tensor_tensor(tmp, X[:, :, c:c + 1, c + 1:CH].broadcast_to((P, IH, rows, cols)),
                                   U[:, :, 0:rows, c:c + 1].broadcast_to((P, IH, rows, cols)),
                                   ALU.mult).then_inc(s["row_ok"], 1)
                done += 1
                pool.wait_ge(s["row_ok"], done)
                dst = U[:, :, 0:rows, c + 1:CH]
                e = pool.tensor_tensor(dst, dst, tmp, ALU.add)
                if c < CH - 2:
                    e.then_inc(s["row_ok"], 1)
                    done += 1
                    pool.wait_ge(s["row_ok"], done)
            e.then_inc(s["inv_ok"], 1)

        pool.sem_inc(s["alo_ok"], 1)
        split_weights(0)
        feed_forward(0)
        attention()
        first_rows()
        pool.wait_ge(s["inv_w"], 16)
        split_weights(1)
        feed_forward(1)

    @block.vector
    def _(v):
        chain = [0]

        def link(ins):
            chain[0] += 1
            ins.then_inc(s["dch"], 1)
            v.wait_ge(s["dch"], chain[0])

        def layernorm(ph):
            if ph == 0:
                for n in range(NT):
                    if n % NC == 0:
                        v.wait_ge(s[f"x_in{n // NC}"], 16 * NQ)
                    e = v.bn_stats(stats[:, n, :], xres[:, n, :])
                e.then_inc(s["st_ok"], 1)
            v.wait_ge(s["st_ok"], (1, 1 + NCHUNK, 1 + NCHUNK + NC)[ph])
            for n in range(NT):
                e = v.bn_aggr(moments[:, n, :], stats[:, n, :])
            link(e)
            v.tensor_scalar(vareps[:, :], moments[:, :, 1], EPS, None, ALU.add).then_inc(s["ln_var"], 1)
            if ph == 2:
                low_part(1)
                v.wait_ge(s["w1l_ok"], 2 * KD)
            v.wait_ge(s["ln_sd"], ph + 1)
            link(v.reciprocal(rstd[:, :], stdev[:, :]))
            v.scalar_tensor_tensor(out=offset[:, :], in0=moments[:, :, 0], scalar=-1.0, in1=rstd[:, :],
                                   op0=ALU.mult, op1=ALU.mult).then_inc(s["offset_ok"], 1)

            def normal(n):
                if n >= 4:
                    v.wait_ge(s["tr_ok"], NT * ph + n - 3)
                v.tensor_scalar(xn[:, n % 4, :], xres[:, n, :], moments[:, n, 0:1], rstd[:, n:n + 1],
                                ALU.subtract, ALU.mult).then_inc(s["xn_even"], 1)

            for n in (0, 2):
                normal(n)
            for m in range(NP):
                v.wait_ge(s["xhi_ok"], NP * ph + m + 1)
                c = slice(m * 2 * P, (m + 1) * 2 * P)
                v.tensor_tensor(xlo[:, :, c], ps[:, m % 4, :].rearrange("p (k t) -> p k t", k=KD),
                                xhi[:, :, c].bitcast(F32), ALU.subtract).then_inc(s["xlo_ok"], 1)
                if 2 * m + 4 < NT:
                    normal(2 * m + 4)

        def low_part(f):
            t = ffn[f]
            if f == 1:
                v.wait_ge(s["w1h_ok"], KD + 1)
                v.tensor_tensor(t["w1l"][:, 0, :], t["r1"][:, 0, :], t["w1h"][:, 0, :].bitcast(F32),
                                ALU.subtract).then_inc(s["w1l_ok"], 1)
            v.wait_ge(s["w3h_ok"], f + 1)
            v.tensor_tensor(t["w3l"][:, :, :], t["r3"][:, :, :], t["w3h"][:, :, :].bitcast(F32),
                            ALU.subtract).then_inc(s["w3l_ok"], 1)

        def route(f):
            t = ffn[f]
            v.wait_ge(s["scT_ok"], f + 1)
            link(v.tensor_copy(t["sc"][:, :, :], ps[:, 0, 0:NT * E].rearrange("p (n e) -> p n e", e=E)))
            over = t["sc"][:, :, :].unsqueeze(2).broadcast_to((P, NT, E, E))
            mine = t["sc"][:, :, :].unsqueeze(3).broadcast_to((P, NT, E, E))
            link(v.tensor_tensor(t["gt"][:, :, :, :], over, mine, ALU.is_ge))
            gtf = t["gt"][:, :, :, :].rearrange("p n a b -> p n (a b)")
            link(v.tensor_tensor(gtf, gtf, tie.unsqueeze(1).broadcast_to((P, NT, E * E)), ALU.mult))
            v.tensor_reduce(t["rank"][:, :, :], t["gt"][:, :, :, :], AX_X, ALU.add)
            link(v.tensor_reduce(t["less"][:, :, :], t["gt"][:, :, :, :].rearrange("p n a b -> p n b a"), AX_X,
                                 ALU.add))
            link(v.tensor_tensor(t["rank"][:, :, :], t["rank"][:, :, :], t["less"][:, :, :], ALU.subtract))
            link(v.tensor_tensor(t["rank"][:, :, :], t["rank"][:, :, :],
                                 places.unsqueeze(1).broadcast_to((P, NT, E)), ALU.is_lt))
            link(v.tensor_tensor(t["ss"][:, :, :], t["rank"][:, :, :], t["sc"][:, :, :], ALU.mult))
            link(v.tensor_reduce(t["cs"][:, :], t["ss"][:, :, :], AX_X, ALU.add))
            link(v.tensor_scalar(t["cs"][:, :], t["cs"][:, :], 1e-20, None, ALU.add))
            link(v.reciprocal(t["cr"][:, :], t["cs"][:, :]))
            v.memset(t["c9"][:, :, E:ROUTE], 0.5)
            v.scalar_tensor_tensor(out=t["c9"][:, :, 0:E], in0=t["ss"][:, :, :], scalar=2.5 * 0.5,
                                   in1=t["cr"][:, :].unsqueeze(2).broadcast_to((P, NT, E)),
                                   op0=ALU.mult, op1=ALU.mult).then_inc(s["c9_ok"], 1)
            if f == 0:
                low_part(0)
            v.wait_ge(s["c9T_ok"], 2 * f + 1)
            v.tensor_copy(t["cT"][0:ROUTE, 0:TOK // 2],
                          ps[0:ROUTE, 4:6, :].rearrange("p b t -> p (b t)")).then_inc(s["cTa_ok"], 1)

        def feed_forward(f):
            t = ffn[f]
            route(f)
            with v.Fori(0, NCHUNK) as i:
                steps = HT * NCHUNK * f + i * HT
                for j in range(HT):
                    v.wait_ge(s["silu_ok"], steps + j + 2)
                    rows, u = slice(0, P), ps[:, 2 + j % 2, :]
                    if j < FULL:
                        v.wait_ge(s["u_ok"], FULL * NCHUNK * f + i * FULL + j + 1)
                    else:
                        rows = slice(0, HALF)
                        u = ps[rows, j % 2, :]
                    v.wait_ge(s["a_ok"], 1 + steps + max(j - 1, 0))
                    v.tensor_tensor(t["p"][rows, j % 2, :], t["s"][rows, j % 2, :], u,
                                    ALU.mult).then_inc(s["p_ok"], 1)
                    v.wait_ge(s["p_ok"], steps + j + 2)
                    v.wait_ge(s["alo_ok"], 1 + steps + max(j - 1, 0))
                    v.wait_ge(s[f"cr{slot(j)}"], arrived(j) * NCHUNK * f + i * arrived(j) + arrived(j, j))
                    v.tensor_tensor(t["a"][rows, j % 2, :], t["p"][rows, j % 2, :], t["cring"][rows, slot(j), :],
                                    ALU.mult).then_inc(s["a_ok"], 1)
                v.wait_ge(s["ystep"], 1 + steps + HT)
                xr = xres[:, bass.ds(i * TPC, TPC), :]
                v.tensor_tensor(xr, xr, ps[:, 6:8, :].rearrange("p b (q d) -> p (b q) d", d=D),
                                ALU.add).then_inc(s["res_ok"], 1)
                if f == 0:
                    v.wait_ge(s["res_ok"], i + 2)
                    for q in range(TPC):
                        e = v.bn_stats(stats[:, bass.ds(i * TPC + q, 1), :].rearrange("p n c -> p (n c)"),
                                       xres[:, bass.ds(i * TPC + q, 1), :].rearrange("p n d -> p (n d)"))
                    e.then_inc(s["st_ok"], 1)

        def convolve():
            m_ = small

            def taps(m):
                v.wait_ge(s["tap_ok"], m + 1)
                v.wait_ge(s["cbz"], 1)
                for i in range(1, PAD):
                    link(v.scalar_tensor_tensor(out=ysums[m][:, :, :], in0=cb[:, m % 2, :, i:i + T],
                                                scalar=cw[:, m, i:i + 1], in1=ysums[m][:, :, :],
                                                op0=ALU.mult, op1=ALU.add))

            def last_tap(m):
                if m > 0:
                    v.wait_ge(s["tq_ok"], 4 * m)
                for b in range(B):
                    g, q = divmod(b, NQ)
                    e = v.scalar_tensor_tensor(out=y[:, g, :, q, :],
                                               in0=cb[:, m % 2, b, 0:T].rearrange("p (c t) -> p c t", t=CH),
                                               scalar=cw[:, m, 0:1],
                                               in1=ysums[m][:, b, :].rearrange("p (c t) -> p c t", t=CH),
                                               op0=ALU.mult, op1=ALU.add)
                e.then_inc(s["conv_ok"], 1)

            def square_sums(m):
                per = P // DK
                for r in range(2):
                    v.wait_ge(s["sq_ok"], 2 * m + r + 1)
                    v.tensor_reduce(ss_qk[:, r * NT // 2:(r + 1) * NT // 2, m * per:(m + 1) * per],
                                    sqs[r][:, :, :].rearrange("p n (h d) -> p n h d", d=DK), AX_X,
                                    ALU.add).then_inc(s["l2_ss"], 1)

            def softplus_in():
                v.wait_ge(s["pj_ev"], (FM - 1) * NCHUNK + NT)
                v.tensor_tensor(m_["z"][:, :, :], ab[:, :, 0:H], dtb[:, :].unsqueeze(1).broadcast_to((P, NT, H)),
                                ALU.add).then_inc(s["dch"], 1)
                chain[0] += 1
                v.wait_ge(s["dch"], chain[0])
                v.scalar_tensor_tensor(out=m_["az"][:, :, :], in0=m_["z"][:, :, :], scalar=-1.0,
                                       in1=m_["z"][:, :, :], op0=ALU.mult, op1=ALU.max).then_inc(s["z_ok"], 1)

            def softplus_mid():
                v.wait_ge(s["ez_ok"], 3)
                link(v.tensor_scalar(m_["w"][:, :, :], m_["ez"][:, :, :], 1.0, None, ALU.add))
                v.tensor_scalar(m_["isone"][:, :, :], m_["w"][:, :, :], 1.0, None, ALU.is_equal).then_inc(s["w_ok"], 1)
                link(v.tensor_scalar(m_["eb"][:, :, :], m_["eb"][:, :, :], 1.0, None, ALU.add))
                v.reciprocal(m_["beta"][:, :, :], m_["eb"][:, :, :]).then_inc(s["beta_ok"], 1)

            def decay():
                v.wait_ge(s["lnw_ok"], 1)
                v.wait_ge(s["w_ok"], 1)
                v.tensor_tensor(m_["lnw"][:, :, :], m_["lnw"][:, :, :], m_["isone"][:, :, :], ALU.add)
                link(v.scalar_tensor_tensor(out=m_["w"][:, :, :], in0=m_["w"][:, :, :], scalar=-1.0,
                                            in1=m_["isone"][:, :, :], op0=ALU.add, op1=ALU.add))
                link(v.reciprocal(m_["w"][:, :, :], m_["w"][:, :, :]))
                link(v.tensor_tensor(m_["lnw"][:, :, :], m_["lnw"][:, :, :], m_["ez"][:, :, :], ALU.mult))
                link(v.tensor_tensor(m_["lnw"][:, :, :], m_["lnw"][:, :, :], m_["w"][:, :, :], ALU.mult))
                link(v.scalar_tensor_tensor(out=m_["sp"][:, :, :], in0=m_["z"][:, :, :], scalar=0.0,
                                            in1=m_["lnw"][:, :, :], op0=ALU.max, op1=ALU.add))
                v.scalar_tensor_tensor(out=m_["g"][:, :, :], in0=m_["sp"][:, :, :], scalar=-1.0,
                                       in1=alog[:, :].unsqueeze(1).broadcast_to((P, NT, H)),
                                       op0=ALU.mult, op1=ALU.mult).then_inc(s["g_ok"], 1)

            for m in range(4):
                taps(m)
                last_tap(m)
                if 0 < m < 3:
                    square_sums(m - 1)
            softplus_in()
            square_sums(2)
            softplus_mid()
            taps(4)
            decay()
            last_tap(4)
            v.wait_ge(s["l2_sd"], 2)
            v.reciprocal(ss_qk[:, :, :], ss_qk[:, :, :]).then_inc(s["unit_ok"], 1)
            v.wait_ge(s["unit_ok"], 1)
            k4 = qkv[:, :, QK:2 * QK].rearrange("p n (h d) -> p n h d", d=DK)
            link(v.tensor_tensor(k4, k4, ss_qk[:, :, H:2 * H].unsqueeze(3).broadcast_to((P, NT, H, DK)), ALU.mult))
            v.wait_ge(s["pj_ev"], FM * NCHUNK + NT)
            v.transpose(kT[:, :, :], qkv[:, :, QK:2 * QK]).then_inc(s["kT_ok"], 1)
            v.wait_ge(s["conv_ok"], 5)
            v.wait_ge(s["beta_ok"], 1)
            for r in range(2):
                half = slice(r * NT // 2, (r + 1) * NT // 2)
                if r > 0:
                    v.wait_ge(s["qT_ok"], r)
                v.tensor_tensor(kb[:, :, :].rearrange("p n (h d) -> p n h d", h=H),
                                qkv[:, half, QK:2 * QK].rearrange("p n (h d) -> p n h d", h=H),
                                small["beta"][:, half, :].unsqueeze(3).broadcast_to((P, NT // 2, H, DK)),
                                ALU.mult).then_inc(s["kb_ok"], 1)
                v.wait_ge(s["kb_ok"], r + 1)
                v.transpose(kq[:, 0, half, :], kb[:, :, :]).then_inc(s["qT_ok"], 1)
            v.wait_ge(s["q_unit"], 1)
            v.transpose(kq[:, 1, :, :], qkv[:, :, 0:QK]).then_inc(s["qk_ok"], 1)
            taps(5)
            last_tap(5)

        def from_start():
            v.wait_ge(s["ge_ok"], 1)
            v.wait_ge(s["conv_ok"], FM)
            q4 = qkv[:, :, 0:QK].rearrange("p n (h d) -> p n h d", d=DK)
            G4 = ge[:, 0, :].rearrange("p (n h) -> p n h", h=H)
            v.wait_ge(s["qk_ok"], 1)
            link(v.tensor_tensor(small["bG"][:, :, :], small["beta"][:, :, :], G4, ALU.mult))
            link(v.tensor_tensor(q4, q4, G4.unsqueeze(3).broadcast_to((P, NT, H, DK)), ALU.mult))
            v.transpose(qgT[:, :, :], qkv[:, :, 0:QK]).then_inc(s["scaled_ok"], 1)

        def triangles():
            v.wait_ge(s["mask_ok"], 2)
            for r in range(INST // 8):
                v.wait_ge(s["gm_ok"], r + 1)
                b = ps[:, r % 4, :].rearrange("p (i w t) -> p i w t", i=8, w=2)
                c = slice(8 * r, 8 * r + 8)
                v.tensor_tensor(ltn[:, c, :], ltn[:, c, :], b[:, :, 0, :], ALU.mult)
                v.tensor_tensor(dec[:, c, :], dec[:, c, :], b[:, :, 1, :], ALU.mult).then_inc(s["gm_ev"], 1)
            from_start()
            v.wait_ge(s["u_init"], 2)
            v.wait_ge(s["tri_r"], 16)
            for c in range(POOL_ROWS, CH - 1):
                rows, cols = c + 1 - POOL_ROWS, CH - 1 - c
                tmp = tmpU[:, :, 0:rows * cols].rearrange("p h (j i) -> p h j i", j=rows)
                mine = slice(POOL_ROWS, c + 1)
                link(v.tensor_tensor(tmp, X[:, :, c:c + 1, c + 1:CH].broadcast_to((P, IH, rows, cols)),
                                     U[:, :, mine, c:c + 1].broadcast_to((P, IH, rows, cols)), ALU.mult))
                dst = U[:, :, mine, c + 1:CH]
                e = v.tensor_tensor(dst, dst, tmp, ALU.add)
                if c < CH - 2:
                    link(e)
            e.then_inc(s["inv_ok"], 1)

        def chunk_steps():
            v.wait_ge(s["kE_ok"], 2)
            heads = "p g (h d) -> p g h d"
            flat = "p n h -> p (n h)"

            def residues(c):
                vb = qkv[:, c:NT:NC, 2 * QK:FEAT]
                if c == 0:
                    v.tensor_copy(R[:, :, :], vb).then_inc(s["R_ok"], 1)
                    return
                v.wait_ge(s["r_ok"], c)
                bg = small["bG"][:, c:NT:NC, :].unsqueeze(3).broadcast_to((P, NG, H, DV))
                link(v.tensor_tensor(tmpR[:, :, :].rearrange(heads, h=H),
                                     ps[:, 0:2, 0:VD].rearrange(heads, h=H), bg, ALU.mult))
                v.tensor_tensor(R[:, :, :], vb, tmpR[:, :, :], ALU.subtract).then_inc(s["R_ok"], 1)
                if c < NC - 1:
                    gt = ge[:, 2, :].rearrange("p (n h) -> p n h", h=H)[:, c:NT:NC, :].unsqueeze(3).broadcast_to(
                        (P, NG, H, DV))
                    link(v.tensor_tensor(tmpS[:, :, :].rearrange(heads, h=H), S[:, c % 2, :, :].rearrange(heads, h=H), gt,
                                         ALU.mult))

            def low(c):
                for g in range(NG):
                    v.wait_ge(s["oh_ok"], NG * c + g + 1)
                    v.tensor_tensor(ol[:, g, :, :].rearrange("p k t -> p (k t)"), ps[:, 6 + g, 0:KO * P],
                                    oh[:, g, :, :].rearrange("p k t -> p (k t)").bitcast(F32),
                                    ALU.subtract).then_inc(s["ol_ok"], 1)

            def mean_square(c):
                cs = slice(c * NG * H, (c + 1) * NG * H)
                ov = qkv[:, c:NT:NC, 2 * QK:FEAT]
                rms = small["orms"][:, :, :].rearrange(flat)[:, cs]
                v.wait_ge(s["o_ev"], c + 1)
                v.wait_ge(s["R_ok"], min(c + 2, NC))
                link(v.tensor_tensor(osq[:, :, :], ov, ov, ALU.mult))
                link(v.tensor_reduce(rms, osq[:, :, :].rearrange("p g (h d) -> p (g h) d", h=H), AX_X, ALU.add))
                v.tensor_scalar(rms, rms, 1.0 / DV, EPS, ALU.mult, ALU.add).then_inc(s["ost_ok"], 1)

            def state(c):
                v.wait_ge(s["su_ok"], c + 1)
                if c == 0:
                    v.tensor_copy(S[:, 1, :, :], ps[:, 0:2, 0:VD]).then_inc(s["S_ok"], 1)
                else:
                    v.tensor_tensor(S[:, (c + 1) % 2, :, :], tmpS[:, :, :], ps[:, 0:2, 0:VD], ALU.add).then_inc(s["S_ok"], 1)

            def normalize(c):
                ov = qkv[:, c:NT:NC, 2 * QK:FEAT]
                ov4 = ov.rearrange(heads, h=H)
                std = small["ostd"][:, :, :].rearrange(flat)[:, c * NG * H:(c + 1) * NG * H]
                v.wait_ge(s["osd_ok"], c + 1)
                link(v.reciprocal(std, std))
                r4 = std.rearrange("p (g h) -> p g h", g=NG).unsqueeze(3).broadcast_to((P, NG, H, DV))
                link(v.tensor_tensor(ov4, ov4, r4, ALU.mult))
                v.tensor_tensor(ov, ov, silug[:, c:NT:NC, :], ALU.mult).then_inc(s["on_ok"], 1)

            def residual(c):
                for g in range(NG):
                    n = g * NC + c
                    v.wait_ge(s["wo_ok"], NG * c + g + 1)
                    v.tensor_tensor(xres[:, n, :], xres[:, n, :], ps[:, 6 + g, 0:D], ALU.add).then_inc(s["wo_ev"], 1)

            def statistics(c):
                v.wait_ge(s["wo_ev"], NG * (c + 1))
                for g in range(NG):
                    n = g * NC + c
                    e = v.bn_stats(stats[:, n, :], xres[:, n, :])
                e.then_inc(s["st_ok"], 1)

            for c in range(NC + 2):
                if c < NC:
                    residues(c)
                if c >= 3:
                    statistics(c - 3)
                if c >= 2:
                    low(c - 2)
                if 0 < c <= NC:
                    mean_square(c - 1)
                if c < NC - 1:
                    state(c)
                if 0 < c <= NC:
                    normalize(c - 1)
                if c >= 2:
                    residual(c - 2)
            statistics(NC - 1)

        for n in ("p_ok", "a_ok", "res_ok"):
            v.sem_inc(s[n], 1)
        layernorm(0)
        feed_forward(0)
        v.wait_ge(s["res_ok"], 1 + NCHUNK)
        v.wait_ge(s["small_in"], 16 * 11)
        v.wait_ge(s["rattn"], 16 * 13)
        v.tensor_scalar(wo_r[:, :, :], wo_r[:, :, :], nwt[:, 0:1], None, ALU.mult).then_inc(s["wo_sc"], 1)
        layernorm(1)
        convolve()
        triangles()
        chunk_steps()
        layernorm(2)
        feed_forward(1)

    ctx.close()


_INS = ["hidden_states", "Wq", "Wk", "Wv", "Wg", "Wa", "Wb", "Wo", "conv_wq", "conv_wk", "conv_wv",
        "A_log", "dt_bias", "norm_weight"]
_FFN = ["gate_w", "w1", "w2", "w3", "sw1", "sw2", "sw3"]


def kernel(**inputs):
    import numpy as _np
    import concourse.bacc as _bacc
    from concourse import mybir as _mybir
    from concourse.bass_utils import run_bass_kernel_spmd as _run

    nc = _bacc.Bacc("TRN2", target_bir_lowering=False, num_devices=1)
    arrays, args = {}, []
    for name in [f"L0_attn_{n}" for n in _INS] + [f"L0_ffn_{n}" for n in _FFN] + ["constants"]:
        a = constants(_np) if name == "constants" else _np.asarray(inputs[name])
        if name in ("L0_attn_A_log", "L0_attn_dt_bias"):
            a = _np.broadcast_to(a[None, :], (P, H))
        if name == "L0_attn_norm_weight":
            a = a.reshape(DV, 1)
        if name == "L0_ffn_gate_w":
            a = a.T
        a = _np.ascontiguousarray(a)
        arrays[f"in_{name}_dram"] = a
        args.append(nc.dram_tensor(f"in_{name}_dram", a.shape, _mybir.dt.from_np(a.dtype), kind="ExternalInput").ap())
    args.append(nc.dram_tensor("out_0_dram", (B, T, D), _mybir.dt.float32, kind="ExternalOutput").ap())
    macaron(nc, *args)
    r = _run(nc, [arrays], core_ids=[0])
    return r.results[0]["out_0_dram"]
```
